# Optimizing a Trainium2 kernel written in Bass

```python
import numpy as np
import jax
import jax.numpy as jnp

def _softmax(x, axis=-1):
    return jax.nn.softmax(x, axis=axis)

def _gelu(x):
    return jax.nn.gelu(x, approximate=True)

def _silu(x):
    return jax.nn.silu(x)

def _sigmoid(x):
    return jax.nn.sigmoid(x)

def _layernorm(x, axis=-1, eps=1e-05):
    m = jnp.mean(x, axis=axis, keepdims=True)
    v = jnp.var(x, axis=axis, keepdims=True)
    return (x - m) / jnp.sqrt(v + eps)

def _scatter_add(tgt, idx, src, axis=0):
    return tgt.at[idx].add(src)

def _segment_sum(src, seg, n):
    return jax.ops.segment_sum(src, seg, n)
kernel_name = 'mk_sandwich_d1_jaxref_r4_c244aa'

def setup_inputs(seed: int=0):
    np.random.seed(seed)
    _w = jnp.asarray

    def _L0_attn_setup():
        import jax, jax.numpy as jnp
        import numpy as np
        D_MODEL = 512
        D_STATE = 64
        D_CONV = 4
        HEADDIM = 64
        NHEADS = D_MODEL // HEADDIM
        D_IN_PROJ = 2 * D_MODEL + 2 * D_STATE + NHEADS
        CONV_DIM = D_MODEL + 2 * D_STATE
        B = 2
        L = 256

        def _mamba_fwd(u, W_in, conv_w, conv_b, W_out, A_log, D_param, dt_bias):
            Bb, Ll, _ = u.shape
            proj = u @ W_in.T
            z, x, B_toks, C_toks, dt_toks = jnp.split(proj, [D_MODEL, 2 * D_MODEL, 2 * D_MODEL + D_STATE, 2 * D_MODEL + 2 * D_STATE], axis=-1)
            xBC = jnp.concatenate([x, B_toks, C_toks], axis=-1).transpose(0, 2, 1)
            xBC = jax.lax.conv_general_dilated(xBC, conv_w, window_strides=(1,), padding=[(D_CONV - 1, 0)], feature_group_count=CONV_DIM) + conv_b[None, :, None]
            xBC = jax.nn.silu(xBC.transpose(0, 2, 1))
            x, B_toks, C_toks = jnp.split(xBC, [D_MODEL, D_MODEL + D_STATE], axis=-1)
            A = -jnp.exp(A_log)
            dt = jax.nn.softplus(dt_toks + dt_bias)
            dA = jnp.exp(dt * A)
            xh = x.reshape(Bb, Ll, NHEADS, HEADDIM)

            def step(S, inp):
                dA_t, dt_t, B_t, C_t, x_t = inp
                S = S * dA_t[:, :, None, None] + jnp.einsum('bh,bn,bhp->bhpn', dt_t, B_t, x_t)
                y_t = jnp.einsum('bhpn,bn->bhp', S, C_t)
                return (S, y_t)
            S0 = jnp.zeros((Bb, NHEADS, HEADDIM, D_STATE), u.dtype)
            xs = (dA.transpose(1, 0, 2), dt.transpose(1, 0, 2), B_toks.transpose(1, 0, 2), C_toks.transpose(1, 0, 2), xh.transpose(1, 0, 2, 3))
            _, ys = jax.lax.scan(step, S0, xs)
            y = ys.transpose(1, 0, 2, 3) + D_param[None, None, :, None] * xh
            y = y * jax.nn.silu(z.reshape(Bb, Ll, NHEADS, HEADDIM))
            return y.reshape(Bb, Ll, D_MODEL) @ W_out.T
        key = jax.random.key(seed)
        ks = jax.random.split(key, 8)
        u = jax.random.normal(ks[0], (B, L, D_MODEL), jnp.float32)
        W_in = jax.random.normal(ks[1], (D_IN_PROJ, D_MODEL), jnp.float32) * 0.02
        conv_w = jax.random.normal(ks[2], (CONV_DIM, 1, D_CONV), jnp.float32) * 0.2
        conv_b = jnp.zeros((CONV_DIM,), jnp.float32)
        W_out = jax.random.normal(ks[3], (D_MODEL, D_MODEL), jnp.float32) * 0.02
        A_log = jnp.log(jax.random.uniform(ks[4], (NHEADS,), jnp.float32, 1.0, 16.0))
        D_param = jnp.ones((NHEADS,), jnp.float32)
        dt = jnp.exp(jax.random.uniform(ks[5], (NHEADS,), jnp.float32) * (np.float32(np.log(0.1)) - np.float32(np.log(0.001))) + np.float32(np.log(0.001)))
        dt = jnp.clip(dt, 0.0001)
        dt_bias = dt + jnp.log(-jnp.expm1(-dt))
        return dict(u=u, W_in=W_in, conv_w=conv_w, conv_b=conv_b, W_out=W_out, A_log=A_log, D_param=D_param, dt_bias=dt_bias)
    _L0_attn_in = _L0_attn_setup()

    def _L0_ffn_setup():
        import jax, jax.numpy as jnp
        import numpy as np
        HIDDEN = 512
        INTER = 1376
        LUT_SIZE = 16

        def _ghost_linear(x, idx, lut):
            w = lut[idx]
            return jnp.einsum('bsh,oh->bso', x, w)
        key = jax.random.key(seed)
        k_x, k_lut, k_g, k_u, k_d = jax.random.split(key, 5)
        x = jax.random.normal(k_x, (2, 1024, HIDDEN), dtype=jnp.float32)
        lut = jax.random.normal(k_lut, (LUT_SIZE,), dtype=jnp.float32) * 0.02
        gate_idx = jax.random.randint(k_g, (INTER, HIDDEN), 0, LUT_SIZE, dtype=jnp.int32)
        up_idx = jax.random.randint(k_u, (INTER, HIDDEN), 0, LUT_SIZE, dtype=jnp.int32)
        down_idx = jax.random.randint(k_d, (HIDDEN, INTER), 0, LUT_SIZE, dtype=jnp.int32)
        return {'x': x, 'lut': lut, 'gate_idx': gate_idx, 'up_idx': up_idx, 'down_idx': down_idx}
    _L0_ffn_in = _L0_ffn_setup()
    _d = {'L0_attn_u': _L0_attn_in['u'], 'L0_attn_W_in': _L0_attn_in['W_in'], 'L0_attn_conv_w': _L0_attn_in['conv_w'], 'L0_attn_conv_b': _L0_attn_in['conv_b'], 'L0_attn_W_out': _L0_attn_in['W_out'], 'L0_attn_A_log': _L0_attn_in['A_log'], 'L0_attn_D_param': _L0_attn_in['D_param'], 'L0_attn_dt_bias': _L0_attn_in['dt_bias'], 'L0_ffn_lut': _L0_ffn_in['lut'], 'L0_ffn_gate_idx': _L0_ffn_in['gate_idx'], 'L0_ffn_up_idx': _L0_ffn_in['up_idx'], 'L0_ffn_down_idx': _L0_ffn_in['down_idx']}
    _x0 = _d['L0_attn_u']
    _d['L0_attn_u'] = jax.random.normal(jax.random.fold_in(jax.random.key(seed), 1), (4, 1024, 512), dtype=_x0.dtype)
    del _x0
    return _d

def reference(L0_attn_u, L0_attn_W_in, L0_attn_conv_w, L0_attn_conv_b, L0_attn_W_out, L0_attn_A_log, L0_attn_D_param, L0_attn_dt_bias, L0_ffn_lut, L0_ffn_gate_idx, L0_ffn_up_idx, L0_ffn_down_idx):

    def _L0_attn_ref(u, W_in, conv_w, conv_b, W_out, A_log, D_param, dt_bias):
        import jax, jax.numpy as jnp
        import numpy as np
        D_MODEL = 512
        D_STATE = 64
        D_CONV = 4
        HEADDIM = 64
        NHEADS = D_MODEL // HEADDIM
        D_IN_PROJ = 2 * D_MODEL + 2 * D_STATE + NHEADS
        CONV_DIM = D_MODEL + 2 * D_STATE
        B = 2
        L = 256

        def _mamba_fwd(u, W_in, conv_w, conv_b, W_out, A_log, D_param, dt_bias):
            Bb, Ll, _ = u.shape
            proj = u @ W_in.T
            z, x, B_toks, C_toks, dt_toks = jnp.split(proj, [D_MODEL, 2 * D_MODEL, 2 * D_MODEL + D_STATE, 2 * D_MODEL + 2 * D_STATE], axis=-1)
            xBC = jnp.concatenate([x, B_toks, C_toks], axis=-1).transpose(0, 2, 1)
            xBC = jax.lax.conv_general_dilated(xBC, conv_w, window_strides=(1,), padding=[(D_CONV - 1, 0)], feature_group_count=CONV_DIM) + conv_b[None, :, None]
            xBC = jax.nn.silu(xBC.transpose(0, 2, 1))
            x, B_toks, C_toks = jnp.split(xBC, [D_MODEL, D_MODEL + D_STATE], axis=-1)
            A = -jnp.exp(A_log)
            dt = jax.nn.softplus(dt_toks + dt_bias)
            dA = jnp.exp(dt * A)
            xh = x.reshape(Bb, Ll, NHEADS, HEADDIM)

            def step(S, inp):
                dA_t, dt_t, B_t, C_t, x_t = inp
                S = S * dA_t[:, :, None, None] + jnp.einsum('bh,bn,bhp->bhpn', dt_t, B_t, x_t)
                y_t = jnp.einsum('bhpn,bn->bhp', S, C_t)
                return (S, y_t)
            S0 = jnp.zeros((Bb, NHEADS, HEADDIM, D_STATE), u.dtype)
            xs = (dA.transpose(1, 0, 2), dt.transpose(1, 0, 2), B_toks.transpose(1, 0, 2), C_toks.transpose(1, 0, 2), xh.transpose(1, 0, 2, 3))
            _, ys = jax.lax.scan(step, S0, xs)
            y = ys.transpose(1, 0, 2, 3) + D_param[None, None, :, None] * xh
            y = y * jax.nn.silu(z.reshape(Bb, Ll, NHEADS, HEADDIM))
            return y.reshape(Bb, Ll, D_MODEL) @ W_out.T
        return _mamba_fwd(u, W_in, conv_w, conv_b, W_out, A_log, D_param, dt_bias)

    def _L0_ffn_ref(x, lut, gate_idx, up_idx, down_idx):
        import jax, jax.numpy as jnp
        import numpy as np
        HIDDEN = 512
        INTER = 1376
        LUT_SIZE = 16

        def _ghost_linear(x, idx, lut):
            w = lut[idx]
            return jnp.einsum('bsh,oh->bso', x, w)
        gate = _ghost_linear(x, gate_idx, lut)
        up = _ghost_linear(x, up_idx, lut)
        h = jax.nn.silu(gate) * up
        return _ghost_linear(h, down_idx, lut)
    x = L0_attn_u
    x = x + _layernorm(_L0_attn_ref(_layernorm(x, axis=-1), L0_attn_W_in, L0_attn_conv_w, L0_attn_conv_b, L0_attn_W_out, L0_attn_A_log, L0_attn_D_param, L0_attn_dt_bias), axis=-1)
    x = x + _layernorm(_L0_ffn_ref(_layernorm(x, axis=-1), L0_ffn_lut, L0_ffn_gate_idx, L0_ffn_up_idx, L0_ffn_down_idx), axis=-1)
    return x

_drawn_inputs = setup_inputs


def setup_inputs(seed=0):
    import zlib

    import numpy as np

    out = dict(_drawn_inputs(seed))
    spreads = {'L0_attn_conv_b': (0.0, 0.1), 'L0_attn_D_param': (1.0, 0.2)}
    factors = {}
    for name, (base, spread) in spreads.items():
        noise = np.random.default_rng([zlib.crc32(name.encode()), seed]).standard_normal(out[name].shape)
        drawn = base * np.exp(spread * noise) if base else spread * noise
        out[name] = jnp.asarray(drawn.astype(out[name].dtype))
    for name, factor in factors.items():
        out[name] = (out[name] * factor).astype(out[name].dtype)
    return out
```

```python
from contextlib import ExitStack

import concourse.bass as bass
from concourse import mybir

P = 128
F32 = mybir.dt.float32
F16 = mybir.dt.float16
I32 = mybir.dt.int32
ALU = mybir.AluOpType
ACT = mybir.ActivationFunctionType
AX_X = mybir.AxisListType.X
AX_XY = mybir.AxisListType.XY
RMAX = bass.bass_isa.ReduceOp.max

EPS = 1e-5
D = 512
KC = D // P
NST = 64
HEADS = 8
HD = D // HEADS
TAPS = 4
HALO = TAPS - 1
INTER = 1376
CODES = 16
TILE = 512
SUB = TILE // P
HALVES = 2
FB = 5
MB = -(-INTER // P)
LAST_OF_SLOT = [MB - (MB - 1 - m) % 2 for m in range(2)]
MW = [min(P, INTER - P * m) for m in range(MB)]

X0 = D
B0 = 2 * D
DT0 = 2 * D + 2 * NST
D_IN = DT0 + HEADS

GATE0, UP0, DOWN0 = 0, KC * INTER, 2 * KC * INTER
WCOLS = DOWN0 + MB * D
UNIT = 832
HUNIT = UNIT // 2
UNITS = WCOLS // UNIT
MASKS = 4
YSTEPS = 9
OSTEPS = 7
assert UNITS * UNIT == WCOLS and UNITS % 2 == 0

XS = 2.0 ** 10
WS = 2.0 ** 14
TINY = 2.0 ** -60
HSCALE = 2.0 ** -54


class Signal:

    def __init__(self, sem, per, step=1, credit=False):
        self.sem, self.per, self.step, self.credit = sem, per, step, credit

    def inc(self, ins):
        ins.then_inc(self.sem, self.step)

    def start(self, eng):
        eng.sem_inc(self.sem, self.per * self.step)

    def now(self, t, k):
        ahead = self.per if self.credit else 0
        return (t * self.per + (k + ahead)) * self.step

    def prev(self, t, k):
        assert self.credit
        return (t * self.per + k) * self.step


def wait_apart(eng, sem, value, passed):
    eng.wait_ge(sem, value)
    eng.sem_inc(passed, 1)


def sandwich_kernel(nc, u, w_in_t, conv_w, conv_b, w_out_t, a_log, d_param, dt_bias, lut, codes, out):
    T = u.shape[0]
    TILES = T // TILE
    BATCHES = TILES // HALVES
    u_tiles = u.rearrange("(n s p) d -> n p s d", s=SUB, p=P)
    out_tiles = out.rearrange("(n s p) d -> n p s d", s=SUB, p=P)
    x1_dram = nc.dram_tensor("x1_scratch", [T, D], F32).ap()
    x1_chunks = x1_dram.rearrange("(c p) d -> c p d", p=P)
    x1_tiles = x1_dram.rearrange("(n s p) d -> n p s d", s=SUB, p=P)

    ctx = ExitStack()
    with ctx:
        def sb(name, shape, dt=F32):
            return ctx.enter_context(nc.sbuf_tensor(name, shape, dt))

        def sem(name):
            return ctx.enter_context(nc.semaphore(name))

        win_hi = sb("win_hi", [P, KC, D_IN], F16)
        win_lo = sb("win_lo", [P, KC, D_IN], F16)
        wout_hi = sb("wout_hi", [P, KC, D], F16)
        wout_lo = sb("wout_lo", [P, KC, D], F16)
        ffn_hi = sb("ffn_hi", [P, WCOLS], F16)
        ffn_lo = sb("ffn_lo", [P, WCOLS], F16)
        ident = sb("ident", [P, P])
        causal = sb("causal", [P, P])
        below = sb("below", [P, P])
        ones = sb("ones", [P, P])
        neg_half = sb("neg_half", [P, SUB])
        lut_sb = sb("lut_sb", [P, CODES])
        conv_w_sb = sb("conv_w_sb", [P, FB, TAPS])
        conv_b_sb = sb("conv_b_sb", [P, FB])
        dt_bias_sb = sb("dt_bias_sb", [P, HEADS])
        a_sb = sb("a_sb", [P, HEADS])
        d_sb = sb("d_sb", [P, HEADS])
        big = sb("big", [P, 3])
        lowest = sb("lowest", [P, 3])
        expo = sb("expo", [P, 3])
        wscale = sb("wscale", [P, 3])
        c_in = sb("c_in", [P, 1])
        c_in_half = sb("c_in_half", [P, 1])
        c_out = sb("c_out", [P, 1])
        c_gate_half = sb("c_gate_half", [P, 1])
        c_down = sb("c_down", [P, 1])
        lut_s = sb("lut_s", [P, CODES])
        lut_hi = sb("lut_hi", [P, CODES], F16)
        lut_hi32 = sb("lut_hi32", [P, CODES])
        lut_lo32 = sb("lut_lo32", [P, CODES])

        dve_passed, pool_passed = sem("dve_waits_passed"), sem("pool_waits_passed")
        banks = [ctx.enter_context(nc.psum_tensor(f"bank{i}", [P, 512], F32)) for i in range(8)]

        with ExitStack() as stage:
            w_in_f = stage.enter_context(nc.sbuf_tensor("w_in_f", [P, KC, D_IN], F32))
            w_out_f = stage.enter_context(nc.sbuf_tensor("w_out_f", [P, KC, D], F32))
            s_win, s_wout, s_small = sem("win_loaded"), sem("wout_loaded"), sem("small_loaded")
            s_fill, s_const = sem("constants_filled"), sem("constants_ready")
            s_big, s_all = sem("partition_maxima"), sem("global_maxima")
            s_step, s_alog = sem("scaling_steps"), sem("a_exponential")
            with nc.Block() as block:
                @block.sync
                def _(sp):
                    sp.dma_start(w_in_f[:], w_in_t.rearrange("(c p) n -> p c n", p=P)).then_inc(s_win, 16)
                    sp.dma_start(w_out_f[:], w_out_t.rearrange("(c p) n -> p c n", p=P)).then_inc(s_wout, 16)

                @block.scalar
                def _(act):
                    def row(v, n):
                        return v.rearrange("(a n) -> a n", a=1).broadcast_to((P, n))
                    act.dma_start(lut_sb[:], row(lut, CODES)).then_inc(s_small, 16)
                    act.dma_start(dt_bias_sb[:], row(dt_bias, HEADS)).then_inc(s_small, 16)
                    act.dma_start(a_sb[:], row(a_log, HEADS)).then_inc(s_small, 16)
                    act.dma_start(d_sb[:], row(d_param, HEADS)).then_inc(s_small, 16)
                    act.dma_start(conv_w_sb[:], conv_w.rearrange("(f p) k -> p f k", p=P)).then_inc(s_small, 16)
                    act.dma_start(conv_b_sb[:], conv_b.rearrange("(f p) -> p f", p=P),
                                  allow_slow_non_contiguous=True).then_inc(s_small, 16)
                    act.wait_ge(s_small, 96)
                    nc.scalar.activation(a_sb[:], a_sb[:], ACT.Exp).then_inc(s_alog, 1)

                @block.gpsimd
                def _(pool):
                    nc.gpsimd.memset(ident[:], 0.0).then_inc(s_fill, 1)
                    nc.gpsimd.memset(causal[:], 1.0).then_inc(s_fill, 1)
                    nc.gpsimd.memset(below[:], 1.0).then_inc(s_fill, 1)
                    nc.gpsimd.memset(ones[:], 1.0).then_inc(s_fill, 1)
                    nc.gpsimd.memset(neg_half[:], -0.5).then_inc(s_fill, 1)
                    pool.wait_ge(s_fill, 5)
                    nc.gpsimd.affine_select(out=ident[:], in_=ident[:], compare_op=ALU.not_equal, fill=1.0,
                                            base=0, pattern=[[-1, P]], channel_multiplier=1).then_inc(s_const, 1)
                    nc.gpsimd.affine_select(out=causal[:], in_=causal[:], compare_op=ALU.is_ge, fill=0.0,
                                            base=0, pattern=[[1, P]], channel_multiplier=-1).then_inc(s_const, 1)
                    nc.gpsimd.affine_select(out=below[:], in_=below[:], compare_op=ALU.is_gt, fill=0.0,
                                            base=0, pattern=[[-1, P]], channel_multiplier=1).then_inc(s_const, 1)
                    pool.wait_ge(s_big, 6)
                    nc.gpsimd.partition_all_reduce(big[:], lowest[:], P, RMAX).then_inc(s_all, 1)

                @block.vector
                def _(dve):
                    steps = [0]

                    def step(ins):
                        steps[0] += 1
                        ins.then_inc(s_step, 1)
                        dve.wait_ge(s_step, steps[0])

                    dve.wait_ge(s_small, 96)
                    dve.wait_ge(s_wout, 16)
                    dve.wait_ge(s_win, 16)
                    for n, (src, ax) in enumerate(((w_in_f[:], AX_XY), (w_out_f[:], AX_XY), (lut_sb[:], AX_X))):
                        nc.vector.tensor_reduce(big[:, n:n + 1], src, ax, ALU.max).then_inc(s_big, 1)
                    for n, (src, ax) in enumerate(((w_in_f[:], AX_XY), (w_out_f[:], AX_XY), (lut_sb[:], AX_X))):
                        ins = nc.vector.tensor_reduce(expo[:, n:n + 1], src, ax, ALU.min)
                        step(ins)
                    dve.wait_ge(s_big, 3)
                    for n in range(3):
                        nc.vector.scalar_tensor_tensor(lowest[:, n:n + 1], expo[:, n:n + 1], -1.0, big[:, n:n + 1],
                                                       ALU.mult, ALU.max).then_inc(s_big, 1)
                    dve.wait_ge(s_all, 1)
                    step(nc.vector.tensor_scalar(big[:], big[:], TINY, None, ALU.max))
                    step(nc.vector.tensor_scalar(expo[:].bitcast(I32), big[:].bitcast(I32), 0x7F800000, None,
                                                 ALU.bitwise_and))
                    step(nc.vector.reciprocal(wscale[:], expo[:]))
                    step(nc.vector.tensor_scalar(wscale[:], wscale[:], WS, None, ALU.mult))
                    step(nc.vector.tensor_scalar(c_in[:], expo[:, 0:1], 1.0 / (XS * WS), None, ALU.mult))
                    step(nc.vector.tensor_scalar(c_in_half[:], c_in[:], 0.5, None, ALU.mult))
                    step(nc.vector.tensor_scalar(c_out[:], c_in[:], expo[:, 1:2], 0.25 / (WS * WS), ALU.mult, ALU.mult))
                    step(nc.vector.tensor_scalar(c_gate_half[:], expo[:, 2:3], 0.5 / (XS * WS), None, ALU.mult))
                    step(nc.vector.tensor_scalar(c_down[:], expo[:, 2:3], expo[:, 2:3], 32.0 / WS, ALU.mult, ALU.mult))
                    step(nc.vector.tensor_scalar(c_down[:], c_down[:], expo[:, 2:3], None, ALU.mult))
                    dve.wait_ge(s_alog, 1)
                    step(nc.vector.tensor_scalar(a_sb[:], a_sb[:], -1.0, None, ALU.mult))
                    step(nc.vector.tensor_scalar(win_hi[:], w_in_f[:], wscale[:, 0:1], None, ALU.mult))
                    step(nc.vector.scalar_tensor_tensor(win_lo[:], w_in_f[:], wscale[:, 0:1], win_hi[:],
                                                        ALU.mult, ALU.subtract))
                    step(nc.vector.tensor_scalar(wout_hi[:], w_out_f[:], wscale[:, 1:2], None, ALU.mult))
                    step(nc.vector.scalar_tensor_tensor(wout_lo[:], w_out_f[:], wscale[:, 1:2], wout_hi[:],
                                                        ALU.mult, ALU.subtract))
                    step(nc.vector.tensor_scalar(lut_s[:], lut_sb[:], wscale[:, 2:3], None, ALU.mult))
                    step(nc.vector.tensor_copy(lut_hi[:], lut_s[:]))
                    step(nc.vector.tensor_copy(lut_hi32[:], lut_hi[:]))
                    step(nc.vector.tensor_sub(lut_lo32[:], lut_s[:], lut_hi32[:]))
                    dve.wait_ge(s_const, 3)

        with ExitStack() as stage:
            def st(name, shape, dt=F32):
                return stage.enter_context(nc.sbuf_tensor(name, shape, dt))
            diag_hi = st("diag_hi", [P, CODES, P], F16)
            diag_lo = st("diag_lo", [P, CODES, P], F16)
            codes_sb = [st(f"codes_sb{i}", [P, UNIT], I32) for i in range(2)]
            codes_h = [st(f"codes_h{i}", [P, UNIT], F16) for i in range(2)]
            mask = st("mask", [P, MASKS, UNIT], F16)
            s_diag = sem("diagonals_ready")
            loaded = [sem(f"codes_loaded{i}") for i in range(2)]
            as_half = Signal(sem("codes_as_half"), 1, credit=True)
            mask_ready = Signal(sem("mask_ready"), CODES, credit=True)
            mask_used = Signal(sem("mask_used"), CODES, credit=True)
            evacuated = Signal(sem("code_sums_evacuated"), 4, credit=True)
            with nc.Block() as block:
                @block.sync
                def _(sp):
                    with sp.Fori(0, UNITS // 2) as pair:
                        for i in range(2):
                            t = pair * 2 + i
                            sp.wait_ge(as_half.sem, as_half.prev(t, 0))
                            sp.dma_start(codes_sb[i][:], codes[:, bass.ds(t * UNIT, UNIT)]).then_inc(loaded[i], 16)

                @block.gpsimd
                def _(pool):
                    as_half.start(pool)
                    with pool.Fori(0, UNITS // 2) as pair:
                        for i in range(2):
                            t = pair * 2 + i
                            pool.wait_ge(loaded[i], pair * 16 + 16)
                            wait_apart(pool, mask_ready.sem, mask_ready.prev(t, 0), pool_passed)
                            as_half.inc(nc.gpsimd.tensor_copy(codes_h[i][:], codes_sb[i][:]))

                @block.vector
                def _(dve):
                    mask_ready.start(dve)
                    for j in range(CODES):
                        nc.vector.tensor_scalar(diag_hi[:, j, :], ident[:], lut_hi32[:, j:j + 1], None,
                                                ALU.mult).then_inc(s_diag, 1)
                        nc.vector.tensor_scalar(diag_lo[:, j, :], ident[:], lut_lo32[:, j:j + 1], None,
                                                ALU.mult).then_inc(s_diag, 1)
                    with dve.Fori(0, UNITS // 2) as pair:
                        for i in range(2):
                            t = pair * 2 + i
                            dve.wait_ge(as_half.sem, as_half.now(t, 1))
                            for j in range(CODES):
                                if j < MASKS:
                                    dve.wait_ge(mask_used.sem, mask_used.prev(t, CODES + 1 + j - MASKS))
                                else:
                                    dve.wait_ge(mask_used.sem, mask_used.now(t, 1 + j - MASKS))
                                mask_ready.inc(nc.vector.tensor_scalar(mask[:, j % MASKS, :], codes_h[i][:],
                                                                       float(j), None, ALU.is_equal))

                @block.tensor
                def _(pe):
                    mask_used.start(pe)
                    pe.wait_ge(s_diag, 2 * CODES)
                    with pe.Fori(0, UNITS // 2) as pair:
                        for i in range(2):
                            t = pair * 2 + i
                            b = banks[4 * i:4 * i + 4]
                            pe.wait_ge(evacuated.sem, evacuated.prev(t, 0))
                            for j in range(CODES):
                                pe.wait_ge(mask_ready.sem, mask_ready.now(t, j + 1))
                                for n, dg in enumerate((diag_hi, diag_lo)):
                                    for half in range(2):
                                        last = nc.tensor.matmul(b[2 * n + half][:, 0:HUNIT], dg[:, j, :],
                                                                mask[:, j % MASKS, half * HUNIT:(half + 1) * HUNIT],
                                                                start=(j == 0), stop=(j == CODES - 1))
                                mask_used.inc(last)

                @block.scalar
                def _(act):
                    evacuated.start(act)
                    with act.Fori(0, UNITS // 2) as pair:
                        for i in range(2):
                            t = pair * 2 + i
                            b = banks[4 * i:4 * i + 4]
                            act.wait_ge(mask_used.sem, mask_used.now(t, CODES))
                            for n, dst in enumerate((ffn_hi, ffn_lo)):
                                for half in range(2):
                                    evacuated.inc(nc.scalar.activation(
                                        dst[:, bass.ds(t * UNIT + half * HUNIT, HUNIT)],
                                        b[2 * n + half][:, 0:HUNIT], ACT.Copy))

        with ExitStack() as stage:
            def st(name, shape, dt=F32):
                return stage.enter_context(nc.sbuf_tensor(name, shape, dt))
            ut = [st(f"ut{i}", [P, SUB, D]) for i in range(HALVES)]
            stats = st("stats", [P, SUB, 6])
            mv = st("mv", [P, SUB, 2])
            vare = st("vare", [P, SUB])
            rstd = st("rstd", [P, SUB])
            xn = st("xn", [P, SUB, D])
            xt_hi = st("xt_hi", [P, KC, TILE], F16)
            xt_lo = st("xt_lo", [P, KC, TILE], F16)
            cin = st("cin", [P, FB, HALO + TILE])
            cacc = st("cacc", [P, 2, TILE])
            ctanh = st("ctanh", [P, 2, TILE])
            xs = st("xs", [P, KC, TILE])
            bs = st("bs", [NST, TILE])
            cs = st("cs", [NST, TILE])
            ztanh = st("ztanh", [P, D])
            zs = st("zs", [P, SUB, D])
            dtx = st("dtx", [P, SUB, HEADS])
            dte = st("dte", [P, SUB, HEADS])
            dtz = st("dtz", [P, SUB, HEADS])
            dtz2 = st("dtz2", [P, SUB, HEADS])
            dtp = st("dtp", [P, SUB, HEADS])
            dt = st("dt", [P, SUB, HEADS])
            dt4 = st("dt4", [P, SUB, HEADS])
            da = st("da", [P, SUB, HEADS])
            seg = st("seg", [P, 2, HEADS, P])
            decay = st("decay", [P, HEADS, P])
            gsb = st("gsb", [P, P])
            bt = st("bt", [P, NST])
            ex = st("ex", [P, 2, 3, HEADS])
            mt = st("mt", [P, HEADS, P])
            xdt = st("xdt", [P, D])
            xd = st("xd", [P, D])
            xw = st("xw", [P, D])
            state = st("state", [NST, D])
            state_d = st("state_d", [NST, D])
            y1 = st("y1", [P, D])
            y2 = st("y2", [P, D])
            ymax = st("ymax", [P, 1])
            yexp = st("yexp", [P, 1])
            yq = st("yq", [P, 1])
            yt_hi = st("yt_hi", [P, KC, P], F16)
            yt_lo = st("yt_lo", [P, KC, P], F16)
            ostat = st("ostat", [P, 6])
            omv = st("omv", [P, 2])
            octok = st("octok", [P, 1])
            ovar = st("ovar", [P, 1])
            orstd = st("orstd", [P, 1])
            oscale = st("oscale", [P, 1])
            on = st("on", [P, D])
            x1 = st("x1", [P, 2, D])

            u_loaded = [Signal(sem(f"u_loaded{i}"), 1, step=16) for i in range(HALVES)]
            ln_steps = Signal(sem("ln_steps"), 4 * SUB)
            rstd_ready = Signal(sem("rstd_ready"), 1)
            xt_filled = Signal(sem("xt_transposed"), KC)
            xhi_ready = Signal(sem("xt_hi_ready"), KC)
            xlo_ready = Signal(sem("xt_lo_ready"), KC)
            proj_done = Signal(sem("conv_inputs_projected"), FB)
            cin_ready = Signal(sem("conv_inputs_ready"), FB)
            dt_done = Signal(sem("dt_projected"), 1)
            dt_steps = Signal(sem("dt_steps"), 18)
            dt_exp = Signal(sem("dt_exponential"), 1)
            z_done = Signal(sem("z_projected"), SUB)
            ztanh_ready = Signal(sem("z_tanh_ready"), SUB)
            zs_ready = Signal(sem("z_gate_ready"), SUB, credit=True)
            conv_steps = Signal(sem("conv_steps"), FB * TAPS)
            ctanh_ready = Signal(sem("conv_tanh_ready"), FB)
            xs_ready = Signal(sem("conv_silu_ready"), FB + 1)
            halo_ready = Signal(sem("halo_ready"), 1)
            xtok_done = Signal(sem("x_tokens_transposed"), SUB)
            small_done = Signal(sem("gram_and_sums_done"), SUB)
            seg_ready = Signal(sem("segment_terms_ready"), SUB * 2)
            seg_done = Signal(sem("segment_sums_done"), SUB)
            decay_ready = Signal(sem("decay_ready"), SUB * 2)
            small_read = Signal(sem("sums_exponentiated"), SUB * 2)
            gram_ready = Signal(sem("gram_masked"), SUB, credit=True)
            mt_ready = Signal(sem("decayed_gram_ready"), SUB, credit=True)
            xtok_read = Signal(sem("x_tokens_read"), SUB * 2)
            xw_ready = Signal(sem("x_weighted_ready"), SUB, credit=True)
            stated = Signal(sem("state_decayed"), SUB)
            state_ready = Signal(sem("state_ready"), SUB, credit=True)
            state_cleared = Signal(sem("state_cleared"), 1)
            y_done = Signal(sem("y_inner_done"), SUB, credit=True)
            yi_done = Signal(sem("y_carried_done"), SUB)
            s_done = Signal(sem("state_update_done"), SUB)
            y_steps = Signal(sem("y_steps"), SUB * YSTEPS, credit=True)
            yt_done = Signal(sem("y_transposed"), SUB)
            yhi_ready = Signal(sem("yt_hi_ready"), SUB)
            ylo_ready = Signal(sem("yt_lo_ready"), SUB, credit=True)
            o_done = Signal(sem("out_projected"), SUB, credit=True)
            o_steps = Signal(sem("o_steps"), SUB * OSTEPS, credit=True)
            orstd_ready = Signal(sem("out_rstd_ready"), SUB)
            x1_ready = Signal(sem("x1_ready"), SUB, credit=True)
            x1_stored = [Signal(sem(f"x1_stored{i}"), SUB // 2, step=16, credit=True) for i in range(2)]

            NPP = KC + FB + 1 + SUB
            assert NPP % 2 == 0

            with nc.Block() as block:
                @block.sync
                def _(sp):
                    for g in x1_stored:
                        g.start(sp)
                    for half in range(HALVES):
                        u_loaded[half].inc(sp.dma_start(ut[half][:], u_tiles[half]))

                    def store_then_load(batch, more):
                        for half in range(HALVES):
                            t = batch * HALVES + half
                            for c in range(SUB):
                                sp.wait_ge(x1_ready.sem, x1_ready.now(t, c + 1))
                                x1_stored[c % 2].inc(sp.dma_start(x1_chunks[t * SUB + c], x1[:, c % 2, :]))
                            if more:
                                u_loaded[half].inc(sp.dma_start(ut[half][:], u_tiles[t + HALVES]))

                    with sp.Fori(0, BATCHES - 1) as batch:
                        store_then_load(batch, True)
                    store_then_load(BATCHES - 1, False)
                    for g in x1_stored:
                        sp.wait_ge(g.sem, g.now(TILES - 1, SUB // 2))

                @block.gpsimd
                def _(pool):
                    xw_ready.start(pool)
                    x1_ready.start(pool)
                    with pool.Fori(0, BATCHES) as batch:
                        for half in range(HALVES):
                            t = batch * HALVES + half
                            pool.wait_ge(ln_steps.sem, ln_steps.now(t, 3 * SUB))
                            rstd_ready.inc(nc.gpsimd.tensor_tensor(rstd[:], vare[:], neg_half[:], ALU.pow))
                            for c in range(SUB):
                                pool.wait_ge(xtok_read.sem, xtok_read.now(t, 2 * c + 1))
                                pool.wait_ge(small_read.sem, small_read.now(t, 2 * c + 1))
                                pool.wait_ge(s_done.sem, s_done.now(t, c))
                                xw_ready.inc(nc.gpsimd.tensor_tensor(
                                    xw[:].rearrange("p (h d) -> p h d", h=HEADS),
                                    xdt[:].rearrange("p (h d) -> p h d", h=HEADS),
                                    ex[:, c % 2, 1, :].unsqueeze(2).broadcast_to((P, HEADS, HD)), ALU.mult))
                                pool.wait_ge(o_steps.sem, o_steps.now(t, OSTEPS * c + 5))
                                orstd_ready.inc(nc.gpsimd.tensor_tensor(orstd[:], ovar[:], neg_half[:, 0:1], ALU.pow))
                                pool.wait_ge(o_steps.sem, o_steps.now(t, OSTEPS * (c + 1)))
                                g = x1_stored[c % 2]
                                pool.wait_ge(g.sem, g.prev(t, SUB // 2) if c < 2 else g.now(t, c // 2))
                                x1_ready.inc(nc.gpsimd.tensor_tensor(x1[:, c % 2, :], on[:], ut[half][:, c, :], ALU.add))

                @block.scalar
                def _(act):
                    with act.Fori(0, BATCHES) as batch:
                        for half in range(HALVES):
                            t = batch * HALVES + half
                            for k in range(KC):
                                act.wait_ge(xt_filled.sem, xt_filled.now(t, k + 1))
                                xhi_ready.inc(nc.scalar.activation(xt_hi[:, k, :], banks[k % 2][:], ACT.Copy))
                            for f in range(FB):
                                act.wait_ge(proj_done.sem, proj_done.now(t, f + 1))
                                if f == 0:
                                    act.wait_ge(halo_ready.sem, halo_ready.now(t, 1))
                                cin_ready.inc(nc.scalar.activation(cin[:, f, HALO:], banks[(KC + f) % 2][:],
                                                                   ACT.Identity, scale=c_in[:]))
                            act.wait_ge(dt_steps.sem, dt_steps.now(t, 3))
                            dt_exp.inc(nc.scalar.activation(dte[:], dtz[:], ACT.Exp, scale=-1.0))

                            def conv_tanh(f):
                                act.wait_ge(conv_steps.sem, conv_steps.now(t, TAPS * (f + 1)))
                                if f >= 2:
                                    act.wait_ge(xs_ready.sem, xs_ready.now(t, f - 1))
                                ctanh_ready.inc(nc.scalar.activation(ctanh[:, f % 2, :], cacc[:, f % 2, :], ACT.Tanh,
                                                                     scale=0.5))

                            def z_tanh(c):
                                act.wait_ge(z_done.sem, z_done.now(t, c + 1))
                                act.wait_ge(zs_ready.sem, zs_ready.now(t, c))
                                ztanh_ready.inc(nc.scalar.activation(ztanh[:], banks[(KC + FB + 1 + c) % 2][:],
                                                                     ACT.Tanh, scale=c_in_half[:]))

                            for f in range(FB):
                                conv_tanh(f)
                                if f >= 1:
                                    z_tanh(f - 1)

                            def exps(c):
                                act.wait_ge(small_done.sem, small_done.now(t, c + 1))
                                if c >= 2:
                                    act.wait_ge(y_steps.sem, y_steps.now(t, YSTEPS * (c - 2) + 3))
                                else:
                                    act.wait_ge(y_steps.sem, y_steps.prev(t, YSTEPS * (c + 2) + 3))
                                small_read.inc(nc.scalar.activation(ex[:, c % 2], banks[3][:, 192:216].rearrange(
                                    "p (k h) -> p k h", k=3), ACT.Exp))
                                act.wait_ge(s_done.sem, s_done.now(t, c))
                                small_read.inc(nc.scalar.activation(bt[:], banks[3][:, 128:192], ACT.Copy))
                                act.wait_ge(seg_done.sem, seg_done.now(t, c + 1))
                                act.wait_ge(mt_ready.sem, mt_ready.prev(t, SUB) if c == 0 else mt_ready.now(t, c))
                                for n in range(2):
                                    decay_ready.inc(nc.scalar.activation(
                                        decay[:, 4 * n:4 * n + 4, :],
                                        banks[4 + n][:].rearrange("p (h t) -> p h t", h=4), ACT.Exp))

                            def y_high(c):
                                act.wait_ge(yt_done.sem, yt_done.now(t, c + 1))
                                act.wait_ge(o_done.sem, o_done.prev(t, SUB) if c == 0 else o_done.now(t, c))
                                yhi_ready.inc(nc.scalar.activation(
                                    yt_hi[:], banks[4][:].rearrange("p (k t) -> p k t", k=KC), ACT.Copy))

                            exps(0)
                            for c in range(SUB):
                                if c + 1 < SUB:
                                    exps(c + 1)
                                y_high(c)

                @block.tensor
                def _(pe):
                    y_done.start(pe)
                    o_done.start(pe)
                    with pe.Fori(0, BATCHES) as batch:
                        for half in range(HALVES):
                            t = batch * HALVES + half

                            for k in range(KC):
                                if k < 2:
                                    pe.wait_ge(zs_ready.sem, zs_ready.prev(t, SUB - 1 + k))
                                else:
                                    pe.wait_ge(xlo_ready.sem, xlo_ready.now(t, k - 1))
                                for s in range(SUB):
                                    if k == 0:
                                        pe.wait_ge(ln_steps.sem, ln_steps.now(t, 3 * SUB + s + 1))
                                    last = nc.tensor.transpose(banks[k % 2][:, s * P:(s + 1) * P],
                                                               xn[:, s, k * P:(k + 1) * P], ident[:])
                                xt_filled.inc(last)

                            def split_products(out_ap, pairs):
                                n = len(pairs)
                                for i, (lhs, rhs) in enumerate(pairs):
                                    last = nc.tensor.matmul(out_ap, lhs, rhs, start=(i == 0), stop=(i == n - 1))
                                return last

                            pe.wait_ge(xlo_ready.sem, xlo_ready.now(t, KC))
                            for f in range(FB):
                                if f >= 2:
                                    pe.wait_ge(cin_ready.sem, cin_ready.now(t, f - 1))
                                cols = slice(X0 + f * P, X0 + (f + 1) * P)
                                proj_done.inc(split_products(banks[(KC + f) % 2][:], [
                                    (w[:, k, cols], x[:, k, :]) for k in range(KC)
                                    for w, x in ((win_hi, xt_hi), (win_hi, xt_lo), (win_lo, xt_hi))]))
                            pe.wait_ge(cin_ready.sem, cin_ready.now(t, FB - 1))
                            for c in range(SUB):
                                tok = slice(c * P, (c + 1) * P)
                                last = split_products(banks[(KC + FB) % 2][:, c * HEADS:(c + 1) * HEADS], [
                                    (x[:, k, tok], w[:, k, DT0:D_IN]) for k in range(KC)
                                    for w, x in ((win_hi, xt_hi), (win_lo, xt_hi), (win_hi, xt_lo))])
                            dt_done.inc(last)
                            for c in range(SUB):
                                if c == 0:
                                    pe.wait_ge(cin_ready.sem, cin_ready.now(t, FB))
                                elif c == 1:
                                    pe.wait_ge(dt_steps.sem, dt_steps.now(t, 1))
                                else:
                                    pe.wait_ge(zs_ready.sem, zs_ready.now(t, c - 1))
                                tok = slice(c * P, (c + 1) * P)
                                z_done.inc(split_products(banks[(KC + FB + 1 + c) % 2][:], [
                                    (x[:, k, tok], w[:, k, 0:D]) for k in range(KC)
                                    for w, x in ((win_hi, xt_hi), (win_lo, xt_hi), (win_hi, xt_lo))]))

                            def prepare(c):
                                tok = slice(c * P, (c + 1) * P)
                                if c == 0:
                                    pe.wait_ge(xs_ready.sem, xs_ready.now(t, FB + 1))
                                pe.wait_ge(state_ready.sem, state_ready.prev(t, SUB) if c == 0 else state_ready.now(t, c))
                                for k in range(KC):
                                    last = nc.tensor.transpose(banks[2][:, k * P:(k + 1) * P], xs[:, k, tok], ident[:])
                                xtok_done.inc(last)
                                pe.wait_ge(gram_ready.sem, gram_ready.prev(t, SUB) if c == 0 else gram_ready.now(t, c))
                                nc.tensor.matmul(banks[3][:, 0:P], bs[:, tok], cs[:, tok], start=True, stop=True)
                                nc.tensor.transpose(banks[3][:, 128:192], bs[:, tok], ident[0:NST, 0:NST])
                                pe.wait_ge(dt_steps.sem, dt_steps.now(t, 17))
                                nc.tensor.matmul(banks[3][:, 192:200], causal[:], da[:, c, :], start=True, stop=True)
                                nc.tensor.matmul(banks[3][:, 200:208], below[:], da[:, c, :], start=True, stop=True)
                                small_done.inc(nc.tensor.matmul(banks[3][:, 208:216], ones[:], da[:, c, :],
                                                                start=True, stop=True))
                                pe.wait_ge(seg_ready.sem, seg_ready.now(t, 2 * c + 2))
                                if c == 0:
                                    pe.wait_ge(ylo_ready.sem, ylo_ready.prev(t, SUB))
                                    pe.wait_ge(o_steps.sem, o_steps.prev(t, OSTEPS * SUB))
                                elif c >= 2:
                                    pe.wait_ge(ylo_ready.sem, ylo_ready.now(t, c - 1))
                                    pe.wait_ge(o_steps.sem, o_steps.now(t, OSTEPS * (c - 1)))
                                for n in range(2):
                                    last = nc.tensor.matmul(banks[4 + n][:], below[:],
                                                            seg[:, c % 2, 4 * n:4 * n + 4, :].rearrange("p h t -> p (h t)"),
                                                            start=True, stop=True)
                                seg_done.inc(last)

                            def scan(c):
                                tok = slice(c * P, (c + 1) * P)
                                pe.wait_ge(y_steps.sem, y_steps.prev(t, YSTEPS * (SUB - 1) + 2) if c == 0
                                           else y_steps.now(t, YSTEPS * (c - 1) + 2))
                                pe.wait_ge(state_ready.sem, state_ready.prev(t, SUB) if c == 0
                                           else state_ready.now(t, c))
                                if half == 0 and c == 0:
                                    pe.wait_ge(state_cleared.sem, state_cleared.now(batch, 1))
                                yi_done.inc(nc.tensor.matmul(banks[7][:], cs[:, tok], state[:], start=True, stop=True))
                                pe.wait_ge(xtok_read.sem, xtok_read.now(t, 2 * c + 2))
                                pe.wait_ge(mt_ready.sem, mt_ready.now(t, c + 1))
                                for h in range(HEADS):
                                    last = nc.tensor.matmul(banks[6][:, h * HD:(h + 1) * HD], mt[:, h, :],
                                                            xdt[:, h * HD:(h + 1) * HD], start=True, stop=True)
                                y_done.inc(last)
                                pe.wait_ge(small_read.sem, small_read.now(t, 2 * c + 2))
                                pe.wait_ge(xw_ready.sem, xw_ready.now(t, c + 1))
                                s_done.inc(nc.tensor.matmul(banks[2][0:NST, :], bt[:], xw[:], start=True, stop=True))

                            def project(c):
                                pe.wait_ge(y_steps.sem, y_steps.now(t, YSTEPS * (c + 1)))
                                m = min(c + 2, SUB)
                                pe.wait_ge(decay_ready.sem, decay_ready.now(t, 2 * m))
                                for k in range(KC):
                                    last = nc.tensor.transpose(banks[4][:, k * P:(k + 1) * P],
                                                               y1[:, k * P:(k + 1) * P], ident[:])
                                yt_done.inc(last)
                                pe.wait_ge(ylo_ready.sem, ylo_ready.now(t, c + 1))
                                pe.wait_ge(o_steps.sem, o_steps.prev(t, OSTEPS * SUB) if c == 0
                                           else o_steps.now(t, OSTEPS * c))
                                o_done.inc(split_products(banks[5][:], [
                                    (y[:, k, :], w[:, k, :]) for k in range(KC)
                                    for y, w in ((yt_hi, wout_hi), (yt_hi, wout_lo), (yt_lo, wout_hi))]))

                            prepare(0)
                            for c in range(SUB):
                                scan(c)
                                if c + 1 < SUB:
                                    prepare(c + 1)
                                project(c)

                @block.vector
                def _(dve):
                    for g in (zs_ready, gram_ready, mt_ready, state_ready, y_steps, ylo_ready, o_steps):
                        g.start(dve)
                    with dve.Fori(0, BATCHES) as batch:
                        for half in range(HALVES):
                            t = batch * HALVES + half

                            def chain(sig, k, ins):
                                sig.inc(ins)
                                dve.wait_ge(sig.sem, sig.now(t, k))

                            dve.wait_ge(u_loaded[half].sem, u_loaded[half].now(batch, 1))
                            for s in range(SUB):
                                ln_steps.inc(nc.vector.bn_stats(stats[:, s, :], ut[half][:, s, :]))
                            for s in range(SUB):
                                wait_apart(dve, ln_steps.sem, ln_steps.now(t, s + 1), dve_passed)
                                ln_steps.inc(nc.vector.bn_aggr(mv[:, s, :], stats[:, s, :]))
                            for s in range(SUB):
                                dve.wait_ge(ln_steps.sem, ln_steps.now(t, SUB + s + 1))
                                ln_steps.inc(nc.vector.tensor_scalar(vare[:, s:s + 1], mv[:, s, 1:2], 1.0 / XS ** 2,
                                                                     EPS / XS ** 2, ALU.mult, ALU.add))
                            dve.wait_ge(rstd_ready.sem, rstd_ready.now(t, 1))
                            for s in range(SUB):
                                ln_steps.inc(nc.vector.tensor_scalar(xn[:, s, :], ut[half][:, s, :], mv[:, s, 0:1],
                                                                     rstd[:, s:s + 1], ALU.subtract, ALU.mult))
                            if half == 0:
                                halo_ready.inc(nc.vector.memset(cin[:, :, 0:HALO], 0.0))
                                dve.wait_ge(halo_ready.sem, halo_ready.now(t, 1))
                                state_cleared.inc(nc.vector.memset(state[:], 0.0))
                            else:
                                halo_ready.inc(nc.vector.tensor_copy(cin[:, :, 0:HALO], cin[:, :, TILE:TILE + HALO]))
                                dve.wait_ge(halo_ready.sem, halo_ready.now(t, 1))
                            for k in range(KC):
                                dve.wait_ge(xhi_ready.sem, xhi_ready.now(t, k + 1))
                                xlo_ready.inc(nc.vector.tensor_sub(xt_lo[:, k, :], banks[k % 2][:], xt_hi[:, k, :]))

                            def conv(f):
                                dve.wait_ge(cin_ready.sem, cin_ready.now(t, f + 1))
                                dve.wait_ge(xs_ready.sem, xs_ready.now(t, max(f - 1, 0)))
                                k0 = TAPS * f
                                chain(conv_steps, k0 + 1, nc.vector.tensor_scalar(
                                    cacc[:, f % 2, :], cin[:, f, 0:TILE], conv_w_sb[:, f, 0:1], conv_b_sb[:, f:f + 1],
                                    ALU.mult, ALU.add))
                                for k in range(1, TAPS):
                                    ins = nc.vector.scalar_tensor_tensor(
                                        cacc[:, f % 2, :], cin[:, f, k:k + TILE], conv_w_sb[:, f, k:k + 1], cacc[:, f % 2, :],
                                        ALU.mult, ALU.add)
                                    if k < TAPS - 1:
                                        chain(conv_steps, k0 + k + 1, ins)
                                    else:
                                        conv_steps.inc(ins)

                            def conv_silu(f):
                                dve.wait_ge(conv_steps.sem, conv_steps.now(t, TAPS * (f + 1)))
                                dve.wait_ge(ctanh_ready.sem, ctanh_ready.now(t, f + 1))
                                if f < KC:
                                    xs_ready.inc(nc.vector.scalar_tensor_tensor(
                                        xs[:, f, :], ctanh[:, f % 2, :], 1.0, cacc[:, f % 2, :], ALU.add, ALU.mult))
                                else:
                                    for dst, lo in ((bs, 0), (cs, NST)):
                                        xs_ready.inc(nc.vector.scalar_tensor_tensor(
                                            dst[:], ctanh[lo:lo + NST, f % 2, :], 1.0, cacc[lo:lo + NST, f % 2, :],
                                            ALU.add, ALU.mult))

                            def z_gate(c):
                                dve.wait_ge(ztanh_ready.sem, ztanh_ready.now(t, c + 1))
                                zs_ready.inc(nc.vector.scalar_tensor_tensor(
                                    zs[:, c, :], ztanh[:], 1.0, banks[(KC + FB + 1 + c) % 2][:],
                                    ALU.add, ALU.mult))

                            def time_steps():
                                dve.wait_ge(dt_done.sem, dt_done.now(t, 1))
                                chain(dt_steps, 1, nc.vector.scalar_tensor_tensor(
                                    dtx[:], banks[(KC + FB) % 2][:, 0:SUB * HEADS].rearrange("p (s h) -> p s h", s=SUB),
                                    c_in[:], dt_bias_sb[:].unsqueeze(1).broadcast_to((P, SUB, HEADS)),
                                    ALU.mult, ALU.add))
                                chain(dt_steps, 2, nc.vector.tensor_scalar(dtp[:], dtx[:], -1.0, None, ALU.mult))
                                chain(dt_steps, 3, nc.vector.tensor_tensor(dtz[:], dtx[:], dtp[:], ALU.max))
                                dve.wait_ge(dt_exp.sem, dt_exp.now(t, 1))
                                chain(dt_steps, 4, nc.vector.tensor_scalar(dtp[:], dte[:], 2.0, None, ALU.add))
                                chain(dt_steps, 5, nc.vector.reciprocal(dtp[:], dtp[:]))
                                chain(dt_steps, 6, nc.vector.tensor_tensor(dtz[:], dte[:], dtp[:], ALU.mult))
                                chain(dt_steps, 7, nc.vector.tensor_tensor(dtz2[:], dtz[:], dtz[:], ALU.mult))
                                chain(dt_steps, 8, nc.vector.tensor_scalar(dtp[:], dtz2[:], 2.0 / 15, None, ALU.mult))
                                for n, k in enumerate((13, 11, 9, 7, 5)):
                                    chain(dt_steps, 9 + n, nc.vector.scalar_tensor_tensor(
                                        dtp[:], dtp[:], 2.0 / k, dtz2[:], ALU.add, ALU.mult))
                                chain(dt_steps, 14, nc.vector.scalar_tensor_tensor(
                                    dtp[:], dtp[:], 2.0 / 3, dtz2[:], ALU.add, ALU.mult))
                                chain(dt_steps, 15, nc.vector.scalar_tensor_tensor(
                                    dtp[:], dtp[:], 2.0, dtz[:], ALU.add, ALU.mult))
                                chain(dt_steps, 16, nc.vector.scalar_tensor_tensor(
                                    dt[:], dtx[:], 0.0, dtp[:], ALU.max, ALU.add))
                                dt_steps.inc(nc.vector.tensor_tensor(
                                    da[:], dt[:], a_sb[:].unsqueeze(1).broadcast_to((P, SUB, HEADS)), ALU.mult))
                                chain(dt_steps, 18, nc.vector.tensor_scalar(dt4[:], dt[:], 0.25, None, ALU.mult))

                            def segment_terms(c):
                                if c >= 2:
                                    dve.wait_ge(seg_done.sem, seg_done.now(t, c - 1))
                                for n in range(2):
                                    seg_ready.inc(nc.vector.tensor_tensor(
                                        seg[:, c % 2, 4 * n:4 * n + 4, :],
                                        causal[:].unsqueeze(1).broadcast_to((P, 4, P)),
                                        da[:, c, 4 * n:4 * n + 4].unsqueeze(2).broadcast_to((P, 4, P)), ALU.mult))

                            conv(0)
                            time_steps()
                            conv(1)
                            conv_silu(0)
                            for f in range(2, FB):
                                z_gate(f - 2)
                                conv(f)
                                conv_silu(f - 1)
                            z_gate(FB - 2)
                            conv_silu(FB - 1)
                            segment_terms(0)

                            def combine(c):
                                if c + 1 < SUB:
                                    segment_terms(c + 1)
                                heads = (P, HEADS, HD)
                                dve.wait_ge(xtok_done.sem, xtok_done.now(t, c + 1))
                                dve.wait_ge(y_done.sem, y_done.prev(t, SUB) if c == 0 else y_done.now(t, c))
                                dve.wait_ge(xw_ready.sem, xw_ready.prev(t, SUB) if c == 0 else xw_ready.now(t, c))
                                x_tok = banks[2][:].rearrange("p (h d) -> p h d", h=HEADS)
                                xtok_read.inc(nc.vector.tensor_tensor(
                                    xdt[:].rearrange("p (h d) -> p h d", h=HEADS), x_tok,
                                    dt4[:, c, :].unsqueeze(2).broadcast_to(heads), ALU.mult))
                                xtok_read.inc(nc.vector.tensor_tensor(
                                    xd[:].rearrange("p (h d) -> p h d", h=HEADS), x_tok,
                                    d_sb[:].unsqueeze(2).broadcast_to(heads), ALU.mult))
                                dve.wait_ge(small_read.sem, small_read.now(t, 2 * c + 2))
                                chain(gram_ready, c + 1, nc.vector.tensor_tensor(gsb[:], banks[3][:, 0:P], causal[:],
                                                                                 ALU.mult))
                                dve.wait_ge(decay_ready.sem, decay_ready.now(t, 2 * c + 2))
                                mt_ready.inc(nc.vector.tensor_tensor(
                                    mt[:], decay[:], gsb[:].unsqueeze(1).broadcast_to((P, HEADS, P)), ALU.mult))
                                dve.wait_ge(yi_done.sem, yi_done.now(t, c + 1))
                                if half == 0 and c == 0:
                                    dve.wait_ge(state_cleared.sem, state_cleared.now(batch, 1))
                                else:
                                    dve.wait_ge(state_ready.sem, state_ready.prev(t, SUB) if c == 0
                                                else state_ready.now(t, c))
                                chain(stated, c + 1, nc.vector.tensor_tensor(
                                    state_d[:].rearrange("p (h d) -> p h d", h=HEADS),
                                    state[:].rearrange("p (h d) -> p h d", h=HEADS),
                                    ex[0:NST, c % 2, 2, :].unsqueeze(2).broadcast_to((NST, HEADS, HD)), ALU.mult))
                                y0 = YSTEPS * c
                                chain(y_steps, y0 + 1, nc.vector.tensor_tensor(
                                    y1[:].rearrange("p (h d) -> p h d", h=HEADS),
                                    banks[7][:].rearrange("p (h d) -> p h d", h=HEADS),
                                    ex[:, c % 2, 0, :].unsqueeze(2).broadcast_to(heads), ALU.mult))
                                dve.wait_ge(y_done.sem, y_done.now(t, c + 1))
                                chain(y_steps, y0 + 2, nc.vector.tensor_tensor(y2[:], y1[:], banks[6][:], ALU.add))
                                dve.wait_ge(s_done.sem, s_done.now(t, c + 1))
                                state_ready.inc(nc.vector.tensor_tensor(state[:], state_d[:], banks[2][0:NST, :], ALU.add))
                                dve.wait_ge(xtok_read.sem, xtok_read.now(t, 2 * c + 2))
                                chain(y_steps, y0 + 3, nc.vector.tensor_tensor(y1[:], y2[:], xd[:], ALU.add))
                                chain(y_steps, y0 + 4, nc.vector.tensor_tensor(y2[:], y1[:], zs[:, c, :], ALU.mult))
                                chain(y_steps, y0 + 5, nc.vector.tensor_reduce(ymax[:], y2[:], AX_X, ALU.max,
                                                                               apply_absolute_value=True))
                                chain(y_steps, y0 + 6, nc.vector.tensor_scalar(ymax[:], ymax[:], TINY, None, ALU.max))
                                chain(y_steps, y0 + 7, nc.vector.tensor_scalar(
                                    yexp[:].bitcast(I32), ymax[:].bitcast(I32), 0x7F800000, None, ALU.bitwise_and))
                                chain(y_steps, y0 + 8, nc.vector.reciprocal(yq[:], yexp[:]))
                                chain(y_steps, y0 + 9, nc.vector.tensor_scalar(y1[:], y2[:], yq[:], WS,
                                                                               ALU.mult, ALU.mult))

                            def finish(c):
                                dve.wait_ge(yhi_ready.sem, yhi_ready.now(t, c + 1))
                                ylo_ready.inc(nc.vector.tensor_sub(
                                    yt_lo[:], banks[4][:].rearrange("p (k t) -> p k t", k=KC), yt_hi[:]))
                                dve.wait_ge(o_done.sem, o_done.now(t, c + 1))
                                o0 = OSTEPS * c
                                o_steps.inc(nc.vector.bn_stats(ostat[:], banks[5][:]))
                                wait_apart(dve, o_steps.sem, o_steps.now(t, o0 + 1), dve_passed)
                                chain(o_steps, o0 + 2, nc.vector.bn_aggr(omv[:], ostat[:]))
                                chain(o_steps, o0 + 3, nc.vector.tensor_scalar(octok[:], yexp[:], c_out[:], None, ALU.mult))
                                chain(o_steps, o0 + 4, nc.vector.tensor_scalar(oscale[:], omv[:, 1:2], octok[:], octok[:],
                                                                               ALU.mult, ALU.mult))
                                chain(o_steps, o0 + 5, nc.vector.tensor_scalar(ovar[:], oscale[:], EPS, None, ALU.add))
                                dve.wait_ge(orstd_ready.sem, orstd_ready.now(t, c + 1))
                                chain(o_steps, o0 + 6, nc.vector.tensor_scalar(oscale[:], orstd[:], octok[:], None,
                                                                               ALU.mult))
                                dve.wait_ge(x1_ready.sem, x1_ready.prev(t, SUB) if c == 0 else x1_ready.now(t, c))
                                o_steps.inc(nc.vector.tensor_scalar(on[:], banks[5][:], omv[:, 0:1], oscale[:],
                                                                    ALU.subtract, ALU.mult))

                            for c in range(SUB):
                                combine(c)
                                finish(c)

        with ExitStack() as stage:
            def st(name, shape, dt=F32):
                return stage.enter_context(nc.sbuf_tensor(name, shape, dt))
            xf = [st(f"xf{i}", [P, SUB, D]) for i in range(2)]
            stats = st("fstats", [P, SUB, 6])
            mv = st("fmv", [P, SUB, 2])
            vare = st("fvare", [P, SUB])
            rstd = st("frstd", [P, SUB])
            xn = st("fxn", [P, SUB, D])
            xt_hi = st("fxt_hi", [P, KC, TILE], F16)
            xt_lo = st("fxt_lo", [P, KC, TILE], F16)
            gtanh = st("gtanh", [P, 2, TILE])
            gsilu = st("gsilu", [P, 2, TILE])
            hf = st("hf", [P, 2, TILE])
            h_hi = st("h_hi", [P, MB, TILE], F16)
            h_lo = st("h_lo", [P, MB, TILE], F16)
            dstat = st("dstat", [P, SUB, 6])
            dmv = st("dmv", [P, SUB, 2])
            dvar = st("dvar", [P, SUB])
            drstd = st("drstd", [P, SUB])
            dscale = st("dscale", [P, SUB])
            dn = st("dn", [P, 2, D])
            res = st("res", [P, 2, D])

            x_loaded = [Signal(sem(f"x1_loaded{i}"), 1, step=16) for i in range(2)]
            ln_steps = Signal(sem("f_ln_steps"), 4 * SUB)
            rstd_ready = Signal(sem("f_rstd_ready"), 1)
            xt_filled = Signal(sem("f_xt_transposed"), KC)
            xhi_ready = Signal(sem("f_xt_hi_ready"), KC)
            xlo_ready = Signal(sem("f_xt_lo_ready"), KC)
            gate_done = Signal(sem("gate_done"), MB)
            up_done = Signal(sem("up_done"), MB)
            gtanh_ready = Signal(sem("gate_tanh_ready"), MB)
            gsilu_ready = Signal(sem("gate_silu_ready"), MB, credit=True)
            hf_ready = Signal(sem("h_ready"), MB, credit=True)
            hhi_ready = Signal(sem("h_hi_ready"), MB)
            hlo_ready = Signal(sem("h_lo_ready"), MB)
            down_done = Signal(sem("down_done"), SUB, credit=True)
            d_steps = Signal(sem("down_ln_steps"), SUB * 5)
            drstd_ready = Signal(sem("down_rstd_ready"), SUB)
            dn_ready = Signal(sem("down_normalised"), SUB, credit=True)
            res_ready = Signal(sem("output_ready"), SUB, credit=True)
            res_stored = [Signal(sem(f"output_stored{i}"), SUB // 2, step=16, credit=True) for i in range(2)]
            out_chunks = out.rearrange("(c p) d -> c p d", p=P)

            with nc.Block() as block:
                @block.sync
                def _(sp):
                    for g in res_stored:
                        g.start(sp)
                    for i in range(2):
                        x_loaded[i].inc(sp.dma_start(xf[i][:], x1_tiles[i]))

                    def store_then_load(pair, more):
                        for i in range(2):
                            t = pair * 2 + i
                            for c in range(SUB):
                                sp.wait_ge(res_ready.sem, res_ready.now(t, c + 1))
                                res_stored[c % 2].inc(sp.dma_start(out_chunks[t * SUB + c], res[:, c % 2, :]))
                            if more:
                                x_loaded[i].inc(sp.dma_start(xf[i][:], x1_tiles[t + 2]))

                    with sp.Fori(0, TILES // 2 - 1) as pair:
                        store_then_load(pair, True)
                    store_then_load(TILES // 2 - 1, False)
                    for g in res_stored:
                        sp.wait_ge(g.sem, g.now(TILES - 1, SUB // 2))

                @block.gpsimd
                def _(pool):
                    res_ready.start(pool)
                    with pool.Fori(0, TILES // 2) as pair:
                        for i in range(2):
                            t = pair * 2 + i
                            pool.wait_ge(ln_steps.sem, ln_steps.now(t, 3 * SUB))
                            rstd_ready.inc(nc.gpsimd.tensor_tensor(rstd[:], vare[:], neg_half[:], ALU.pow))
                            for c in range(SUB):
                                pool.wait_ge(d_steps.sem, d_steps.now(t, 5 * c + 4))
                                drstd_ready.inc(nc.gpsimd.tensor_tensor(drstd[:, c:c + 1], dvar[:, c:c + 1],
                                                                        neg_half[:, 0:1], ALU.pow))
                                pool.wait_ge(dn_ready.sem, dn_ready.now(t, c + 1))
                                g = res_stored[c % 2]
                                pool.wait_ge(g.sem, g.prev(t, SUB // 2) if c < 2 else g.now(t, c // 2))
                                res_ready.inc(nc.gpsimd.tensor_tensor(res[:, c % 2, :], dn[:, c % 2, :],
                                                                      xf[i][:, c, :], ALU.add))

                @block.scalar
                def _(act):
                    with act.Fori(0, TILES // 2) as pair:
                        for i in range(2):
                            t = pair * 2 + i
                            for k in range(KC):
                                act.wait_ge(xt_filled.sem, xt_filled.now(t, k + 1))
                                xhi_ready.inc(nc.scalar.activation(xt_hi[:, k, :], banks[k % 2][:], ACT.Copy))
                            def high(m):
                                w = MW[m]
                                act.wait_ge(hf_ready.sem, hf_ready.now(t, m + 1))
                                if m == 0:
                                    act.wait_ge(down_done.sem, down_done.prev(t, SUB))
                                hhi_ready.inc(nc.scalar.activation(h_hi[0:w, m, :], hf[0:w, m % 2, :], ACT.Copy))
                            for m in range(MB):
                                w = MW[m]
                                act.wait_ge(gate_done.sem, gate_done.now(t, m + 1))
                                act.wait_ge(gsilu_ready.sem, gsilu_ready.prev(t, LAST_OF_SLOT[m]) if m < 2
                                            else gsilu_ready.now(t, m - 1))
                                gtanh_ready.inc(nc.scalar.activation(gtanh[0:w, m % 2, :], banks[2 + m % 2][0:w, :],
                                                                     ACT.Tanh, scale=c_gate_half[0:w, :]))
                                if m >= 1:
                                    high(m - 1)
                            high(MB - 1)

                @block.tensor
                def _(pe):
                    down_done.start(pe)
                    with pe.Fori(0, TILES // 2) as pair:
                        for i in range(2):
                            t = pair * 2 + i
                            for k in range(KC):
                                if k >= 2:
                                    pe.wait_ge(xlo_ready.sem, xlo_ready.now(t, k - 1))
                                for s in range(SUB):
                                    if k == 0:
                                        pe.wait_ge(ln_steps.sem, ln_steps.now(t, 3 * SUB + s + 1))
                                    last = nc.tensor.transpose(banks[k % 2][:, s * P:(s + 1) * P],
                                                               xn[:, s, k * P:(k + 1) * P], ident[:])
                                xt_filled.inc(last)
                            pe.wait_ge(xlo_ready.sem, xlo_ready.now(t, KC))
                            for m in range(MB):
                                w = MW[m]
                                for col0, base, done, free in ((GATE0, 2, gate_done, gsilu_ready), (UP0, 4, up_done, hf_ready)):
                                    if m < 2:
                                        pe.wait_ge(free.sem, free.prev(t, LAST_OF_SLOT[m]))
                                    else:
                                        pe.wait_ge(free.sem, free.now(t, m - 1))
                                    bank = banks[base + m % 2][0:w, :]
                                    for k in range(KC):
                                        c0 = col0 + k * INTER + m * P
                                        for n, (wt, x) in enumerate(((ffn_hi, xt_hi), (ffn_hi, xt_lo), (ffn_lo, xt_hi))):
                                            last = nc.tensor.matmul(bank, wt[:, c0:c0 + w], x[:, k, :],
                                                                    start=(k == 0 and n == 0),
                                                                    stop=(k == KC - 1 and n == 2))
                                    done.inc(last)
                            for c in range(SUB):
                                tok = slice(c * P, (c + 1) * P)
                                pe.wait_ge(dn_ready.sem, dn_ready.prev(t, SUB - 1 + c) if c < 2 else dn_ready.now(t, c - 1))
                                for m in range(MB):
                                    w = MW[m]
                                    if c == 0:
                                        pe.wait_ge(hlo_ready.sem, hlo_ready.now(t, m + 1))
                                    d0 = DOWN0 + m * D
                                    for n, (h, wt) in enumerate(((h_hi, ffn_hi), (h_hi, ffn_lo), (h_lo, ffn_hi))):
                                        last = nc.tensor.matmul(banks[6 + c % 2][:], h[0:w, m, tok], wt[0:w, d0:d0 + D],
                                                                start=(m == 0 and n == 0), stop=(m == MB - 1 and n == 2))
                                down_done.inc(last)

                @block.vector
                def _(dve):
                    for g in (gsilu_ready, hf_ready, dn_ready):
                        g.start(dve)
                    with dve.Fori(0, TILES // 2) as pair:
                        for i in range(2):
                            t = pair * 2 + i

                            def chain(sig, k, ins):
                                sig.inc(ins)
                                dve.wait_ge(sig.sem, sig.now(t, k))

                            dve.wait_ge(x_loaded[i].sem, x_loaded[i].now(pair, 1))
                            for s in range(SUB):
                                ln_steps.inc(nc.vector.bn_stats(stats[:, s, :], xf[i][:, s, :]))
                            for s in range(SUB):
                                wait_apart(dve, ln_steps.sem, ln_steps.now(t, s + 1), dve_passed)
                                ln_steps.inc(nc.vector.bn_aggr(mv[:, s, :], stats[:, s, :]))
                            for s in range(SUB):
                                dve.wait_ge(ln_steps.sem, ln_steps.now(t, SUB + s + 1))
                                ln_steps.inc(nc.vector.tensor_scalar(vare[:, s:s + 1], mv[:, s, 1:2], 1.0 / XS ** 2,
                                                                     EPS / XS ** 2, ALU.mult, ALU.add))
                            dve.wait_ge(rstd_ready.sem, rstd_ready.now(t, 1))
                            for s in range(SUB):
                                ln_steps.inc(nc.vector.tensor_scalar(xn[:, s, :], xf[i][:, s, :], mv[:, s, 0:1],
                                                                     rstd[:, s:s + 1], ALU.subtract, ALU.mult))
                            for k in range(KC):
                                dve.wait_ge(xhi_ready.sem, xhi_ready.now(t, k + 1))
                                xlo_ready.inc(nc.vector.tensor_sub(xt_lo[:, k, :], banks[k % 2][:], xt_hi[:, k, :]))

                            def low(m):
                                w = MW[m]
                                dve.wait_ge(hhi_ready.sem, hhi_ready.now(t, m + 1))
                                hlo_ready.inc(nc.vector.tensor_sub(h_lo[0:w, m, :], hf[0:w, m % 2, :], h_hi[0:w, m, :]))

                            for m in range(MB):
                                w = MW[m]
                                dve.wait_ge(gtanh_ready.sem, gtanh_ready.now(t, m + 1))
                                gsilu_ready.inc(nc.vector.scalar_tensor_tensor(
                                    gsilu[0:w, m % 2, :], gtanh[0:w, m % 2, :], 1.0, banks[2 + m % 2][0:w, :],
                                    ALU.add, ALU.mult))
                                dve.wait_ge(gsilu_ready.sem, gsilu_ready.now(t, m + 1))
                                dve.wait_ge(up_done.sem, up_done.now(t, m + 1))
                                hf_ready.inc(nc.vector.scalar_tensor_tensor(
                                    hf[0:w, m % 2, :], gsilu[0:w, m % 2, :], HSCALE, banks[4 + m % 2][0:w, :],
                                    ALU.mult, ALU.mult))
                                if m >= 1:
                                    low(m - 1)
                            low(MB - 1)
                            for c in range(SUB):
                                dve.wait_ge(down_done.sem, down_done.now(t, c + 1))
                                bank = banks[6 + c % 2]
                                d0 = 5 * c
                                d_steps.inc(nc.vector.bn_stats(dstat[:, c, :], bank[:]))
                                wait_apart(dve, d_steps.sem, d_steps.now(t, d0 + 1), dve_passed)
                                chain(d_steps, d0 + 2, nc.vector.bn_aggr(dmv[:, c, :], dstat[:, c, :]))
                                chain(d_steps, d0 + 3, nc.vector.tensor_scalar(dscale[:, c:c + 1], dmv[:, c, 1:2],
                                                                               c_down[:], c_down[:], ALU.mult, ALU.mult))
                                chain(d_steps, d0 + 4, nc.vector.tensor_scalar(dvar[:, c:c + 1], dscale[:, c:c + 1],
                                                                               EPS, None, ALU.add))
                                dve.wait_ge(drstd_ready.sem, drstd_ready.now(t, c + 1))
                                chain(d_steps, d0 + 5, nc.vector.tensor_scalar(dscale[:, c:c + 1], drstd[:, c:c + 1],
                                                                               c_down[:], None, ALU.mult))
                                dve.wait_ge(res_ready.sem, res_ready.prev(t, SUB - 1 + c) if c < 2
                                            else res_ready.now(t, c - 1))
                                dn_ready.inc(nc.vector.tensor_scalar(dn[:, c % 2, :], bank[:], dmv[:, c, 0:1],
                                                                     dscale[:, c:c + 1], ALU.subtract, ALU.mult))


def kernel(**inputs):
    import numpy as np
    import concourse.bacc as bacc
    from concourse.bass_utils import run_bass_kernel_spmd

    v = {k[3:]: np.asarray(a) for k, a in inputs.items()}
    B, L, _ = v["attn_u"].shape

    def blocks(codes_t):
        rows, n = codes_t.shape
        full = np.zeros((-(-rows // P) * P, n), codes_t.dtype)
        full[:rows] = codes_t
        return full.reshape(-1, P, n).transpose(1, 0, 2).reshape(P, -1)

    arrays = {
        "u": v["attn_u"].reshape(B * L, D),
        "w_in_t": v["attn_W_in"].T,
        "conv_w": v["attn_conv_w"].reshape(-1, TAPS),
        "conv_b": v["attn_conv_b"],
        "w_out_t": v["attn_W_out"].T,
        "a_log": v["attn_A_log"],
        "d_param": v["attn_D_param"],
        "dt_bias": v["attn_dt_bias"],
        "lut": v["ffn_lut"],
        "codes": np.concatenate([blocks(v["ffn_gate_idx"].T), blocks(v["ffn_up_idx"].T),
                                 blocks(v["ffn_down_idx"].T)], axis=1),
    }
    arrays = {k: np.ascontiguousarray(a) for k, a in arrays.items()}
    nc = bacc.Bacc("TRN2", target_bir_lowering=False, num_devices=1)
    args = [nc.dram_tensor(k, a.shape, mybir.dt.from_np(a.dtype), kind="ExternalInput").ap()
            for k, a in arrays.items()]
    out = nc.dram_tensor("out", (B * L, D), F32, kind="ExternalOutput").ap()
    sandwich_kernel(nc, *args, out)
    r = run_bass_kernel_spmd(nc, [arrays], core_ids=[0])
    return r.results[0]["out"].reshape(B, L, D)
```

```python
from contextlib import ExitStack

import concourse.bass as bass
from concourse import mybir

P = 128
F32 = mybir.dt.float32
F16 = mybir.dt.float16
I32 = mybir.dt.int32
ALU = mybir.AluOpType
ACT = mybir.ActivationFunctionType
AX_X = mybir.AxisListType.X
AX_XY = mybir.AxisListType.XY
RMAX = bass.bass_isa.ReduceOp.max

EPS = 1e-5
D = 512
KC = D // P
NST = 64
HEADS = 8
HD = D // HEADS
TAPS = 4
HALO = TAPS - 1
INTER = 1376
CODES = 16
TILE = 512
SUB = TILE // P
HALVES = 2
FB = 5
MB = -(-INTER // P)
LAST_OF_SLOT = [MB - (MB - 1 - m) % 2 for m in range(2)]
MW = [min(P, INTER - P * m) for m in range(MB)]

X0 = D
B0 = 2 * D
DT0 = 2 * D + 2 * NST
D_IN = DT0 + HEADS

GATE0, UP0, DOWN0 = 0, KC * INTER, 2 * KC * INTER
WCOLS = DOWN0 + MB * D
UNIT = 416
TILE_UNITS = 5
GROUP = 4
GROUPS = CODES // GROUP
YSTEPS = 11
OSTEPS = 7
CSTEPS = TAPS + 2

FRONT_USES = ["T0", "T1", "T2", "T3", "X0", "X1", "X2", "X3", "X4", "dt"]
USES = ["z0", "z1", "z2", "z3", "D0", "D0'", "T0", "T1", "T2", "T3", "D1", "D1'", "X0", "X1", "X2",
        "D2", "D2'", "X3", "X4", "dt", "D3", "D3'", "D4", "D4'"]
LAST_USES = [x for x in USES if x[0] not in "Xd"]
assert len(USES) % 2 == 0 and len(FRONT_USES) % 2 == 0

XS = 2.0 ** 10
WS = 2.0 ** 14
TINY = 2.0 ** -60
HSCALE = 2.0 ** -54


class Signal:

    def __init__(self, sem, per, step=1, credit=False):
        self.sem, self.per, self.step, self.credit = sem, per, step, credit

    def inc(self, ins):
        ins.then_inc(self.sem, self.step)

    def start(self, eng):
        eng.sem_inc(self.sem, self.per * self.step)

    def now(self, t, k):
        ahead = self.per if self.credit else 0
        return (t * self.per + (k + ahead)) * self.step

    def prev(self, t, k):
        assert self.credit
        return (t * self.per + k) * self.step


def wait_apart(eng, sem, value, passed):
    eng.wait_ge(sem, value)
    eng.sem_inc(passed, 1)


def sandwich_kernel(nc, u, w_in_t, conv_w, conv_b, w_out_t, a_log, d_param, dt_bias, lut, codes, out):
    T = u.shape[0]
    TILES = T // TILE
    BATCHES = TILES // HALVES
    assert TILES * TILE_UNITS * UNIT == WCOLS
    u_chunks = u.rearrange("(c p) d -> c p d", p=P)
    u_tiles = u.rearrange("(n s p) d -> n p s d", s=SUB, p=P)
    x1_dram = nc.dram_tensor("x1_scratch", [T, D], F32).ap()
    x1_chunks = x1_dram.rearrange("(c p) d -> c p d", p=P)
    x1_tiles = x1_dram.rearrange("(n s p) d -> n p s d", s=SUB, p=P)

    ctx = ExitStack()
    with ctx:
        def sb(name, shape, dt=F32):
            return ctx.enter_context(nc.sbuf_tensor(name, shape, dt))

        def sem(name):
            return ctx.enter_context(nc.semaphore(name))

        win_hi = sb("win_hi", [P, KC, D_IN], F16)
        win_lo = sb("win_lo", [P, KC, D_IN], F16)
        wout_hi = sb("wout_hi", [P, KC, D], F16)
        wout_lo = sb("wout_lo", [P, KC, D], F16)
        ffn_hi = sb("ffn_hi", [P, WCOLS], F16)
        ffn_lo = sb("ffn_lo", [P, WCOLS], F16)
        ident = sb("ident", [P, P])
        causal = sb("causal", [P, P])
        below = sb("below", [P, P])
        ones = sb("ones", [P, P])
        neg_half = sb("neg_half", [P, SUB])
        lut_sb = sb("lut_sb", [P, CODES])
        conv_w_sb = sb("conv_w_sb", [P, FB, TAPS])
        conv_b_sb = sb("conv_b_sb", [P, FB])
        dt_bias_sb = sb("dt_bias_sb", [P, HEADS])
        a_sb = sb("a_sb", [P, HEADS])
        d_sb = sb("d_sb", [P, HEADS])
        big = sb("big", [P, 3])
        lowest = sb("lowest", [P, 3])
        expo = sb("expo", [P, 3])
        wscale = sb("wscale", [P, 3])
        c_in = sb("c_in", [P, 1])
        c_in_half = sb("c_in_half", [P, 1])
        c_out = sb("c_out", [P, 1])
        c_gate_half = sb("c_gate_half", [P, 1])
        c_down = sb("c_down", [P, 1])
        lut_s = sb("lut_s", [P, CODES])
        lut_hi = sb("lut_hi", [P, CODES], F16)
        lut_hi32 = sb("lut_hi32", [P, CODES])
        lut_lo32 = sb("lut_lo32", [P, CODES])

        xt = sb("xt", [P, 2, KC, TILE], F16)
        ident_h = sb("ident_h", [P, P], F16)
        dve_passed, pool_passed = sem("dve_waits_passed"), sem("pool_waits_passed")
        banks = [ctx.enter_context(nc.psum_tensor(f"bank{i}", [P, 512], F32)) for i in range(8)]

        with ExitStack() as stage:
            w_in_f = stage.enter_context(nc.sbuf_tensor("w_in_f", [P, KC, D_IN], F32))
            w_out_f = stage.enter_context(nc.sbuf_tensor("w_out_f", [P, KC, D], F32))
            s_win, s_wout, s_small = sem("win_loaded"), sem("wout_loaded"), sem("small_loaded")
            s_fill, s_const = sem("constants_filled"), sem("constants_ready")
            s_big, s_all = sem("partition_maxima"), sem("global_maxima")
            s_step, s_alog = sem("scaling_steps"), sem("a_exponential")
            with nc.Block() as block:
                @block.sync
                def _(sp):
                    sp.dma_start(w_in_f[:], w_in_t.rearrange("(c p) n -> p c n", p=P)).then_inc(s_win, 16)
                    sp.dma_start(w_out_f[:], w_out_t.rearrange("(c p) n -> p c n", p=P)).then_inc(s_wout, 16)

                @block.scalar
                def _(act):
                    def row(v, n):
                        return v.rearrange("(a n) -> a n", a=1).broadcast_to((P, n))
                    act.dma_start(lut_sb[:], row(lut, CODES)).then_inc(s_small, 16)
                    act.dma_start(dt_bias_sb[:], row(dt_bias, HEADS)).then_inc(s_small, 16)
                    act.dma_start(a_sb[:], row(a_log, HEADS)).then_inc(s_small, 16)
                    act.dma_start(d_sb[:], row(d_param, HEADS)).then_inc(s_small, 16)
                    act.dma_start(conv_w_sb[:], conv_w.rearrange("(f p) k -> p f k", p=P)).then_inc(s_small, 16)
                    act.dma_start(conv_b_sb[:], conv_b.rearrange("(f p) -> p f", p=P),
                                  allow_slow_non_contiguous=True).then_inc(s_small, 16)
                    act.wait_ge(s_small, 96)
                    nc.scalar.activation(a_sb[:], a_sb[:], ACT.Exp).then_inc(s_alog, 1)

                @block.gpsimd
                def _(pool):
                    nc.gpsimd.memset(ident[:], 0.0).then_inc(s_fill, 1)
                    nc.gpsimd.memset(causal[:], 1.0).then_inc(s_fill, 1)
                    nc.gpsimd.memset(below[:], 1.0).then_inc(s_fill, 1)
                    nc.gpsimd.memset(ones[:], 1.0).then_inc(s_fill, 1)
                    nc.gpsimd.memset(neg_half[:], -0.5).then_inc(s_fill, 1)
                    pool.wait_ge(s_fill, 5)
                    nc.gpsimd.affine_select(out=ident[:], in_=ident[:], compare_op=ALU.not_equal, fill=1.0,
                                            base=0, pattern=[[-1, P]], channel_multiplier=1).then_inc(s_const, 1)
                    nc.gpsimd.affine_select(out=causal[:], in_=causal[:], compare_op=ALU.is_ge, fill=0.0,
                                            base=0, pattern=[[1, P]], channel_multiplier=-1).then_inc(s_const, 1)
                    nc.gpsimd.affine_select(out=below[:], in_=below[:], compare_op=ALU.is_gt, fill=0.0,
                                            base=0, pattern=[[-1, P]], channel_multiplier=1).then_inc(s_const, 1)
                    pool.wait_ge(s_big, 6)
                    nc.gpsimd.partition_all_reduce(big[:], lowest[:], P, RMAX).then_inc(s_all, 1)

                @block.vector
                def _(dve):
                    steps = [0]

                    def step(ins):
                        steps[0] += 1
                        ins.then_inc(s_step, 1)
                        dve.wait_ge(s_step, steps[0])

                    dve.wait_ge(s_small, 96)
                    dve.wait_ge(s_wout, 16)
                    dve.wait_ge(s_win, 16)
                    for n, (src, ax) in enumerate(((w_in_f[:], AX_XY), (w_out_f[:], AX_XY), (lut_sb[:], AX_X))):
                        nc.vector.tensor_reduce(big[:, n:n + 1], src, ax, ALU.max).then_inc(s_big, 1)
                    for n, (src, ax) in enumerate(((w_in_f[:], AX_XY), (w_out_f[:], AX_XY), (lut_sb[:], AX_X))):
                        ins = nc.vector.tensor_reduce(expo[:, n:n + 1], src, ax, ALU.min)
                        step(ins)
                    dve.wait_ge(s_big, 3)
                    for n in range(3):
                        nc.vector.scalar_tensor_tensor(lowest[:, n:n + 1], expo[:, n:n + 1], -1.0, big[:, n:n + 1],
                                                       ALU.mult, ALU.max).then_inc(s_big, 1)
                    dve.wait_ge(s_all, 1)
                    step(nc.vector.tensor_scalar(big[:], big[:], TINY, None, ALU.max))
                    step(nc.vector.tensor_scalar(expo[:].bitcast(I32), big[:].bitcast(I32), 0x7F800000, None,
                                                 ALU.bitwise_and))
                    step(nc.vector.reciprocal(wscale[:], expo[:]))
                    step(nc.vector.tensor_scalar(wscale[:], wscale[:], WS, None, ALU.mult))
                    step(nc.vector.tensor_scalar(c_in[:], expo[:, 0:1], 1.0 / (XS * WS), None, ALU.mult))
                    step(nc.vector.tensor_scalar(c_in_half[:], c_in[:], 0.5, None, ALU.mult))
                    step(nc.vector.tensor_scalar(c_out[:], c_in[:], expo[:, 1:2], 0.25 / (WS * WS), ALU.mult, ALU.mult))
                    step(nc.vector.tensor_scalar(c_gate_half[:], expo[:, 2:3], 0.5 / (XS * WS), None, ALU.mult))
                    step(nc.vector.tensor_scalar(c_down[:], expo[:, 2:3], expo[:, 2:3], 32.0 / WS, ALU.mult, ALU.mult))
                    step(nc.vector.tensor_scalar(c_down[:], c_down[:], expo[:, 2:3], None, ALU.mult))
                    dve.wait_ge(s_alog, 1)
                    step(nc.vector.tensor_scalar(a_sb[:], a_sb[:], -1.0, None, ALU.mult))
                    step(nc.vector.tensor_scalar(win_hi[:], w_in_f[:], wscale[:, 0:1], None, ALU.mult))
                    step(nc.vector.scalar_tensor_tensor(win_lo[:], w_in_f[:], wscale[:, 0:1], win_hi[:],
                                                        ALU.mult, ALU.subtract))
                    step(nc.vector.tensor_scalar(wout_hi[:], w_out_f[:], wscale[:, 1:2], None, ALU.mult))
                    step(nc.vector.scalar_tensor_tensor(wout_lo[:], w_out_f[:], wscale[:, 1:2], wout_hi[:],
                                                        ALU.mult, ALU.subtract))
                    step(nc.vector.tensor_scalar(lut_s[:], lut_sb[:], wscale[:, 2:3], None, ALU.mult))
                    step(nc.vector.tensor_copy(lut_hi[:], lut_s[:]))
                    step(nc.vector.tensor_copy(lut_hi32[:], lut_hi[:]))
                    step(nc.vector.tensor_sub(lut_lo32[:], lut_s[:], lut_hi32[:]))
                    dve.wait_ge(s_const, 3)
                    step(nc.vector.tensor_copy(ident_h[:], ident[:]))

        with ExitStack() as stage:
            def st(name, shape, dt=F32):
                return stage.enter_context(nc.sbuf_tensor(name, shape, dt))
            diag = st("diag", [P, 2, CODES, P], F16)
            codes_sb = st("codes_sb", [P, UNIT], I32)
            codes_h = st("codes_h", [P, UNIT], F16)
            mask = st("mask", [P, CODES, UNIT], F16)
            ut = st("ut", [P, SUB, D])
            stats = st("stats", [P, SUB, 6])
            mv = st("mv", [P, SUB, 2])
            vare = st("vare", [P, SUB])
            rstd = st("rstd", [P, SUB])
            xsplit = st("xsplit", [P, 2, 2, D], F16)
            cin = st("cin", [P, 2, HALO + TILE])
            halo = st("halo", [P, FB, HALO])
            cacc = st("cacc", [P, 2, TILE])
            ctanh = st("ctanh", [P, TILE])
            dtr = st("dtr", [P, SUB, HEADS])
            dtx = st("dtx", [P, SUB, HEADS])
            dte = st("dte", [P, SUB, HEADS])
            dtz = st("dtz", [P, SUB, HEADS])
            dtz2 = st("dtz2", [P, SUB, HEADS])
            dtp = st("dtp", [P, SUB, HEADS])
            dt = st("dt", [P, SUB, HEADS])
            dt4 = st("dt4", [P, 2, SUB, HEADS])
            da = st("da", [P, 2, SUB, HEADS])
            xs = st("xs", [P, 2, KC, TILE])
            bs = st("bs", [P, TILE])
            cs = st("cs", [P, TILE])
            ztanh = st("ztanh", [P, D])
            zs = st("zs", [P, SUB, D])
            seg = st("seg", [P, HEADS, P])
            decay = st("decay", [P, HEADS, P])
            gsb = st("gsb", [P, P])
            bt = st("bt", [P, NST])
            ex = st("ex", [P, 3, HEADS])
            xtok = st("xtok", [P, D])
            xdt = st("xdt", [P, D])
            xd = st("xd", [P, D])
            state = st("state", [P, D])
            y = st("y", [P, D])
            ymax = st("ymax", [P, 1])
            yexp = st("yexp", [P, SUB])
            yq = st("yq", [P, 1])
            ysplit = st("ysplit", [P, 2, D], F16)
            yt = st("yt", [P, 2, KC, P], F16)
            ostat = st("ostat", [P, 6])
            omv = st("omv", [P, 2])
            octok = st("octok", [P, 1])
            ovar = st("ovar", [P, 1])
            orstd = st("orstd", [P, 1])
            oscale = st("oscale", [P, 1])
            obias = st("obias", [P, 1])
            ures = st("ures", [P, D])
            x1 = st("x1", [P, D])

            filled = Signal(sem("shared_bank_filled"), len(USES))
            freed = Signal(sem("shared_bank_freed"), len(USES))
            s_diag = sem("diagonals_ready")
            loaded = Signal(sem("codes_loaded"), TILE_UNITS, step=16)
            as_half = Signal(sem("codes_as_half"), TILE_UNITS)
            masks_ready = Signal(sem("masks_ready"), TILE_UNITS * GROUPS)
            masks_used = Signal(sem("masks_used"), TILE_UNITS * (GROUPS - 1), credit=True)
            u_loaded = Signal(sem("u_loaded"), 1, step=16)
            ln_steps = Signal(sem("ln_steps"), 3 * SUB)
            rstd_ready = Signal(sem("rstd_ready"), 1)
            split_steps = Signal(sem("split_steps"), 3 * SUB)
            conv_steps = Signal(sem("conv_steps"), FB * CSTEPS)
            ctanh_ready = Signal(sem("conv_tanh_ready"), FB)
            xs_ready = Signal(sem("conv_silu_ready"), FB + 1)
            dt_steps = Signal(sem("dt_steps"), 18)
            dt_exp = Signal(sem("dt_exponential"), 1)
            z_tanh = Signal(sem("z_tanh_ready"), SUB)
            zs_ready = Signal(sem("z_gate_ready"), SUB)
            seg_ready = Signal(sem("segment_terms_ready"), SUB)
            xtok_done = Signal(sem("x_tokens_transposed"), SUB)
            small_done = Signal(sem("gram_and_sums_done"), SUB)
            seg_done = Signal(sem("segment_sums_done"), SUB)
            xtok_ready = Signal(sem("x_tokens_ready"), SUB)
            sums_ready = Signal(sem("sums_exponentiated"), SUB * 2)
            decay_ready = Signal(sem("decay_ready"), SUB * 2)
            xdt_ready = Signal(sem("x_dt_ready"), SUB)
            gram_ready = Signal(sem("gram_masked"), SUB, credit=True)
            mt_ready = Signal(sem("decayed_gram_ready"), SUB)
            xd_ready = Signal(sem("x_d_ready"), SUB)
            xw_ready = Signal(sem("x_weighted_ready"), SUB)
            stated = Signal(sem("state_decayed"), SUB)
            state_ready = Signal(sem("state_ready"), SUB, credit=True)
            state_cleared = Signal(sem("state_cleared"), 1)
            y_done = Signal(sem("y_inner_done"), SUB)
            yi_done = Signal(sem("y_carried_done"), SUB)
            s_done = Signal(sem("state_update_done"), SUB)
            y_steps = Signal(sem("y_steps"), SUB * YSTEPS, credit=True)
            yt_done = Signal(sem("y_transposed"), SUB)
            yt_ready = Signal(sem("yt_ready"), SUB, credit=True)
            o_done = Signal(sem("out_projected"), SUB)
            o_steps = Signal(sem("o_steps"), SUB * OSTEPS)
            orstd_ready = Signal(sem("out_rstd_ready"), SUB)
            o_read = Signal(sem("out_projection_read"), SUB, credit=True)
            normalised = Signal(sem("out_normalised"), SUB)
            ures_loaded = Signal(sem("u_chunk_loaded"), SUB, step=16)
            x1_ready = Signal(sem("x1_ready"), SUB, credit=True)
            x1_stored = Signal(sem("x1_stored"), SUB, step=16, credit=True)

            def use(t, name, more=True):
                if isinstance(t, int) and t < 0:
                    return FRONT_USES.index(name)
                return t * len(USES) + (len(FRONT_USES) + (USES if more else LAST_USES).index(name))

            def bank_of(name, more=True):
                return banks[(USES if more else LAST_USES).index(name) % 2]

            def front_bank(t, name, more=True):
                return banks[FRONT_USES.index(name) % 2] if isinstance(t, int) and t < 0 else bank_of(name, more)

            def following(row, half):
                return (row, 1) if half == 0 else (row + 1, 0)

            def iterations(eng, body):
                with eng.Fori(0, BATCHES - 1) as row:
                    for half in range(HALVES):
                        body(row * HALVES + half, half, row, True)
                for half in range(HALVES):
                    body((BATCHES - 1) * HALVES + half, half, BATCHES - 1, half < HALVES - 1)

            with nc.Block() as block:
                @block.sync
                def _(sp):
                    x1_stored.start(sp)
                    u_loaded.inc(sp.dma_start(ut[:], u_tiles[0]))
                    sp.wait_ge(split_steps.sem, split_steps.now(0, 3 * SUB))
                    u_loaded.inc(sp.dma_start(ut[:], u_tiles[1]))

                    def residual(t, c):
                        sp.wait_ge(x1_ready.sem, x1_ready.prev(t, SUB + c))
                        ures_loaded.inc(sp.dma_start(ures[:], u_chunks[t * SUB + c]))

                    def body(t, half, row, more):
                        residual(t, 0)
                        for c in range(SUB):
                            sp.wait_ge(x1_ready.sem, x1_ready.now(t, c + 1))
                            x1_stored.inc(sp.dma_start(x1_chunks[t * SUB + c], x1[:]))
                            if c + 1 < SUB:
                                residual(t, c + 1)
                            if c == 1 and more:
                                sp.wait_ge(split_steps.sem, split_steps.now(t + 1, 3 * SUB))
                                if isinstance(t, int):
                                    sp.wait_ge(x1_stored.sem, x1_stored.now(0, SUB))
                                    u_loaded.inc(sp.dma_start(ut[:], x1_tiles[0]))
                                else:
                                    u_loaded.inc(sp.dma_start(ut[:], u_tiles[t + 2]))

                    iterations(sp, body)
                    sp.wait_ge(x1_stored.sem, x1_stored.now(TILES - 1, SUB))

                @block.gpsimd
                def _(pool):
                    x1_ready.start(pool)

                    def front_rstd(i):
                        pool.wait_ge(ln_steps.sem, ln_steps.now(i, 3 * SUB))
                        rstd_ready.inc(nc.gpsimd.tensor_tensor(rstd[:], vare[:], neg_half[:], ALU.pow))

                    def to_half(row, half, k):
                        t = row * HALVES + half
                        pool.wait_ge(loaded.sem, loaded.now(t, k + 1))
                        pool.wait_ge(masks_ready.sem, masks_ready.now(t, k * GROUPS))
                        pool.sem_inc(pool_passed, 1)
                        as_half.inc(nc.gpsimd.tensor_copy(codes_h[:], codes_sb[:]))

                    def segments(t, p, c):
                        pool.wait_ge(seg_done.sem, seg_done.now(t, c))
                        if c == 0:
                            pool.wait_ge(dt_steps.sem, dt_steps.now(t, 17))
                        seg_ready.inc(nc.gpsimd.tensor_tensor(
                            seg[:], causal[:].unsqueeze(1).broadcast_to((P, HEADS, P)),
                            da[:, p, c, :].unsqueeze(2).broadcast_to((P, HEADS, P)), ALU.mult))

                    def weights(t, half, c):
                        pool.wait_ge(xtok_ready.sem, xtok_ready.now(t, c + 1))
                        pool.wait_ge(y_steps.sem, y_steps.prev(t, YSTEPS * (SUB + c - 1) + 4))
                        pool.wait_ge(stated.sem, stated.now(t, c))
                        xd_ready.inc(nc.gpsimd.tensor_tensor(
                            xd[:].rearrange("p (h d) -> p h d", h=HEADS),
                            xtok[:].rearrange("p (h d) -> p h d", h=HEADS),
                            d_sb[:].unsqueeze(2).broadcast_to((P, HEADS, HD)), ALU.mult))
                        pool.wait_ge(sums_ready.sem, sums_ready.now(t, 2 * c + 1))
                        pool.wait_ge(xdt_ready.sem, xdt_ready.now(t, c + 1))
                        pool.wait_ge(xd_ready.sem, xd_ready.now(t, c + 1))
                        xw_ready.inc(nc.gpsimd.tensor_tensor(
                            xtok[:].rearrange("p (h d) -> p h d", h=HEADS),
                            xdt[:].rearrange("p (h d) -> p h d", h=HEADS),
                            ex[:, 1, :].unsqueeze(2).broadcast_to((P, HEADS, HD)), ALU.mult))

                    def decay_state(t, half, row, c, apart):
                        h0 = half * NST
                        if half == 0 and c == 0:
                            pool.wait_ge(state_cleared.sem, state_cleared.now(row, 1))
                        else:
                            pool.wait_ge(state_ready.sem, state_ready.prev(t, SUB + c))
                        pool.wait_ge(yi_done.sem, yi_done.now(t, c + 1))
                        pool.wait_ge(*apart)
                        stated.inc(nc.gpsimd.tensor_tensor(
                            state[h0:h0 + NST, :].rearrange("p (h d) -> p h d", h=HEADS),
                            state[h0:h0 + NST, :].rearrange("p (h d) -> p h d", h=HEADS),
                            ex[h0:h0 + NST, 2, :].unsqueeze(2).broadcast_to((NST, HEADS, HD)), ALU.mult))
                        pool.wait_ge(stated.sem, stated.now(t, c + 1))

                    def out_rstd(t, c):
                        pool.wait_ge(o_steps.sem, o_steps.now(t, OSTEPS * c + 5))
                        orstd_ready.inc(nc.gpsimd.tensor_tensor(orstd[:], ovar[:], neg_half[:, 0:1], ALU.pow))

                    def add_residual(t, c):
                        pool.wait_ge(normalised.sem, normalised.now(t, c + 1))
                        pool.wait_ge(ures_loaded.sem, ures_loaded.now(t, c + 1))
                        x1_ready.inc(nc.gpsimd.tensor_tensor(x1[:], x1[:], ures[:], ALU.add))

                    def body(t, half, row, more):
                        weights(t, half, 0)
                        front_rstd(t + 1)
                        segments(t, half, 1)
                        decay_state(t, half, row, 0, (seg_ready.sem, seg_ready.now(t, 2)))
                        to_half(row, half, 1)
                        weights(t, half, 1)
                        segments(t, half, 2)
                        decay_state(t, half, row, 1, (seg_ready.sem, seg_ready.now(t, 3)))
                        weights(t, half, 2)
                        to_half(row, half, 2)
                        segments(t, half, 3)
                        out_rstd(t, 0)
                        add_residual(t, 0)
                        decay_state(t, half, row, 2, (x1_ready.sem, x1_ready.now(t, 1)))
                        weights(t, half, 3)
                        to_half(row, half, 3)
                        out_rstd(t, 1)
                        add_residual(t, 1)
                        decay_state(t, half, row, 3, (x1_ready.sem, x1_ready.now(t, 2)))
                        to_half(row, half, 4)
                        out_rstd(t, 2)
                        add_residual(t, 2)
                        if more:
                            segments(t + 1, 1 - half, 0)
                        out_rstd(t, 3)
                        if more:
                            to_half(*following(row, half), 0)
                        add_residual(t, 3)

                    front_rstd(0)
                    to_half(0, 0, 0)
                    segments(0, 0, 0)
                    iterations(pool, body)

                @block.scalar
                def _(act):
                    yt_ready.start(act)
                    o_read.start(act)

                    def load_codes(row, half, k):
                        t = row * HALVES + half
                        act.wait_ge(as_half.sem, as_half.now(t, k))
                        loaded.inc(act.dma_start(codes_sb[:],
                                                 codes[:, bass.ds((t * TILE_UNITS + k) * UNIT, UNIT)]))

                    def input_transposed(t, s, more=True):
                        act.wait_ge(filled.sem, use(t, f"T{s}", more) + 1)
                        freed.inc(nc.scalar.activation(
                            xt[:, :, :, s * P:(s + 1) * P],
                            front_bank(t, f"T{s}", more)[:].bitcast(F16).rearrange("p (n k t) -> p n k t", n=2, k=KC), ACT.Copy))

                    def conv_input(t, f):
                        act.wait_ge(filled.sem, use(t, f"X{f}") + 1)
                        if f >= 2:
                            act.wait_ge(conv_steps.sem, conv_steps.now(t + 1, CSTEPS * (f - 1)))
                        elif not (isinstance(t, int) and t < 0):
                            act.wait_ge(conv_steps.sem, conv_steps.now(t + 1, 0))
                        freed.inc(nc.scalar.activation(cin[:, f % 2, HALO:], front_bank(t, f"X{f}")[:], ACT.Identity,
                                                       scale=c_in[:]))

                    def conv_tanh(i, f):
                        act.wait_ge(conv_steps.sem, conv_steps.now(i, CSTEPS * f + TAPS + 1))
                        act.wait_ge(xs_ready.sem, xs_ready.now(i, f))
                        ctanh_ready.inc(nc.scalar.activation(ctanh[:], cacc[:, f % 2, :], ACT.Tanh, scale=0.5))

                    def dt_input(t):
                        act.wait_ge(filled.sem, use(t, "dt") + 1)
                        freed.inc(nc.scalar.activation(
                            dtr[:], front_bank(t, "dt")[:, 0:SUB * HEADS].rearrange("p (s h) -> p s h", s=SUB),
                            ACT.Identity, scale=c_in[:]))

                    def dt_exponential(i):
                        act.wait_ge(dt_steps.sem, dt_steps.now(i, 3))
                        dt_exp.inc(nc.scalar.activation(dte[:], dtz[:], ACT.Exp, scale=-1.0))

                    def z_input(t, c, more):
                        act.wait_ge(filled.sem, use(t, f"z{c}", more) + 1)
                        freed.inc(nc.scalar.activation(zs[:, c, :], bank_of(f"z{c}", more)[:], ACT.Copy))

                    def z_tanh_half(t, c, more):
                        act.wait_ge(freed.sem, use(t, f"z{c}", more) + 1)
                        act.wait_ge(zs_ready.sem, zs_ready.now(t, c))
                        z_tanh.inc(nc.scalar.activation(ztanh[:], zs[:, c, :], ACT.Tanh, scale=c_in_half[:]))

                    def decoded(t, k, more):
                        for n, dst in enumerate((ffn_hi, ffn_lo)):
                            name = f"D{k}" + "'" * n
                            act.wait_ge(filled.sem, use(t, name, more) + 1)
                            freed.inc(nc.scalar.activation(dst[:, bass.ds((t * TILE_UNITS + k) * UNIT, UNIT)],
                                                           bank_of(name, more)[:, 0:UNIT], ACT.Copy))

                    def small(t, c):
                        act.wait_ge(xtok_done.sem, xtok_done.now(t, c + 1))
                        xtok_ready.inc(nc.scalar.activation(xtok[:], banks[2][:], ACT.Copy))
                        act.wait_ge(small_done.sem, small_done.now(t, c + 1))
                        sums_ready.inc(nc.scalar.activation(
                            ex[:], banks[3][:, 192:216].rearrange("p (k h) -> p k h", k=3), ACT.Exp))
                        sums_ready.inc(nc.scalar.activation(bt[:], banks[3][:, 128:192], ACT.Copy))

                    def decays(t, c):
                        act.wait_ge(seg_done.sem, seg_done.now(t, c + 1))
                        for n in range(2):
                            decay_ready.inc(nc.scalar.activation(
                                decay[:, 4 * n:4 * n + 4, :], banks[4 + n][:].rearrange("p (h t) -> p h t", h=4), ACT.Exp))

                    def y_transposed(t, c):
                        act.wait_ge(yt_done.sem, yt_done.now(t, c + 1))
                        yt_ready.inc(nc.scalar.activation(
                            yt[:], banks[4][:].bitcast(F16).rearrange("p (n k t) -> p n k t", n=2, k=KC), ACT.Copy))

                    def out_projected(t, c):
                        act.wait_ge(o_done.sem, o_done.now(t, c + 1))
                        act.wait_ge(x1_stored.sem, x1_stored.prev(t, SUB + c))
                        o_read.inc(nc.scalar.activation(x1[:], banks[5][:], ACT.Copy))

                    def normalise(t, c):
                        act.wait_ge(o_steps.sem, o_steps.now(t, OSTEPS * (c + 1)))
                        normalised.inc(nc.scalar.activation(x1[:], x1[:], ACT.Identity, bias=obias[:], scale=oscale[:]))

                    def body(t, half, row, more):
                        i = t + 1
                        z_input(t, 0, more)
                        z_tanh_half(t, 0, more)
                        z_input(t, 1, more)
                        small(t, 0)
                        decays(t, 0)
                        z_input(t, 2, more)
                        z_tanh_half(t, 1, more)
                        z_input(t, 3, more)
                        small(t, 1)
                        decays(t, 1)
                        z_tanh_half(t, 2, more)
                        decoded(t, 0, more)
                        load_codes(row, half, 2)
                        y_transposed(t, 0)
                        input_transposed(t, 0, more)
                        input_transposed(t, 1, more)
                        z_tanh_half(t, 3, more)
                        out_projected(t, 0)
                        small(t, 2)
                        decays(t, 2)
                        input_transposed(t, 2, more)
                        input_transposed(t, 3, more)
                        decoded(t, 1, more)
                        load_codes(row, half, 3)
                        normalise(t, 0)
                        y_transposed(t, 1)
                        if more:
                            conv_input(t, 0)
                        out_projected(t, 1)
                        small(t, 3)
                        decays(t, 3)
                        if more:
                            conv_tanh(i, 0)
                            conv_input(t, 1)
                            conv_input(t, 2)
                        y_transposed(t, 2)
                        if more:
                            conv_tanh(i, 1)
                        decoded(t, 2, more)
                        load_codes(row, half, 4)
                        if more:
                            conv_input(t, 3)
                            conv_tanh(i, 2)
                        normalise(t, 1)
                        out_projected(t, 2)
                        if more:
                            conv_input(t, 4)
                            dt_input(t)
                            dt_exponential(i)
                        decoded(t, 3, more)
                        y_transposed(t, 3)
                        normalise(t, 2)
                        if more:
                            load_codes(*following(row, half), 0)
                            conv_tanh(i, 3)
                        decoded(t, 4, more)
                        out_projected(t, 3)
                        if more:
                            conv_tanh(i, 4)
                        normalise(t, 3)
                        if more:
                            load_codes(*following(row, half), 1)

                    load_codes(0, 0, 0)
                    for s in range(SUB):
                        input_transposed(-1, s)
                    for f in range(FB):
                        conv_input(-1, f)
                        if f >= 1:
                            conv_tanh(0, f - 1)
                    dt_input(-1)
                    conv_tanh(0, FB - 1)
                    dt_exponential(0)
                    load_codes(0, 0, 1)
                    iterations(act, body)

                @block.tensor
                def _(pe):
                    masks_used.start(pe)

                    def take(n):
                        if not (isinstance(n, int) and n < 2):
                            pe.wait_ge(freed.sem, n - 1)

                    def split_products(out_ap, pairs):
                        for k, (lhs, rhs) in enumerate(pairs):
                            last = nc.tensor.matmul(out_ap, lhs, rhs, start=(k == 0), stop=(k == len(pairs) - 1))
                        return last

                    def input_transpose(t, s, more=True):
                        take(use(t, f"T{s}", more))
                        pe.wait_ge(split_steps.sem, split_steps.now(t + 1, 3 * (s + 1)))
                        b = front_bank(t, f"T{s}", more)[:].bitcast(F16).rearrange("p (n k t) -> p n k t", n=2, k=KC)
                        for n in range(2):
                            for k in range(KC):
                                last = nc.tensor.transpose(b[:, n, k, :], xsplit[:, s % 2, n, k * P:(k + 1) * P],
                                                           ident_h[:])
                        filled.inc(last)

                    def project_conv(t, f):
                        take(use(t, f"X{f}"))
                        if f == 0:
                            pe.wait_ge(freed.sem, use(t, f"T{SUB - 1}") + 1)
                        cols = slice(X0 + f * P, X0 + (f + 1) * P)
                        filled.inc(split_products(front_bank(t, f"X{f}")[:], [
                            (w[:, k, cols], xt[:, n, k, :]) for k in range(KC)
                            for w, n in ((win_hi, 0), (win_hi, 1), (win_lo, 0))]))

                    def project_dt(t):
                        take(use(t, "dt"))
                        b = front_bank(t, "dt")
                        for c in range(SUB):
                            tok = slice(c * P, (c + 1) * P)
                            last = split_products(b[:, c * HEADS:(c + 1) * HEADS], [
                                (xt[:, n, k, tok], w[:, k, DT0:D_IN]) for k in range(KC)
                                for w, n in ((win_hi, 0), (win_lo, 0), (win_hi, 1))])
                        filled.inc(last)

                    def project_z(t, c, more):
                        take(use(t, f"z{c}", more))
                        tok = slice(c * P, (c + 1) * P)
                        filled.inc(split_products(bank_of(f"z{c}", more)[:], [
                            (xt[:, n, k, tok], w[:, k, 0:D]) for k in range(KC)
                            for w, n in ((win_hi, 0), (win_lo, 0), (win_hi, 1))]))

                    def decode(t, k, more):
                        for n in range(2):
                            take(use(t, f"D{k}" + "'" * n, more))
                        for g in range(GROUPS):
                            pe.wait_ge(masks_ready.sem, masks_ready.now(t, k * GROUPS + g + 1))
                            for j in range(g * GROUP, (g + 1) * GROUP):
                                for n in range(2):
                                    last = nc.tensor.matmul(bank_of(f"D{k}" + "'" * n, more)[:, 0:UNIT], diag[:, n, j, :],
                                                            mask[:, j, :], start=(j == 0), stop=(j == CODES - 1))
                                    if j == CODES - 1:
                                        filled.inc(last)
                            if g < GROUPS - 1:
                                masks_used.inc(last)

                    def prepare(t, half, c):
                        tok = slice(c * P, (c + 1) * P)
                        h = slice(half * NST, (half + 1) * NST)
                        if c == 0:
                            pe.wait_ge(xs_ready.sem, xs_ready.now(t, FB + 1))
                        pe.wait_ge(state_ready.sem, state_ready.prev(t, SUB + c))
                        for k in range(KC):
                            last = nc.tensor.transpose(banks[2][:, k * P:(k + 1) * P], xs[:, half, k, tok], ident[:])
                        xtok_done.inc(last)
                        pe.wait_ge(gram_ready.sem, gram_ready.prev(t, SUB + c))
                        nc.tensor.matmul(banks[3][:, 0:P], bs[h, tok], cs[h, tok], start=True, stop=True)
                        nc.tensor.transpose(banks[3][:, 128:192], bs[h, tok], ident[h, h])
                        pe.wait_ge(dt_steps.sem, dt_steps.now(t, 17))
                        for n, sums in enumerate((causal, below, ones)):
                            last = nc.tensor.matmul(banks[3][:, 192 + n * HEADS:192 + (n + 1) * HEADS], sums[:],
                                                    da[:, half, c, :], start=True, stop=True)
                        small_done.inc(last)

                    def segment_sums(t, c):
                        pe.wait_ge(seg_ready.sem, seg_ready.now(t, c + 1))
                        pe.wait_ge(yt_ready.sem, yt_ready.prev(t, SUB + max(c - 1, 0)))
                        pe.wait_ge(o_read.sem, o_read.prev(t, SUB + max(c - 1, 0)))
                        for n in range(2):
                            last = nc.tensor.matmul(banks[4 + n][:], below[:],
                                                    seg[:, 4 * n:4 * n + 4, :].rearrange("p h t -> p (h t)"),
                                                    start=True, stop=True)
                        seg_done.inc(last)

                    def scan(t, half, row, c):
                        tok = slice(c * P, (c + 1) * P)
                        h = slice(half * NST, (half + 1) * NST)
                        if half == 0 and c == 0:
                            pe.wait_ge(state_cleared.sem, state_cleared.now(row, 1))
                        pe.wait_ge(state_ready.sem, state_ready.prev(t, SUB + c))
                        yi_done.inc(nc.tensor.matmul(banks[7][:], cs[h, tok], state[h, :], start=True, stop=True))
                        pe.wait_ge(xdt_ready.sem, xdt_ready.now(t, c + 1))
                        pe.wait_ge(mt_ready.sem, mt_ready.now(t, c + 1))
                        for n in range(HEADS):
                            last = nc.tensor.matmul(banks[6][:, n * HD:(n + 1) * HD], decay[:, n, :],
                                                    xdt[:, n * HD:(n + 1) * HD], start=True, stop=True)
                        y_done.inc(last)
                        pe.wait_ge(sums_ready.sem, sums_ready.now(t, 2 * c + 2))
                        pe.wait_ge(xw_ready.sem, xw_ready.now(t, c + 1))
                        s_done.inc(nc.tensor.matmul(banks[2][h, :], bt[:], xtok[:], start=True, stop=True))

                    def transpose_y(t, c):
                        pe.wait_ge(y_steps.sem, y_steps.now(t, YSTEPS * (c + 1)))
                        pe.wait_ge(decay_ready.sem, decay_ready.now(t, 2 * min(c + 2, SUB)))
                        b = banks[4][:].bitcast(F16).rearrange("p (n k t) -> p n k t", n=2, k=KC)
                        for n in range(2):
                            for k in range(KC):
                                last = nc.tensor.transpose(b[:, n, k, :], ysplit[:, n, k * P:(k + 1) * P], ident_h[:])
                        yt_done.inc(last)

                    def project_out(t, c):
                        pe.wait_ge(yt_ready.sem, yt_ready.now(t, c + 1))
                        pe.wait_ge(o_read.sem, o_read.prev(t, SUB + c))
                        o_done.inc(split_products(banks[5][:], [
                            (yt[:, n, k, :], w[:, k, :]) for k in range(KC)
                            for n, w in ((0, wout_hi), (0, wout_lo), (1, wout_hi))]))

                    def body(t, half, row, more):
                        project_z(t, 0, more)
                        project_z(t, 1, more)
                        prepare(t, half, 0)
                        segment_sums(t, 0)
                        project_z(t, 2, more)
                        scan(t, half, row, 0)
                        project_z(t, 3, more)
                        prepare(t, half, 1)
                        segment_sums(t, 1)
                        decode(t, 0, more)
                        transpose_y(t, 0)
                        input_transpose(t, 0, more)
                        input_transpose(t, 1, more)
                        scan(t, half, row, 1)
                        project_out(t, 0)
                        prepare(t, half, 2)
                        segment_sums(t, 2)
                        input_transpose(t, 2, more)
                        input_transpose(t, 3, more)
                        decode(t, 1, more)
                        transpose_y(t, 1)
                        if more:
                            project_conv(t, 0)
                        scan(t, half, row, 2)
                        project_out(t, 1)
                        prepare(t, half, 3)
                        segment_sums(t, 3)
                        if more:
                            project_conv(t, 1)
                            project_conv(t, 2)
                        transpose_y(t, 2)
                        decode(t, 2, more)
                        if more:
                            project_conv(t, 3)
                        scan(t, half, row, 3)
                        project_out(t, 2)
                        if more:
                            project_conv(t, 4)
                            project_dt(t)
                        decode(t, 3, more)
                        transpose_y(t, 3)
                        decode(t, 4, more)
                        project_out(t, 3)

                    for s in range(SUB):
                        input_transpose(-1, s)
                    for f in range(FB):
                        project_conv(-1, f)
                    project_dt(-1)
                    pe.wait_ge(s_diag, 2 * CODES)
                    iterations(pe, body)

                @block.vector
                def _(dve):
                    for g in (gram_ready, state_ready, y_steps):
                        g.start(dve)

                    def chain(sig, t, k, ins):
                        sig.inc(ins)
                        dve.wait_ge(sig.sem, sig.now(t, k))

                    def masks(row, half, k, more=True):
                        t = row * HALVES + half
                        for g in range(GROUPS):
                            if g == 0:
                                dve.wait_ge(as_half.sem, as_half.now(t, k + 1))
                            if g < GROUPS - 1:
                                dve.wait_ge(masks_used.sem, masks_used.prev(t, (TILE_UNITS + k - 1) * (GROUPS - 1) + g + 1))
                            elif k > 0:
                                dve.wait_ge(filled.sem, use(t, f"D{k - 1}'", more) + 1)
                            elif not (isinstance(t, int) and t == 0):
                                dve.wait_ge(filled.sem, use(t - 1, f"D{TILE_UNITS - 1}'") + 1)
                            for j in range(g * GROUP, (g + 1) * GROUP):
                                last = nc.vector.tensor_scalar(mask[:, j, :], codes_h[:], float(j),
                                                               None, ALU.is_equal)
                            masks_ready.inc(last)

                    def ln_stats(i):
                        dve.wait_ge(u_loaded.sem, u_loaded.now(i, 1))
                        for s in range(SUB):
                            ln_steps.inc(nc.vector.bn_stats(stats[:, s, :], ut[:, s, :]))
                        for s in range(SUB):
                            wait_apart(dve, ln_steps.sem, ln_steps.now(i, s + 1), dve_passed)
                            ln_steps.inc(nc.vector.bn_aggr(mv[:, s, :], stats[:, s, :]))
                        for s in range(SUB):
                            dve.wait_ge(ln_steps.sem, ln_steps.now(i, SUB + s + 1))
                            ln_steps.inc(nc.vector.tensor_scalar(vare[:, s:s + 1], mv[:, s, 1:2], 1.0 / XS ** 2,
                                                                 EPS / XS ** 2, ALU.mult, ALU.add))

                    def ln_split(i, s, more=True):
                        if s == 0:
                            dve.wait_ge(rstd_ready.sem, rstd_ready.now(i, 1))
                        chain(split_steps, i, 3 * s + 1, nc.vector.tensor_scalar(
                            ut[:, s, :], ut[:, s, :], mv[:, s, 0:1], rstd[:, s:s + 1], ALU.subtract, ALU.mult))
                        if s >= 2:
                            dve.wait_ge(filled.sem, use_of_front(i, f"T{s - 2}", more) + 1)
                        chain(split_steps, i, 3 * s + 2, nc.vector.tensor_copy(xsplit[:, s % 2, 0, :], ut[:, s, :]))
                        split_steps.inc(nc.vector.tensor_sub(xsplit[:, s % 2, 1, :], ut[:, s, :], xsplit[:, s % 2, 0, :]))

                    def use_of_front(i, name, more=True):
                        return use(-1, name) if isinstance(i, int) and i == 0 else use(i - 1, name, more)

                    def conv(i, p, f):
                        n0 = CSTEPS * f
                        slot = f % 2
                        if p == 0:
                            chain(conv_steps, i, n0 + 1, nc.vector.memset(cin[:, slot, 0:HALO], 0.0))
                        else:
                            chain(conv_steps, i, n0 + 1, nc.vector.tensor_copy(cin[:, slot, 0:HALO], halo[:, f, :]))
                        dve.wait_ge(freed.sem, use_of_front(i, f"X{f}") + 1)
                        if not (isinstance(i, int) and i == 0 and f < 2):
                            dve.wait_ge(xs_ready.sem, xs_ready.now(i, max(f - 1, 0)))
                        chain(conv_steps, i, n0 + 2, nc.vector.tensor_scalar(
                            cacc[:, slot, :], cin[:, slot, 0:TILE], conv_w_sb[:, f, 0:1], conv_b_sb[:, f:f + 1],
                            ALU.mult, ALU.add))
                        for k in range(1, TAPS):
                            chain(conv_steps, i, n0 + 2 + k, nc.vector.scalar_tensor_tensor(
                                cacc[:, slot, :], cin[:, slot, k:k + TILE], conv_w_sb[:, f, k:k + 1],
                                cacc[:, slot, :], ALU.mult, ALU.add))
                        chain(conv_steps, i, n0 + 6, nc.vector.tensor_copy(halo[:, f, :], cin[:, slot, TILE:TILE + HALO]))

                    def conv_silu(i, p, f):
                        dve.wait_ge(ctanh_ready.sem, ctanh_ready.now(i, f + 1))
                        if f < KC:
                            xs_ready.inc(nc.vector.scalar_tensor_tensor(
                                xs[:, p, f, :], ctanh[:], 1.0, cacc[:, f % 2, :], ALU.add, ALU.mult))
                        else:
                            h = slice(p * NST, (p + 1) * NST)
                            for dst, lo in ((bs, 0), (cs, NST)):
                                xs_ready.inc(nc.vector.scalar_tensor_tensor(
                                    dst[h, :], ctanh[lo:lo + NST, :], 1.0, cacc[lo:lo + NST, f % 2, :],
                                    ALU.add, ALU.mult))

                    def dt_input(i):
                        dve.wait_ge(freed.sem, use_of_front(i, "dt") + 1)
                        chain(dt_steps, i, 1, nc.vector.tensor_tensor(
                            dtx[:], dtr[:], dt_bias_sb[:].unsqueeze(1).broadcast_to((P, SUB, HEADS)), ALU.add))
                        chain(dt_steps, i, 2, nc.vector.tensor_scalar(dtp[:], dtx[:], -1.0, None, ALU.mult))
                        chain(dt_steps, i, 3, nc.vector.tensor_tensor(dtz[:], dtx[:], dtp[:], ALU.max))

                    def time_steps(i, p):
                        dve.wait_ge(dt_exp.sem, dt_exp.now(i, 1))
                        chain(dt_steps, i, 4, nc.vector.tensor_scalar(dtp[:], dte[:], 2.0, None, ALU.add))
                        chain(dt_steps, i, 5, nc.vector.reciprocal(dtp[:], dtp[:]))
                        chain(dt_steps, i, 6, nc.vector.tensor_tensor(dtz[:], dte[:], dtp[:], ALU.mult))
                        chain(dt_steps, i, 7, nc.vector.tensor_tensor(dtz2[:], dtz[:], dtz[:], ALU.mult))
                        chain(dt_steps, i, 8, nc.vector.tensor_scalar(dtp[:], dtz2[:], 2.0 / 15, None, ALU.mult))
                        for n, k in enumerate((13, 11, 9, 7, 5, 3)):
                            chain(dt_steps, i, 9 + n, nc.vector.scalar_tensor_tensor(
                                dtp[:], dtp[:], 2.0 / k, dtz2[:], ALU.add, ALU.mult))
                        chain(dt_steps, i, 15, nc.vector.scalar_tensor_tensor(
                            dtp[:], dtp[:], 2.0, dtz[:], ALU.add, ALU.mult))
                        chain(dt_steps, i, 16, nc.vector.scalar_tensor_tensor(
                            dt[:], dtx[:], 0.0, dtp[:], ALU.max, ALU.add))
                        dt_steps.inc(nc.vector.tensor_tensor(
                            da[:, p], dt[:], a_sb[:].unsqueeze(1).broadcast_to((P, SUB, HEADS)), ALU.mult))
                        chain(dt_steps, i, 18, nc.vector.tensor_scalar(dt4[:, p], dt[:], 0.25, None, ALU.mult))

                    def z_gate(t, c, more):
                        dve.wait_ge(z_tanh.sem, z_tanh.now(t, c + 1))
                        dve.wait_ge(freed.sem, use(t, f"z{c}", more) + 1)
                        zs_ready.inc(nc.vector.scalar_tensor_tensor(
                            zs[:, c, :], ztanh[:], 1.0, zs[:, c, :], ALU.add, ALU.mult))

                    def weigh(t, half, c):
                        dve.wait_ge(xtok_ready.sem, xtok_ready.now(t, c + 1))
                        xdt_ready.inc(nc.vector.tensor_tensor(
                            xdt[:].rearrange("p (h d) -> p h d", h=HEADS),
                            xtok[:].rearrange("p (h d) -> p h d", h=HEADS),
                            dt4[:, half, c, :].unsqueeze(2).broadcast_to((P, HEADS, HD)), ALU.mult))
                        dve.wait_ge(sums_ready.sem, sums_ready.now(t, 2 * c + 2))
                        chain(gram_ready, t, c + 1, nc.vector.tensor_tensor(gsb[:], banks[3][:, 0:P], causal[:], ALU.mult))

                    def decayed(t, c):
                        dve.wait_ge(decay_ready.sem, decay_ready.now(t, 2 * c + 2))
                        mt_ready.inc(nc.vector.tensor_tensor(
                            decay[:], decay[:], gsb[:].unsqueeze(1).broadcast_to((P, HEADS, P)), ALU.mult))

                    def outputs(t, half, row, c):
                        h = slice(half * NST, (half + 1) * NST)
                        n0 = YSTEPS * c
                        dve.wait_ge(yi_done.sem, yi_done.now(t, c + 1))
                        dve.wait_ge(yt_done.sem, yt_done.now(t, c))
                        chain(y_steps, t, n0 + 1, nc.vector.tensor_tensor(
                            y[:].rearrange("p (h d) -> p h d", h=HEADS),
                            banks[7][:].rearrange("p (h d) -> p h d", h=HEADS),
                            ex[:, 0, :].unsqueeze(2).broadcast_to((P, HEADS, HD)), ALU.mult))
                        dve.wait_ge(s_done.sem, s_done.now(t, c + 1))
                        dve.wait_ge(stated.sem, stated.now(t, c + 1))
                        to = slice(NST, P) if half == 0 and c == SUB - 1 else h
                        chain(state_ready, t, c + 1, nc.vector.tensor_tensor(state[to, :], state[h, :], banks[2][h, :],
                                                                            ALU.add))
                        dve.wait_ge(y_done.sem, y_done.now(t, c + 1))
                        chain(y_steps, t, n0 + 2, nc.vector.tensor_tensor(y[:], y[:], banks[6][:], ALU.add))
                        dve.wait_ge(xd_ready.sem, xd_ready.now(t, c + 1))
                        chain(y_steps, t, n0 + 3, nc.vector.tensor_tensor(y[:], y[:], xd[:], ALU.add))
                        dve.wait_ge(zs_ready.sem, zs_ready.now(t, c + 1))
                        chain(y_steps, t, n0 + 4, nc.vector.tensor_tensor(y[:], y[:], zs[:, c, :], ALU.mult))
                        chain(y_steps, t, n0 + 5, nc.vector.tensor_reduce(ymax[:], y[:], AX_X, ALU.max,
                                                                          apply_absolute_value=True))
                        chain(y_steps, t, n0 + 6, nc.vector.tensor_scalar(ymax[:], ymax[:], TINY, None, ALU.max))
                        chain(y_steps, t, n0 + 7, nc.vector.tensor_scalar(
                            yexp[:, c:c + 1].bitcast(I32), ymax[:].bitcast(I32), 0x7F800000, None, ALU.bitwise_and))
                        chain(y_steps, t, n0 + 8, nc.vector.reciprocal(yq[:], yexp[:, c:c + 1]))
                        chain(y_steps, t, n0 + 9, nc.vector.tensor_scalar(yq[:], yq[:], WS, None, ALU.mult))
                        chain(y_steps, t, n0 + 10, nc.vector.tensor_scalar(ysplit[:, 0, :], y[:], yq[:], None, ALU.mult))
                        chain(y_steps, t, n0 + 11, nc.vector.scalar_tensor_tensor(
                            ysplit[:, 1, :], y[:], yq[:], ysplit[:, 0, :], ALU.mult, ALU.subtract))

                    def out_stats(t, c):
                        n0 = OSTEPS * c
                        dve.wait_ge(o_read.sem, o_read.now(t, c + 1))
                        o_steps.inc(nc.vector.bn_stats(ostat[:], x1[:]))
                        wait_apart(dve, o_steps.sem, o_steps.now(t, n0 + 1), dve_passed)
                        chain(o_steps, t, n0 + 2, nc.vector.bn_aggr(omv[:], ostat[:]))
                        chain(o_steps, t, n0 + 3, nc.vector.tensor_scalar(octok[:], yexp[:, c:c + 1], c_out[:], None, ALU.mult))
                        chain(o_steps, t, n0 + 4, nc.vector.tensor_scalar(oscale[:], omv[:, 1:2], octok[:], octok[:],
                                                                          ALU.mult, ALU.mult))
                        chain(o_steps, t, n0 + 5, nc.vector.tensor_scalar(ovar[:], oscale[:], EPS, None, ALU.add))
                        dve.wait_ge(orstd_ready.sem, orstd_ready.now(t, c + 1))
                        chain(o_steps, t, n0 + 6, nc.vector.tensor_scalar(oscale[:], orstd[:], octok[:], None, ALU.mult))
                        chain(o_steps, t, n0 + 7, nc.vector.tensor_scalar(obias[:], omv[:, 0:1], oscale[:], -1.0,
                                                                          ALU.mult, ALU.mult))

                    def body(t, half, row, more):
                        i, p = t + 1, 1 - half
                        weigh(t, half, 0)
                        ln_stats(i)
                        if half == 0:
                            state_cleared.inc(nc.vector.memset(state[0:NST, :], 0.0))
                        decayed(t, 0)
                        z_gate(t, 0, more)
                        outputs(t, half, row, 0)
                        weigh(t, half, 1)
                        z_gate(t, 1, more)
                        decayed(t, 1)
                        ln_split(i, 0, more)
                        ln_split(i, 1, more)
                        z_gate(t, 2, more)
                        ln_split(i, 2, more)
                        ln_split(i, 3, more)
                        outputs(t, half, row, 1)
                        weigh(t, half, 2)
                        masks(row, half, 1, more)
                        decayed(t, 2)
                        z_gate(t, 3, more)
                        out_stats(t, 0)
                        if more:
                            conv(i, p, 0)
                        outputs(t, half, row, 2)
                        weigh(t, half, 3)
                        decayed(t, 3)
                        masks(row, half, 2, more)
                        if more:
                            conv_silu(i, p, 0)
                            conv(i, p, 1)
                            conv_silu(i, p, 1)
                            conv(i, p, 2)
                        out_stats(t, 1)
                        masks(row, half, 3, more)
                        outputs(t, half, row, 3)
                        if more:
                            dt_input(i)
                        out_stats(t, 2)
                        if more:
                            conv_silu(i, p, 2)
                            conv(i, p, 3)
                            time_steps(i, p)
                        masks(row, half, 4, more)
                        if more:
                            conv_silu(i, p, 3)
                            conv(i, p, 4)
                        out_stats(t, 3)
                        if more:
                            conv_silu(i, p, 4)
                            masks(*following(row, half), 0)

                    ln_stats(0)
                    for s in range(SUB):
                        ln_split(0, s)
                    for j in range(CODES):
                        for n, v in enumerate((lut_hi32, lut_lo32)):
                            nc.vector.tensor_scalar(diag[:, n, j, :], ident[:], v[:, j:j + 1], None,
                                                    ALU.mult).then_inc(s_diag, 1)
                    for f in range(FB):
                        conv(0, 0, f)
                        if f >= 1:
                            conv_silu(0, 0, f - 1)
                    dt_input(0)
                    conv_silu(0, 0, FB - 1)
                    time_steps(0, 0)
                    masks(0, 0, 0)
                    iterations(dve, body)

        with ExitStack() as stage:
            def st(name, shape, dt=F32):
                return stage.enter_context(nc.sbuf_tensor(name, shape, dt))
            xf = [st(f"xf{i}", [P, SUB, D]) for i in range(2)]
            stats = st("fstats", [P, SUB, 6])
            mv = st("fmv", [P, SUB, 2])
            vare = st("fvare", [P, SUB])
            rstd = st("frstd", [P, SUB])
            xn = st("fxn", [P, D])
            xsplit = st("fxsplit", [P, SUB, 2, D], F16)
            xts = [xt, st("xt_odd", [P, 2, KC, TILE], F16)]
            gtanh = st("gtanh", [P, 2, TILE])
            gsilu = st("gsilu", [P, 2, TILE])
            hf = st("hf", [P, 2, TILE])
            h_hi = st("h_hi", [P, MB, TILE], F16)
            h_lo = st("h_lo", [P, MB, TILE], F16)
            dstat = st("dstat", [P, SUB, 6])
            dmv = st("dmv", [P, SUB, 2])
            dvar = st("dvar", [P, SUB])
            drstd = st("drstd", [P, SUB])
            dscale = st("dscale", [P, SUB])
            dn = st("dn", [P, 2, D])
            res = st("res", [P, 2, D])

            x_loaded = [Signal(sem(f"x1_loaded{i}"), 1, step=16) for i in range(2)]
            ln_steps = Signal(sem("f_ln_steps"), 3 * SUB)
            rstd_ready = Signal(sem("f_rstd_ready"), 1)
            split_steps = Signal(sem("f_split_steps"), 3 * SUB)
            xt_filled = Signal(sem("f_xt_transposed"), SUB)
            xt_ready = Signal(sem("f_xt_ready"), SUB)
            gate_done = Signal(sem("gate_done"), MB)
            up_done = Signal(sem("up_done"), MB)
            gtanh_ready = Signal(sem("gate_tanh_ready"), MB)
            gsilu_ready = Signal(sem("gate_silu_ready"), MB, credit=True)
            hf_ready = Signal(sem("h_ready"), MB, credit=True)
            hhi_ready = Signal(sem("h_hi_ready"), MB)
            hlo_ready = Signal(sem("h_lo_ready"), MB)
            down_done = Signal(sem("down_done"), SUB, credit=True)
            d_steps = Signal(sem("down_ln_steps"), SUB * 5)
            drstd_ready = Signal(sem("down_rstd_ready"), SUB)
            dn_ready = Signal(sem("down_normalised"), SUB, credit=True)
            res_ready = Signal(sem("output_ready"), SUB, credit=True)
            res_stored = [Signal(sem(f"output_stored{i}"), SUB // 2, step=16, credit=True) for i in range(2)]
            out_chunks = out.rearrange("(c p) d -> c p d", p=P)
            STATS_AT, SPLIT_AT, TRANSPOSE_AT = 2, 3, 5
            assert TRANSPOSE_AT + SUB <= MB

            def tiles(eng, body):
                with eng.Fori(0, TILES // 2 - 1) as pair:
                    for i in range(2):
                        body(pair * 2 + i, i, pair, True)
                for i in range(2):
                    body(TILES - 2 + i, i, TILES // 2 - 1, i == 0)

            with nc.Block() as block:
                @block.sync
                def _(sp):
                    for g in res_stored:
                        g.start(sp)
                    for i in range(2):
                        x_loaded[i].inc(sp.dma_start(xf[i][:], x1_tiles[i]))

                    def store_then_load(pair, more):
                        for i in range(2):
                            t = pair * 2 + i
                            for c in range(SUB):
                                sp.wait_ge(res_ready.sem, res_ready.now(t, c + 1))
                                res_stored[c % 2].inc(sp.dma_start(out_chunks[t * SUB + c], res[:, c % 2, :]))
                            if more:
                                x_loaded[i].inc(sp.dma_start(xf[i][:], x1_tiles[t + 2]))

                    with sp.Fori(0, TILES // 2 - 1) as pair:
                        store_then_load(pair, True)
                    store_then_load(TILES // 2 - 1, False)
                    for g in res_stored:
                        sp.wait_ge(g.sem, g.now(TILES - 1, SUB // 2))

                @block.gpsimd
                def _(pool):
                    res_ready.start(pool)

                    def body(t, i, pair, more):
                        if more:
                            pool.wait_ge(ln_steps.sem, ln_steps.now(t, 3 * SUB))
                            rstd_ready.inc(nc.gpsimd.tensor_tensor(rstd[:], vare[:], neg_half[:], ALU.pow))
                        pool.wait_ge(x_loaded[i].sem, x_loaded[i].now(pair, 1))
                        for c in range(SUB):
                            pool.wait_ge(d_steps.sem, d_steps.now(t, 5 * c + 4))
                            drstd_ready.inc(nc.gpsimd.tensor_tensor(drstd[:, c:c + 1], dvar[:, c:c + 1],
                                                                    neg_half[:, 0:1], ALU.pow))
                            pool.wait_ge(dn_ready.sem, dn_ready.now(t, c + 1))
                            g = res_stored[c % 2]
                            pool.wait_ge(g.sem, g.prev(t, SUB // 2) if c < 2 else g.now(t, c // 2))
                            res_ready.inc(nc.gpsimd.tensor_tensor(res[:, c % 2, :], dn[:, c % 2, :],
                                                                  xf[i][:, c, :], ALU.add))

                    tiles(pool, body)

                @block.scalar
                def _(act):
                    def body(t, i, pair, more):
                        def high(m):
                            w = MW[m]
                            act.wait_ge(hf_ready.sem, hf_ready.now(t, m + 1))
                            if m == 0:
                                act.wait_ge(down_done.sem, down_done.prev(t, SUB))
                            hhi_ready.inc(nc.scalar.activation(h_hi[0:w, m, :], hf[0:w, m % 2, :], ACT.Copy))

                        for m in range(MB):
                            w = MW[m]
                            act.wait_ge(gate_done.sem, gate_done.now(t, m + 1))
                            act.wait_ge(gsilu_ready.sem, gsilu_ready.prev(t, LAST_OF_SLOT[m]) if m < 2
                                        else gsilu_ready.now(t, m - 1))
                            gtanh_ready.inc(nc.scalar.activation(gtanh[0:w, m % 2, :], banks[2 + m % 2][0:w, :],
                                                                 ACT.Tanh, scale=c_gate_half[0:w, :]))
                            if m >= 1:
                                high(m - 1)
                            s = m - TRANSPOSE_AT - 1
                            if more and 0 <= s < SUB:
                                act.wait_ge(xt_filled.sem, xt_filled.now(t, s + 1))
                                xt_ready.inc(nc.scalar.activation(
                                    xts[1 - i][:, :, :, s * P:(s + 1) * P],
                                    banks[s % 2][:].bitcast(F16).rearrange("p (n k t) -> p n k t", n=2, k=KC), ACT.Copy))
                        high(MB - 1)

                    tiles(act, body)

                @block.tensor
                def _(pe):
                    down_done.start(pe)

                    def body(t, i, pair, more):
                        if not isinstance(t, int) or t > 0:
                            pe.wait_ge(xt_ready.sem, xt_ready.now(t, 0))
                        for m in range(MB):
                            w = MW[m]
                            for col0, base, done, free in ((GATE0, 2, gate_done, gsilu_ready), (UP0, 4, up_done, hf_ready)):
                                if m < 2:
                                    pe.wait_ge(free.sem, free.prev(t, LAST_OF_SLOT[m]))
                                else:
                                    pe.wait_ge(free.sem, free.now(t, m - 1))
                                bank = banks[base + m % 2][0:w, :]
                                for k in range(KC):
                                    c0 = col0 + k * INTER + m * P
                                    for n, (wt, half) in enumerate(((ffn_hi, 0), (ffn_hi, 1), (ffn_lo, 0))):
                                        last = nc.tensor.matmul(bank, wt[:, c0:c0 + w], xts[i][:, half, k, :],
                                                                start=(k == 0 and n == 0),
                                                                stop=(k == KC - 1 and n == 2))
                                done.inc(last)
                            s = m - TRANSPOSE_AT
                            if more and 0 <= s < SUB:
                                pe.wait_ge(split_steps.sem, split_steps.now(t, 3 * (s + 1)))
                                pe.wait_ge(xt_ready.sem, xt_ready.now(t, max(s - 1, 0)))
                                b = banks[s % 2][:].bitcast(F16).rearrange("p (n k t) -> p n k t", n=2, k=KC)
                                for n in range(2):
                                    for k in range(KC):
                                        last = nc.tensor.transpose(b[:, n, k, :], xsplit[:, s, n, k * P:(k + 1) * P],
                                                                   ident_h[:])
                                xt_filled.inc(last)
                        for c in range(SUB):
                            tok = slice(c * P, (c + 1) * P)
                            pe.wait_ge(dn_ready.sem, dn_ready.prev(t, SUB - 1 + c) if c < 2 else dn_ready.now(t, c - 1))
                            for m in range(MB):
                                w = MW[m]
                                if c == 0:
                                    pe.wait_ge(hlo_ready.sem, hlo_ready.now(t, m + 1))
                                d0 = DOWN0 + m * D
                                for n, (h, wt) in enumerate(((h_hi, ffn_hi), (h_hi, ffn_lo), (h_lo, ffn_hi))):
                                    last = nc.tensor.matmul(banks[6 + c % 2][:], h[0:w, m, tok], wt[0:w, d0:d0 + D],
                                                            start=(m == 0 and n == 0), stop=(m == MB - 1 and n == 2))
                            down_done.inc(last)

                    tiles(pe, body)

                @block.vector
                def _(dve):
                    for g in (gsilu_ready, hf_ready, dn_ready):
                        g.start(dve)

                    def body(t, i, pair, more):
                        def chain(sig, k, ins):
                            sig.inc(ins)
                            dve.wait_ge(sig.sem, sig.now(t, k))

                        def next_stats():
                            x = x_loaded[1 - i]
                            dve.wait_ge(x.sem, x.now(pair + i, 1))
                            for s in range(SUB):
                                ln_steps.inc(nc.vector.bn_stats(stats[:, s, :], xf[1 - i][:, s, :]))
                            for s in range(SUB):
                                wait_apart(dve, ln_steps.sem, ln_steps.now(t, s + 1), dve_passed)
                                ln_steps.inc(nc.vector.bn_aggr(mv[:, s, :], stats[:, s, :]))
                            for s in range(SUB):
                                dve.wait_ge(ln_steps.sem, ln_steps.now(t, SUB + s + 1))
                                ln_steps.inc(nc.vector.tensor_scalar(vare[:, s:s + 1], mv[:, s, 1:2], 1.0 / XS ** 2,
                                                                     EPS / XS ** 2, ALU.mult, ALU.add))

                        def next_split(s):
                            dve.wait_ge(rstd_ready.sem, rstd_ready.now(t, 1))
                            chain(split_steps, 3 * s + 1, nc.vector.tensor_scalar(
                                xn[:], xf[1 - i][:, s, :], mv[:, s, 0:1], rstd[:, s:s + 1], ALU.subtract, ALU.mult))
                            chain(split_steps, 3 * s + 2, nc.vector.tensor_copy(xsplit[:, s, 0, :], xn[:]))
                            chain(split_steps, 3 * s + 3, nc.vector.tensor_sub(xsplit[:, s, 1, :], xn[:],
                                                                               xsplit[:, s, 0, :]))

                        def low(m):
                            w = MW[m]
                            dve.wait_ge(hhi_ready.sem, hhi_ready.now(t, m + 1))
                            hlo_ready.inc(nc.vector.tensor_sub(h_lo[0:w, m, :], hf[0:w, m % 2, :], h_hi[0:w, m, :]))

                        for m in range(MB):
                            w = MW[m]
                            dve.wait_ge(gtanh_ready.sem, gtanh_ready.now(t, m + 1))
                            gsilu_ready.inc(nc.vector.scalar_tensor_tensor(
                                gsilu[0:w, m % 2, :], gtanh[0:w, m % 2, :], 1.0, banks[2 + m % 2][0:w, :],
                                ALU.add, ALU.mult))
                            dve.wait_ge(gsilu_ready.sem, gsilu_ready.now(t, m + 1))
                            dve.wait_ge(up_done.sem, up_done.now(t, m + 1))
                            hf_ready.inc(nc.vector.scalar_tensor_tensor(
                                hf[0:w, m % 2, :], gsilu[0:w, m % 2, :], HSCALE, banks[4 + m % 2][0:w, :],
                                ALU.mult, ALU.mult))
                            if m >= 1:
                                low(m - 1)
                            if more and m == STATS_AT:
                                next_stats()
                            if more and 0 <= m - SPLIT_AT < SUB:
                                next_split(m - SPLIT_AT)
                        low(MB - 1)
                        for c in range(SUB):
                            dve.wait_ge(down_done.sem, down_done.now(t, c + 1))
                            bank = banks[6 + c % 2]
                            d0 = 5 * c
                            d_steps.inc(nc.vector.bn_stats(dstat[:, c, :], bank[:]))
                            wait_apart(dve, d_steps.sem, d_steps.now(t, d0 + 1), dve_passed)
                            chain(d_steps, d0 + 2, nc.vector.bn_aggr(dmv[:, c, :], dstat[:, c, :]))
                            chain(d_steps, d0 + 3, nc.vector.tensor_scalar(dscale[:, c:c + 1], dmv[:, c, 1:2],
                                                                           c_down[:], c_down[:], ALU.mult, ALU.mult))
                            chain(d_steps, d0 + 4, nc.vector.tensor_scalar(dvar[:, c:c + 1], dscale[:, c:c + 1],
                                                                           EPS, None, ALU.add))
                            dve.wait_ge(drstd_ready.sem, drstd_ready.now(t, c + 1))
                            chain(d_steps, d0 + 5, nc.vector.tensor_scalar(dscale[:, c:c + 1], drstd[:, c:c + 1],
                                                                           c_down[:], None, ALU.mult))
                            dve.wait_ge(res_ready.sem, res_ready.prev(t, SUB - 1 + c) if c < 2
                                        else res_ready.now(t, c - 1))
                            dn_ready.inc(nc.vector.tensor_scalar(dn[:, c % 2, :], bank[:], dmv[:, c, 0:1],
                                                                 dscale[:, c:c + 1], ALU.subtract, ALU.mult))

                    tiles(dve, body)


def kernel(**inputs):
    import numpy as np
    import concourse.bacc as bacc
    from concourse.bass_utils import run_bass_kernel_spmd

    v = {k[3:]: np.asarray(a) for k, a in inputs.items()}
    B, L, _ = v["attn_u"].shape

    def blocks(codes_t):
        rows, n = codes_t.shape
        full = np.zeros((-(-rows // P) * P, n), codes_t.dtype)
        full[:rows] = codes_t
        return full.reshape(-1, P, n).transpose(1, 0, 2).reshape(P, -1)

    arrays = {
        "u": v["attn_u"].reshape(B * L, D),
        "w_in_t": v["attn_W_in"].T,
        "conv_w": v["attn_conv_w"].reshape(-1, TAPS),
        "conv_b": v["attn_conv_b"],
        "w_out_t": v["attn_W_out"].T,
        "a_log": v["attn_A_log"],
        "d_param": v["attn_D_param"],
        "dt_bias": v["attn_dt_bias"],
        "lut": v["ffn_lut"],
        "codes": np.concatenate([blocks(v["ffn_gate_idx"].T), blocks(v["ffn_up_idx"].T),
                                 blocks(v["ffn_down_idx"].T)], axis=1),
    }
    arrays = {k: np.ascontiguousarray(a) for k, a in arrays.items()}
    nc = bacc.Bacc("TRN2", target_bir_lowering=False, num_devices=1)
    args = [nc.dram_tensor(k, a.shape, mybir.dt.from_np(a.dtype), kind="ExternalInput").ap()
            for k, a in arrays.items()]
    out = nc.dram_tensor("out", (B * L, D), F32, kind="ExternalOutput").ap()
    sandwich_kernel(nc, *args, out)
    r = run_bass_kernel_spmd(nc, [arrays], core_ids=[0])
    return r.results[0]["out"].reshape(B, L, D)
```

```python
from contextlib import ExitStack

import concourse.bass as bass
from concourse import mybir

P = 128
F32 = mybir.dt.float32
F16 = mybir.dt.float16
I32 = mybir.dt.int32
ALU = mybir.AluOpType
ACT = mybir.ActivationFunctionType
AX_X = mybir.AxisListType.X
AX_XY = mybir.AxisListType.XY
RMAX = bass.bass_isa.ReduceOp.max

EPS = 1e-5
D = 512
KC = D // P
NST = 64
HEADS = 8
HD = D // HEADS
TAPS = 4
HALO = TAPS - 1
INTER = 1376
CODES = 16
TILE = 512
SUB = TILE // P
HALVES = 2
FB = 5
MB = -(-INTER // P)
LAST_OF_SLOT = [MB - (MB - 1 - m) % 2 for m in range(2)]
MW = [min(P, INTER - P * m) for m in range(MB)]

X0 = D
B0 = 2 * D
DT0 = 2 * D + 2 * NST
D_IN = DT0 + HEADS

GATE0, UP0, DOWN0 = 0, KC * INTER, 2 * KC * INTER
WCOLS = DOWN0 + MB * D
UNIT = 416
TILE_UNITS = 5
PAIRS = CODES // 2
GROUP = 4
GROUPS = 2 * PAIRS // GROUP
assert PAIRS == 2 * GROUP
YSTEPS = 11
OSTEPS = 2
TSTEPS = 15
CSTEPS = TAPS - 1

FRONT_USES = ["T0", "T1", "T2", "T3", "dt", "X0", "X1", "X2", "X3", "X4"]
USES = ["z0", "z1", "z2", "z3", "D0", "D0'", "T0", "T1", "D1", "D1'", "T2", "T3", "X0", "X1", "X2",
        "D2", "D2'", "X3", "X4", "dt", "D3", "D3'", "D4", "D4'"]
LAST_USES = [x for x in USES if x[0] not in "Xd"]
assert len(USES) % 2 == 0 and len(FRONT_USES) % 2 == 0

XS = 2.0 ** 10
WS = 2.0 ** 14
TINY = 2.0 ** -60
HSCALE = 2.0 ** -54


class Signal:

    def __init__(self, sem, per, step=1, credit=False):
        self.sem, self.per, self.step, self.credit = sem, per, step, credit

    def inc(self, ins):
        ins.then_inc(self.sem, self.step)

    def start(self, eng):
        eng.sem_inc(self.sem, self.per * self.step)

    def now(self, t, k):
        ahead = self.per if self.credit else 0
        return (t * self.per + (k + ahead)) * self.step

    def prev(self, t, k):
        assert self.credit
        return (t * self.per + k) * self.step


def wait_apart(eng, sem, value, passed):
    eng.wait_ge(sem, value)
    eng.sem_inc(passed, 1)


def sandwich_kernel(nc, u, w_in_t, conv_w, conv_b, w_out_t, a_log, d_param, dt_bias, lut, codes, out):
    T = u.shape[0]
    TILES = T // TILE
    BATCHES = TILES // HALVES
    assert TILES * TILE_UNITS * UNIT == WCOLS
    codes_blocks = codes.rearrange("(a r) n -> r a n", r=NST)
    u_chunks = u.rearrange("(c p) d -> c p d", p=P)
    u_tiles = u.rearrange("(n s p) d -> n p s d", s=SUB, p=P)
    x1_dram = nc.dram_tensor("x1_scratch", [T, D], F32).ap()
    x1_chunks = x1_dram.rearrange("(c p) d -> c p d", p=P)
    x1_tiles = x1_dram.rearrange("(n s p) d -> n p s d", s=SUB, p=P)

    ctx = ExitStack()
    with ctx:
        def sb(name, shape, dt=F32):
            return ctx.enter_context(nc.sbuf_tensor(name, shape, dt))

        def sem(name):
            return ctx.enter_context(nc.semaphore(name))

        win_hi = sb("win_hi", [P, KC, D_IN], F16)
        win_lo = sb("win_lo", [P, KC, D_IN], F16)
        wout_hi = sb("wout_hi", [P, KC, D], F16)
        wout_lo = sb("wout_lo", [P, KC, D], F16)
        ffn_hi = sb("ffn_hi", [P, WCOLS], F16)
        ffn_lo = sb("ffn_lo", [P, WCOLS], F16)
        ident = sb("ident", [P, P])
        causal = sb("causal", [P, P])
        below = sb("below", [P, P])
        ones = sb("ones", [P, P])
        neg_half = sb("neg_half", [P, SUB])
        lut_sb = sb("lut_sb", [P, CODES])
        conv_w_sb = sb("conv_w_sb", [P, FB, TAPS])
        conv_b_sb = sb("conv_b_sb", [P, FB])
        dt_bias_sb = sb("dt_bias_sb", [P, HEADS])
        a_sb = sb("a_sb", [P, HEADS])
        d_sb = sb("d_sb", [P, HEADS])
        big = sb("big", [P, 3])
        lowest = sb("lowest", [P, 3])
        win_max = sb("win_max", [P, KC])
        expo = sb("expo", [P, 3])
        wscale = sb("wscale", [P, 3])
        c_in = sb("c_in", [P, 1])
        c_in_half = sb("c_in_half", [P, 1])
        c_out = sb("c_out", [P, 1])
        c_gate_half = sb("c_gate_half", [P, 1])
        c_down = sb("c_down", [P, 1])
        lut_s = sb("lut_s", [P, CODES])
        lut_hi = sb("lut_hi", [P, CODES], F16)
        lut_hi32 = sb("lut_hi32", [P, CODES])
        lut_lo32 = sb("lut_lo32", [P, CODES])

        xt = sb("xt", [P, 2, KC, TILE], F16)
        eps_c = sb("eps_c", [P, SUB])
        neg_one = sb("neg_one", [P, SUB])
        xs_c = sb("xs_c", [P, SUB])
        zero_c = sb("zero_c", [P, SUB])
        ident_h = sb("ident_h", [P, P], F16)
        dve_passed, pool_passed = sem("dve_waits_passed"), sem("pool_waits_passed")
        banks = [ctx.enter_context(nc.psum_tensor(f"bank{i}", [P, 512], F32)) for i in range(8)]

        with ExitStack() as stage:
            def st(name, shape, dt=F32):
                return stage.enter_context(nc.sbuf_tensor(name, shape, dt))
            fold = st("fold", [P, NST])
            lut_sel = st("lut_sel", [P, 2, PAIRS])
            diag = st("diag", [P, PAIRS, 2, NST], F16)
            codes_sb = st("codes_sb", [P, 2, UNIT], I32)
            codes_h = st("codes_h", [P, 2, UNIT], F16)
            mask = st("mask", [P, 2, PAIRS, UNIT], F16)
            assert KC == SUB
            ut = st("ut", [P, SUB, D])
            stats = st("stats", [P, SUB, 6])
            mv = st("mv", [P, SUB, 2])
            vare = st("vare", [P, SUB])
            rstd = st("rstd", [P, SUB])
            shift = st("shift", [P, SUB])
            xsplit = st("xsplit", [P, 2, 2, D], F16)
            cin = st("cin", [P, 2, HALO + TILE])
            halo = st("halo", [P, FB, HALO])
            cacc = st("cacc", [P, 2, TILE])
            ctanh = st("ctanh", [P, TILE])
            dtr = st("dtr", [P, SUB, HEADS])
            dtx = st("dtx", [P, SUB, HEADS])
            dte = st("dte", [P, SUB, HEADS])
            dtz = st("dtz", [P, SUB, HEADS])
            dtz2 = st("dtz2", [P, SUB, HEADS])
            dtp = st("dtp", [P, SUB, HEADS])
            dt = st("dt", [P, SUB, HEADS])
            dt4 = st("dt4", [P, 2, SUB, HEADS])
            da = st("da", [P, 2, SUB, HEADS])
            xs = st("xs", [P, 2, KC, TILE])
            bs = st("bs", [P, TILE])
            cs = st("cs", [P, TILE])
            ztanh = st("ztanh", [P, D])
            zs = st("zs", [P, SUB, D])
            seg = st("seg", [P, HEADS, P])
            decay = st("decay", [P, HEADS, P])
            gsb = st("gsb", [P, P])
            bt = st("bt", [P, NST])
            ex = st("ex", [P, 3, HEADS])
            xtok = st("xtok", [P, D])
            xdt = st("xdt", [P, D])
            xd = st("xd", [P, D])
            state = st("state", [P, D])
            y = st("y", [P, D])
            ymax = st("ymax", [P, 1])
            yexp = st("yexp", [P, SUB])
            yq = st("yq", [P, 1])
            ysplit = st("ysplit", [P, 2, D], F16)
            yt = st("yt", [P, 2, KC, P], F16)
            ostat = st("ostat", [P, 6])
            omv = st("omv", [P, 2, 2])
            octok = st("octok", [P, 1])
            ovar = st("ovar", [P, 1])
            orstd = st("orstd", [P, 1])
            oscale = st("oscale", [P, 1])
            obias = st("obias", [P, 1])
            ures = st("ures", [P, D])
            x1 = st("x1", [P, 2, D])

            raw = ffn_hi[:].bitcast(F32)
            w_in_f = raw[:, 0:KC * D_IN].rearrange("p (k n) -> p k n", k=KC)
            w_out_f = raw[:, KC * D_IN:KC * (D_IN + D)].rearrange("p (k n) -> p k n", k=KC)
            PIECES = [(w_in_f[:, k:k + KC // 2, X0:], win_hi[:, k:k + KC // 2, X0:], win_lo[:, k:k + KC // 2, X0:], 0)
                      for k in (0, KC // 2)]
            PIECES += [(w_in_f[:, :, 0:X0], win_hi[:, :, 0:X0], win_lo[:, :, 0:X0], 0),
                       (w_out_f, wout_hi[:], wout_lo[:], 1)]
            s_win = [sem(f"win_loaded{k}") for k in range(KC)]
            s_wout, s_small = sem("wout_loaded"), sem("small_loaded")
            s_fill, s_const = sem("constants_filled"), sem("constants_ready")
            s_big, s_all = sem("partition_maxima"), sem("global_maxima")
            s_step, s_alog = sem("scaling_steps"), sem("a_exponential")
            s_ident, s_scale = sem("identity_as_half"), sem("weight_scales_ready")
            s_hi, s_lo = sem("weights_hi_ready"), sem("weights_lo_ready")

            filled = Signal(sem("shared_bank_filled"), len(USES))
            freed = Signal(sem("shared_bank_freed"), len(USES))
            s_diag = sem("diagonals_ready")
            loaded = Signal(sem("codes_loaded"), 2 * TILE_UNITS, step=16)
            as_half = Signal(sem("codes_as_half"), TILE_UNITS)
            lowered = Signal(sem("second_codes_lowered"), TILE_UNITS)
            masks_ready = Signal(sem("masks_ready"), TILE_UNITS * GROUPS)
            masks_used = Signal(sem("masks_used"), TILE_UNITS * 2, credit=True)
            u_loaded = Signal(sem("u_loaded"), 1, step=16)
            ln_steps = Signal(sem("ln_steps"), 2 * SUB)
            rstd_steps = Signal(sem("rstd_steps"), 5)
            norm_steps = Signal(sem("input_normalised"), 2 * SUB)
            split_ready = Signal(sem("input_split"), SUB)
            cin_steps = Signal(sem("conv_halo_steps"), FB * 2)
            conv_first = Signal(sem("conv_first_tap"), FB)
            conv_steps = Signal(sem("conv_steps"), FB * CSTEPS)
            ctanh_ready = Signal(sem("conv_tanh_ready"), FB)
            xs_ready = Signal(sem("conv_silu_ready"), FB + 1)
            dt_steps = Signal(sem("dt_steps"), 3 + TSTEPS)
            dt_exp = Signal(sem("dt_exponential"), 1)
            z_tanh = Signal(sem("z_tanh_steps"), 2 * SUB)
            zs_ready = Signal(sem("z_gate_ready"), SUB)
            seg_ready = Signal(sem("segment_terms_ready"), SUB)
            xtok_done = Signal(sem("x_tokens_transposed"), SUB)
            small_done = Signal(sem("gram_and_sums_done"), SUB)
            seg_done = Signal(sem("segment_sums_done"), SUB)
            xtok_ready = Signal(sem("x_tokens_ready"), SUB)
            sums_ready = Signal(sem("sums_exponentiated"), SUB * 2)
            decay_ready = Signal(sem("decay_ready"), SUB * 2)
            xdt_ready = Signal(sem("x_dt_ready"), SUB)
            gram_ready = Signal(sem("gram_masked"), SUB, credit=True)
            mt_ready = Signal(sem("decayed_gram_ready"), SUB)
            xd_ready = Signal(sem("x_d_ready"), SUB)
            xw_ready = Signal(sem("x_weighted_ready"), SUB)
            stated = Signal(sem("state_decayed"), SUB)
            state_ready = Signal(sem("state_ready"), SUB, credit=True)
            state_cleared = Signal(sem("state_cleared"), 1)
            y_done = Signal(sem("y_inner_done"), SUB)
            yi_done = Signal(sem("y_carried_done"), SUB)
            s_done = Signal(sem("state_update_done"), SUB)
            y_steps = Signal(sem("y_steps"), SUB * YSTEPS, credit=True)
            yt_done = Signal(sem("y_transposed"), SUB)
            yt_ready = Signal(sem("yt_ready"), SUB, credit=True)
            o_done = Signal(sem("out_projected"), SUB)
            o_steps = Signal(sem("o_steps"), SUB * OSTEPS)
            oscale_steps = Signal(sem("out_scale_steps"), SUB * 8)
            o_read = Signal(sem("out_projection_read"), SUB, credit=True)
            normalised = Signal(sem("out_normalised"), SUB)
            ures_loaded = Signal(sem("u_chunk_loaded"), SUB, step=16)
            x1_ready = Signal(sem("x1_ready"), SUB, credit=True)
            x1_stored = [Signal(sem(f"x1_stored{i}"), SUB // 2, step=16, credit=True) for i in range(2)]

            def use(t, name, more=True):
                if isinstance(t, int) and t < 0:
                    return FRONT_USES.index(name)
                return t * len(USES) + (len(FRONT_USES) + (USES if more else LAST_USES).index(name))

            def bank_of(name, more=True):
                return banks[(USES if more else LAST_USES).index(name) % 2]

            def front_bank(t, name, more=True):
                return banks[FRONT_USES.index(name) % 2] if isinstance(t, int) and t < 0 else bank_of(name, more)

            def following(row, half):
                return (row, 1) if half == 0 else (row + 1, 0)

            def use_of_front(i, name, more=True):
                return use(-1, name) if isinstance(i, int) and i == 0 else use(i - 1, name, more)

            def iterations(eng, body):
                with eng.Fori(0, BATCHES - 1) as row:
                    for half in range(HALVES):
                        body(row * HALVES + half, half, row, True)
                for half in range(HALVES):
                    body((BATCHES - 1) * HALVES + half, half, BATCHES - 1, half < HALVES - 1)

            with nc.Block() as block:
                @block.sync
                def _(sp):
                    for g in x1_stored:
                        g.start(sp)

                    def load_codes(row, half, k):
                        t = row * HALVES + half
                        sp.wait_ge(as_half.sem, as_half.now(t, k))
                        for copy in range(2):
                            loaded.inc(sp.dma_start(codes_sb[copy * NST:(copy + 1) * NST],
                                                     codes_blocks[:, :, bass.ds((t * TILE_UNITS + k) * UNIT, UNIT)]))

                    u_loaded.inc(sp.dma_start(ut[:], u_tiles[0]))
                    w_in_blocks = w_in_t.rearrange("(c p) n -> c p n", p=P)
                    for k in range(KC):
                        sp.dma_start(w_in_f[:, k, :], w_in_blocks[k]).then_inc(s_win[k], 16)
                    sp.dma_start(w_out_f, w_out_t.rearrange("(c p) n -> p c n", p=P)).then_inc(s_wout, 16)
                    load_codes(0, 0, 0)
                    sp.wait_ge(split_ready.sem, split_ready.now(0, SUB))
                    u_loaded.inc(sp.dma_start(ut[:], u_tiles[1]))
                    load_codes(0, 0, 1)

                    def residual(t, c):
                        sp.wait_ge(x1_ready.sem, x1_ready.prev(t, SUB + c))
                        ures_loaded.inc(sp.dma_start(ures[:], u_chunks[t * SUB + c]))

                    def body(t, half, row, more):
                        residual(t, 0)
                        load_codes(row, half, 2)
                        if more:
                            sp.wait_ge(split_ready.sem, split_ready.now(t + 1, SUB))
                            if isinstance(t, int):
                                for g in x1_stored:
                                    sp.wait_ge(g.sem, g.now(0, SUB // 2))
                                u_loaded.inc(sp.dma_start(ut[:], x1_tiles[0]))
                            else:
                                u_loaded.inc(sp.dma_start(ut[:], u_tiles[t + 2]))
                        for c in range(SUB):
                            if c < 2:
                                load_codes(row, half, 3 + c)
                            elif more:
                                load_codes(*following(row, half), c - 2)
                            sp.wait_ge(x1_ready.sem, x1_ready.now(t, c + 1))
                            x1_stored[c % 2].inc(sp.dma_start(x1_chunks[t * SUB + c], x1[:, c % 2, :]))
                            if c + 1 < SUB:
                                residual(t, c + 1)

                    iterations(sp, body)
                    for g in x1_stored:
                        sp.wait_ge(g.sem, g.now(TILES - 1, SUB // 2))

                @block.gpsimd
                def _(pool):
                    x1_ready.start(pool)

                    def front_rstd(i):
                        pool.wait_ge(ln_steps.sem, ln_steps.now(i, 2 * SUB))
                        for n, (dst, a, b, op) in enumerate((
                                (vare[:], mv[:, :, 1], eps_c[:], ALU.add), (vare[:], vare[:], neg_half[:], ALU.pow),
                                (rstd[:], vare[:], xs_c[:], ALU.mult), (vare[:], mv[:, :, 0], neg_one[:], ALU.mult),
                                (shift[:], vare[:], rstd[:], ALU.mult))):
                            rstd_steps.inc(nc.gpsimd.tensor_tensor(dst, a, b, op))
                            pool.wait_ge(rstd_steps.sem, rstd_steps.now(i, n + 1))

                    def to_half(row, half, k):
                        t = row * HALVES + half
                        pool.wait_ge(loaded.sem, loaded.now(t, 2 * (k + 1)))
                        pool.wait_ge(masks_ready.sem, masks_ready.now(t, k * GROUPS))
                        pool.sem_inc(pool_passed, 1)
                        as_half.inc(nc.gpsimd.tensor_copy(codes_h[:], codes_sb[:]))

                    def segments(t, p, c):
                        pool.wait_ge(seg_done.sem, seg_done.now(t, c))
                        if c == 0:
                            pool.wait_ge(dt_steps.sem, dt_steps.now(t, 17))
                        seg_ready.inc(nc.gpsimd.tensor_tensor(
                            seg[:], causal[:].unsqueeze(1).broadcast_to((P, HEADS, P)),
                            da[:, p, c, :].unsqueeze(2).broadcast_to((P, HEADS, P)), ALU.mult))

                    def weights(t, half, c):
                        pool.wait_ge(xtok_ready.sem, xtok_ready.now(t, c + 1))
                        pool.wait_ge(y_steps.sem, y_steps.prev(t, YSTEPS * (SUB + c - 1) + 4))
                        pool.wait_ge(stated.sem, stated.now(t, c))
                        if c == 0:
                            pool.wait_ge(dt_steps.sem, dt_steps.now(t, 18))
                        xdt_ready.inc(nc.gpsimd.tensor_tensor(
                            xdt[:].rearrange("p (h d) -> p h d", h=HEADS),
                            xtok[:].rearrange("p (h d) -> p h d", h=HEADS),
                            dt4[:, half, c, :].unsqueeze(2).broadcast_to((P, HEADS, HD)), ALU.mult))
                        xd_ready.inc(nc.gpsimd.tensor_tensor(
                            xd[:].rearrange("p (h d) -> p h d", h=HEADS),
                            xtok[:].rearrange("p (h d) -> p h d", h=HEADS),
                            d_sb[:].unsqueeze(2).broadcast_to((P, HEADS, HD)), ALU.mult))
                        pool.wait_ge(sums_ready.sem, sums_ready.now(t, 2 * c + 1))
                        pool.wait_ge(xdt_ready.sem, xdt_ready.now(t, c + 1))
                        pool.wait_ge(xd_ready.sem, xd_ready.now(t, c + 1))
                        xw_ready.inc(nc.gpsimd.tensor_tensor(
                            xtok[:].rearrange("p (h d) -> p h d", h=HEADS),
                            xdt[:].rearrange("p (h d) -> p h d", h=HEADS),
                            ex[:, 1, :].unsqueeze(2).broadcast_to((P, HEADS, HD)), ALU.mult))

                    def z_gate(t, c):
                        pool.wait_ge(z_tanh.sem, z_tanh.now(t, 2 * (c + 1)))
                        zs_ready.inc(nc.gpsimd.tensor_tensor(zs[:, c, :], zs[:, c, :], ztanh[:], ALU.mult))

                    def decay_state(t, half, row, c, apart):
                        h0 = half * NST
                        if half == 0 and c == 0:
                            pool.wait_ge(state_cleared.sem, state_cleared.now(row, 1))
                        else:
                            pool.wait_ge(state_ready.sem, state_ready.prev(t, SUB + c))
                        pool.wait_ge(yi_done.sem, yi_done.now(t, c + 1))
                        pool.wait_ge(*apart)
                        stated.inc(nc.gpsimd.tensor_tensor(
                            state[h0:h0 + NST, :].rearrange("p (h d) -> p h d", h=HEADS),
                            state[h0:h0 + NST, :].rearrange("p (h d) -> p h d", h=HEADS),
                            ex[h0:h0 + NST, 2, :].unsqueeze(2).broadcast_to((NST, HEADS, HD)), ALU.mult))
                        pool.wait_ge(stated.sem, stated.now(t, c + 1))

                    def out_rstd(t, c):
                        pool.wait_ge(o_steps.sem, o_steps.now(t, OSTEPS * (c + 1)))
                        for n, (dst, a, b, op) in enumerate((
                                (octok[:], yexp[:, c:c + 1], c_out[:], ALU.mult), (ovar[:], omv[:, c % 2, 1:2], octok[:], ALU.mult),
                                (ovar[:], ovar[:], octok[:], ALU.mult), (ovar[:], ovar[:], eps_c[:, 0:1], ALU.add),
                                (orstd[:], ovar[:], neg_half[:, 0:1], ALU.pow), (oscale[:], orstd[:], octok[:], ALU.mult),
                                (ovar[:], omv[:, c % 2, 0:1], neg_one[:, 0:1], ALU.mult),
                                (obias[:], ovar[:], oscale[:], ALU.mult))):
                            oscale_steps.inc(nc.gpsimd.tensor_tensor(dst, a, b, op))
                            pool.wait_ge(oscale_steps.sem, oscale_steps.now(t, 8 * c + n + 1))

                    def add_residual(t, c):
                        pool.wait_ge(normalised.sem, normalised.now(t, c + 1))
                        pool.wait_ge(ures_loaded.sem, ures_loaded.now(t, c + 1))
                        x1_ready.inc(nc.gpsimd.tensor_tensor(x1[:, c % 2, :], x1[:, c % 2, :], ures[:], ALU.add))

                    def body(t, half, row, more):
                        weights(t, half, 0)
                        decay_state(t, half, row, 0, (xw_ready.sem, xw_ready.now(t, 1)))
                        z_gate(t, 0)
                        segments(t, half, 1)
                        z_gate(t, 1)
                        to_half(row, half, 1)
                        weights(t, half, 1)
                        z_gate(t, 2)
                        segments(t, half, 2)
                        decay_state(t, half, row, 1, (seg_ready.sem, seg_ready.now(t, 3)))
                        z_gate(t, 3)
                        weights(t, half, 2)
                        to_half(row, half, 2)
                        decay_state(t, half, row, 2, (as_half.sem, as_half.now(t, 3)))
                        segments(t, half, 3)
                        out_rstd(t, 0)
                        add_residual(t, 0)
                        weights(t, half, 3)
                        to_half(row, half, 3)
                        if more:
                            front_rstd(t + 2)
                        decay_state(t, half, row, 3, (as_half.sem, as_half.now(t, 4)))
                        out_rstd(t, 1)
                        add_residual(t, 1)
                        to_half(row, half, 4)
                        out_rstd(t, 2)
                        add_residual(t, 2)
                        if more:
                            segments(t + 1, 1 - half, 0)
                        out_rstd(t, 3)
                        if more:
                            to_half(*following(row, half), 0)
                        add_residual(t, 3)

                    nc.gpsimd.memset(ident[:], 0.0).then_inc(s_fill, 1)
                    nc.gpsimd.memset(causal[:], 1.0).then_inc(s_fill, 1)
                    nc.gpsimd.memset(below[:], 1.0).then_inc(s_fill, 1)
                    nc.gpsimd.memset(ones[:], 1.0).then_inc(s_fill, 1)
                    nc.gpsimd.memset(neg_half[:], -0.5).then_inc(s_fill, 1)
                    nc.gpsimd.memset(eps_c[:], EPS).then_inc(s_fill, 1)
                    nc.gpsimd.memset(neg_one[:], -1.0).then_inc(s_fill, 1)
                    nc.gpsimd.memset(xs_c[:], XS).then_inc(s_fill, 1)
                    nc.gpsimd.memset(zero_c[:], 0.0).then_inc(s_fill, 1)
                    pool.wait_ge(s_fill, 9)
                    nc.gpsimd.affine_select(out=ident[:], in_=ident[:], compare_op=ALU.not_equal, fill=1.0,
                                            base=0, pattern=[[-1, P]], channel_multiplier=1).then_inc(s_const, 1)
                    nc.gpsimd.affine_select(out=causal[:], in_=causal[:], compare_op=ALU.is_ge, fill=0.0,
                                            base=0, pattern=[[1, P]], channel_multiplier=-1).then_inc(s_const, 1)
                    nc.gpsimd.affine_select(out=below[:], in_=below[:], compare_op=ALU.is_gt, fill=0.0,
                                            base=0, pattern=[[-1, P]], channel_multiplier=1).then_inc(s_const, 1)
                    pool.wait_ge(s_const, 3)
                    front_rstd(0)
                    pool.wait_ge(s_big, KC + 3)
                    nc.gpsimd.partition_all_reduce(big[:], lowest[:], P, RMAX).then_inc(s_all, 1)
                    to_half(0, 0, 0)
                    segments(0, 0, 0)
                    front_rstd(1)
                    iterations(pool, body)

                @block.scalar
                def _(act):
                    yt_ready.start(act)
                    o_read.start(act)

                    def normalise_input(i, s, more=True):
                        if s == 0:
                            act.wait_ge(rstd_steps.sem, rstd_steps.now(i, 5))
                        norm_steps.inc(nc.scalar.activation(ut[:, s, :], ut[:, s, :], ACT.Identity,
                                                            bias=shift[:, s:s + 1], scale=rstd[:, s:s + 1]))
                        act.wait_ge(norm_steps.sem, norm_steps.now(i, 2 * s + 1))
                        if s >= 2:
                            act.wait_ge(filled.sem, use_of_front(i, f"T{s - 2}", more) + 1)
                        norm_steps.inc(nc.scalar.activation(xsplit[:, s % 2, 0, :], ut[:, s, :], ACT.Copy))

                    def input_transposed(t, s, more=True):
                        act.wait_ge(filled.sem, use(t, f"T{s}", more) + 1)
                        freed.inc(nc.scalar.activation(
                            xt[:, :, :, s * P:(s + 1) * P],
                            front_bank(t, f"T{s}", more)[:].bitcast(F16).rearrange("p (n k t) -> p n k t", n=2, k=KC), ACT.Copy))

                    def conv_input(t, f, p):
                        i = t + 1
                        slot = f % 2
                        if f >= 2:
                            act.wait_ge(conv_steps.sem, conv_steps.now(i, CSTEPS * (f - 1)))
                        elif not (isinstance(t, int) and t < 0):
                            act.wait_ge(conv_steps.sem, conv_steps.now(i, 0))
                        cin_steps.inc(nc.scalar.activation(cin[:, slot, 0:HALO], zero_c[:, 0:HALO] if p == 0
                                                           else halo[:, f, :], ACT.Copy))
                        act.wait_ge(filled.sem, use(t, f"X{f}") + 1)
                        freed.inc(nc.scalar.activation(cin[:, slot, HALO:], front_bank(t, f"X{f}")[:], ACT.Identity,
                                                       scale=c_in[:]))
                        act.wait_ge(cin_steps.sem, cin_steps.now(i, 2 * f + 1))
                        act.wait_ge(freed.sem, use(t, f"X{f}") + 1)
                        cin_steps.inc(nc.scalar.activation(halo[:, f, :], cin[:, slot, TILE:TILE + HALO], ACT.Copy))
                        if f >= 2 or not (isinstance(t, int) and t < 0):
                            act.wait_ge(xs_ready.sem, xs_ready.now(i, max(f - 1, 0)))
                        conv_first.inc(nc.scalar.activation(cacc[:, slot, :], cin[:, slot, 0:TILE], ACT.Identity,
                                                            bias=conv_b_sb[:, f:f + 1], scale=conv_w_sb[:, f, 0:1]))

                    def conv_tanh(i, f):
                        act.wait_ge(conv_steps.sem, conv_steps.now(i, CSTEPS * (f + 1)))
                        act.wait_ge(xs_ready.sem, xs_ready.now(i, f))
                        ctanh_ready.inc(nc.scalar.activation(ctanh[:], cacc[:, f % 2, :], ACT.Tanh, scale=0.5))

                    def dt_input(t):
                        act.wait_ge(filled.sem, use(t, "dt") + 1)
                        freed.inc(nc.scalar.activation(
                            dtr[:], front_bank(t, "dt")[:, 0:SUB * HEADS].rearrange("p (s h) -> p s h", s=SUB),
                            ACT.Identity, scale=c_in[:]))

                    def dt_exponential(i):
                        act.wait_ge(dt_steps.sem, dt_steps.now(i, 3))
                        dt_exp.inc(nc.scalar.activation(dte[:], dtz[:], ACT.Exp, scale=-1.0))

                    def z_input(t, c, more):
                        act.wait_ge(filled.sem, use(t, f"z{c}", more) + 1)
                        freed.inc(nc.scalar.activation(zs[:, c, :], bank_of(f"z{c}", more)[:], ACT.Copy))

                    def z_tanh_half(t, c, more):
                        act.wait_ge(freed.sem, use(t, f"z{c}", more) + 1)
                        act.wait_ge(zs_ready.sem, zs_ready.now(t, c))
                        z_tanh.inc(nc.scalar.activation(ztanh[:], zs[:, c, :], ACT.Tanh, scale=c_in_half[:]))
                        act.wait_ge(z_tanh.sem, z_tanh.now(t, 2 * c + 1))
                        z_tanh.inc(nc.scalar.activation(ztanh[:], ztanh[:], ACT.Identity, bias=ones[:, 0:1]))

                    def decoded(t, k, more):
                        cols = bass.ds((t * TILE_UNITS + k) * UNIT, UNIT)
                        for n in range(2):
                            name = f"D{k}" + "'" * n
                            rows = slice(n * NST, (n + 1) * NST)
                            act.wait_ge(filled.sem, use(t, name, more) + 1)
                            nc.scalar.activation(ffn_hi[rows, cols], bank_of(name, more)[0:NST, 0:UNIT], ACT.Copy)
                            freed.inc(nc.scalar.activation(ffn_lo[rows, cols], bank_of(name, more)[NST:P, 0:UNIT],
                                                           ACT.Copy))

                    def small(t, c):
                        act.wait_ge(xtok_done.sem, xtok_done.now(t, c + 1))
                        xtok_ready.inc(nc.scalar.activation(xtok[:], banks[2][:], ACT.Copy))
                        act.wait_ge(small_done.sem, small_done.now(t, c + 1))
                        sums_ready.inc(nc.scalar.activation(
                            ex[:], banks[3][:, 192:216].rearrange("p (k h) -> p k h", k=3), ACT.Exp))
                        sums_ready.inc(nc.scalar.activation(bt[:], banks[3][:, 128:192], ACT.Copy))

                    def decays(t, c):
                        act.wait_ge(seg_done.sem, seg_done.now(t, c + 1))
                        for n in range(2):
                            decay_ready.inc(nc.scalar.activation(
                                decay[:, 4 * n:4 * n + 4, :], banks[4 + n][:].rearrange("p (h t) -> p h t", h=4), ACT.Exp))

                    def y_transposed(t, c):
                        act.wait_ge(yt_done.sem, yt_done.now(t, c + 1))
                        yt_ready.inc(nc.scalar.activation(
                            yt[:], banks[4][:].bitcast(F16).rearrange("p (n k t) -> p n k t", n=2, k=KC), ACT.Copy))

                    def out_projected(t, c):
                        act.wait_ge(o_done.sem, o_done.now(t, c + 1))
                        g = x1_stored[c % 2]
                        act.wait_ge(g.sem, g.prev(t, SUB // 2 + c // 2))
                        o_read.inc(nc.scalar.activation(x1[:, c % 2, :], banks[5][:], ACT.Copy))

                    def normalise(t, c):
                        act.wait_ge(oscale_steps.sem, oscale_steps.now(t, 8 * (c + 1)))
                        normalised.inc(nc.scalar.activation(x1[:, c % 2, :], x1[:, c % 2, :], ACT.Identity, bias=obias[:], scale=oscale[:]))

                    def body(t, half, row, more):
                        i = t + 1
                        z_input(t, 0, more)
                        z_input(t, 1, more)
                        small(t, 0)
                        z_tanh_half(t, 0, more)
                        decays(t, 0)
                        z_input(t, 2, more)
                        z_tanh_half(t, 1, more)
                        z_input(t, 3, more)
                        normalise_input(i, 0, more)
                        normalise_input(i, 1, more)
                        small(t, 1)
                        decays(t, 1)
                        z_tanh_half(t, 2, more)
                        decoded(t, 0, more)
                        y_transposed(t, 0)
                        input_transposed(t, 0, more)
                        input_transposed(t, 1, more)
                        z_tanh_half(t, 3, more)
                        normalise_input(i, 2, more)
                        normalise_input(i, 3, more)
                        out_projected(t, 0)
                        small(t, 2)
                        decays(t, 2)
                        decoded(t, 1, more)
                        input_transposed(t, 2, more)
                        input_transposed(t, 3, more)
                        y_transposed(t, 1)
                        if more:
                            conv_input(t, 0, 1 - half)
                        out_projected(t, 1)
                        small(t, 3)
                        decays(t, 3)
                        normalise(t, 0)
                        if more:
                            conv_tanh(i, 0)
                            conv_input(t, 1, 1 - half)
                            conv_input(t, 2, 1 - half)
                        y_transposed(t, 2)
                        decoded(t, 2, more)
                        if more:
                            conv_tanh(i, 1)
                            conv_input(t, 3, 1 - half)
                            conv_tanh(i, 2)
                        normalise(t, 1)
                        out_projected(t, 2)
                        if more:
                            conv_input(t, 4, 1 - half)
                            dt_input(t)
                        y_transposed(t, 3)
                        if more:
                            dt_exponential(i)
                        decoded(t, 3, more)
                        normalise(t, 2)
                        if more:
                            conv_tanh(i, 3)
                        out_projected(t, 3)
                        decoded(t, 4, more)
                        if more:
                            conv_tanh(i, 4)
                        normalise(t, 3)

                    def vector_row(v, n):
                        return v.rearrange("(a n) -> a n", a=1).broadcast_to((P, n))

                    def high_half(n):
                        src, hi, _, which = PIECES[n]
                        act.wait_ge(s_scale, 1)
                        nc.scalar.activation(hi, src, ACT.Copy, scale=wscale[:, which:which + 1]).then_inc(s_hi, 1)

                    act.dma_start(lut_sb[:], vector_row(lut, CODES)).then_inc(s_small, 16)
                    act.dma_start(dt_bias_sb[:], vector_row(dt_bias, HEADS)).then_inc(s_small, 16)
                    act.dma_start(a_sb[:], vector_row(a_log, HEADS)).then_inc(s_small, 16)
                    act.dma_start(d_sb[:], vector_row(d_param, HEADS)).then_inc(s_small, 16)
                    act.dma_start(conv_w_sb[:], conv_w.rearrange("(f p) k -> p f k", p=P)).then_inc(s_small, 16)
                    act.dma_start(conv_b_sb[:], conv_b.rearrange("(f p) -> p f", p=P),
                                  allow_slow_non_contiguous=True).then_inc(s_small, 16)
                    normalise_input(0, 0)
                    normalise_input(0, 1)
                    for s in range(SUB):
                        input_transposed(-1, s)
                        if s + 2 < SUB:
                            normalise_input(0, s + 2)
                    act.wait_ge(s_small, 96)
                    nc.scalar.activation(a_sb[:], a_sb[:], ACT.Exp).then_inc(s_alog, 1)
                    for n in range(3):
                        high_half(n)
                    dt_input(-1)
                    high_half(3)
                    for f in range(FB):
                        conv_input(-1, f, 0)
                        if f >= 1:
                            conv_tanh(0, f - 1)
                        if f == 1:
                            dt_exponential(0)
                    conv_tanh(0, FB - 1)
                    iterations(act, body)

                @block.tensor
                def _(pe):
                    masks_used.start(pe)

                    def take(n):
                        if not (isinstance(n, int) and n < 2):
                            pe.wait_ge(freed.sem, n - 1)

                    def split_products(out_ap, pairs):
                        for k, (lhs, rhs) in enumerate(pairs):
                            last = nc.tensor.matmul(out_ap, lhs, rhs, start=(k == 0), stop=(k == len(pairs) - 1))
                        return last

                    def input_transpose(t, s, more=True):
                        take(use(t, f"T{s}", more))
                        pe.wait_ge(split_ready.sem, split_ready.now(t + 1, s + 1))
                        b = front_bank(t, f"T{s}", more)[:].bitcast(F16).rearrange("p (n k t) -> p n k t", n=2, k=KC)
                        for n in range(2):
                            for k in range(KC):
                                last = nc.tensor.transpose(b[:, n, k, :], xsplit[:, s % 2, n, k * P:(k + 1) * P],
                                                           ident_h[:])
                        filled.inc(last)

                    def project_conv(t, f):
                        take(use(t, f"X{f}"))
                        if f == 0:
                            pe.wait_ge(freed.sem, use(t, f"T{SUB - 1}") + 1)
                        cols = slice(X0 + f * P, X0 + (f + 1) * P)
                        filled.inc(split_products(front_bank(t, f"X{f}")[:], [
                            (w[:, k, cols], xt[:, n, k, :]) for k in range(KC)
                            for w, n in ((win_hi, 0), (win_hi, 1), (win_lo, 0))]))

                    def project_dt(t):
                        take(use(t, "dt"))
                        b = front_bank(t, "dt")
                        for c in range(SUB):
                            tok = slice(c * P, (c + 1) * P)
                            last = split_products(b[:, c * HEADS:(c + 1) * HEADS], [
                                (xt[:, n, k, tok], w[:, k, DT0:D_IN]) for k in range(KC)
                                for w, n in ((win_hi, 0), (win_lo, 0), (win_hi, 1))])
                        filled.inc(last)

                    def project_z(t, c, more):
                        take(use(t, f"z{c}", more))
                        tok = slice(c * P, (c + 1) * P)
                        filled.inc(split_products(bank_of(f"z{c}", more)[:], [
                            (xt[:, n, k, tok], w[:, k, 0:D]) for k in range(KC)
                            for w, n in ((win_hi, 0), (win_lo, 0), (win_hi, 1))]))

                    def decode(t, k, more):
                        for n in range(2):
                            b = bank_of(f"D{k}" + "'" * n, more)[:, 0:UNIT]
                            take(use(t, f"D{k}" + "'" * n, more))
                            for q in range(PAIRS):
                                if q % GROUP == 0:
                                    pe.wait_ge(masks_ready.sem, masks_ready.now(
                                        t, k * GROUPS + n * (GROUPS // 2) + q // GROUP + 1))
                                last = nc.tensor.matmul(b, diag[:, q].rearrange("p n m -> p (n m)"), mask[:, n, q, :],
                                                        start=(q == 0), stop=(q == PAIRS - 1))
                                if q == GROUP - 1:
                                    masks_used.inc(last)
                            filled.inc(last)

                    def prepare(t, half, c):
                        tok = slice(c * P, (c + 1) * P)
                        h = slice(half * NST, (half + 1) * NST)
                        if c == 0:
                            pe.wait_ge(xs_ready.sem, xs_ready.now(t, FB + 1))
                        pe.wait_ge(state_ready.sem, state_ready.prev(t, SUB + c))
                        for k in range(KC):
                            last = nc.tensor.transpose(banks[2][:, k * P:(k + 1) * P], xs[:, half, k, tok], ident[:])
                        xtok_done.inc(last)
                        pe.wait_ge(gram_ready.sem, gram_ready.prev(t, SUB + c))
                        nc.tensor.matmul(banks[3][:, 0:P], bs[h, tok], cs[h, tok], start=True, stop=True)
                        nc.tensor.transpose(banks[3][:, 128:192], bs[h, tok], ident[h, h])
                        pe.wait_ge(dt_steps.sem, dt_steps.now(t, 17))
                        for n, sums in enumerate((causal, below, ones)):
                            last = nc.tensor.matmul(banks[3][:, 192 + n * HEADS:192 + (n + 1) * HEADS], sums[:],
                                                    da[:, half, c, :], start=True, stop=True)
                        small_done.inc(last)

                    def segment_sums(t, c):
                        pe.wait_ge(seg_ready.sem, seg_ready.now(t, c + 1))
                        pe.wait_ge(yt_ready.sem, yt_ready.prev(t, SUB + max(c - 1, 0)))
                        pe.wait_ge(o_read.sem, o_read.prev(t, SUB + max(c - 1, 0)))
                        for n in range(2):
                            last = nc.tensor.matmul(banks[4 + n][:], below[:],
                                                    seg[:, 4 * n:4 * n + 4, :].rearrange("p h t -> p (h t)"),
                                                    start=True, stop=True)
                        seg_done.inc(last)

                    def scan(t, half, row, c):
                        tok = slice(c * P, (c + 1) * P)
                        h = slice(half * NST, (half + 1) * NST)
                        if half == 0 and c == 0:
                            pe.wait_ge(state_cleared.sem, state_cleared.now(row, 1))
                        pe.wait_ge(state_ready.sem, state_ready.prev(t, SUB + c))
                        yi_done.inc(nc.tensor.matmul(banks[7][:], cs[h, tok], state[h, :], start=True, stop=True))
                        pe.wait_ge(xdt_ready.sem, xdt_ready.now(t, c + 1))
                        pe.wait_ge(mt_ready.sem, mt_ready.now(t, c + 1))
                        for n in range(HEADS):
                            last = nc.tensor.matmul(banks[6][:, n * HD:(n + 1) * HD], decay[:, n, :],
                                                    xdt[:, n * HD:(n + 1) * HD], start=True, stop=True)
                        y_done.inc(last)
                        pe.wait_ge(sums_ready.sem, sums_ready.now(t, 2 * c + 2))
                        pe.wait_ge(xw_ready.sem, xw_ready.now(t, c + 1))
                        s_done.inc(nc.tensor.matmul(banks[2][h, :], bt[:], xtok[:], start=True, stop=True))

                    def transpose_y(t, c):
                        pe.wait_ge(y_steps.sem, y_steps.now(t, YSTEPS * (c + 1)))
                        pe.wait_ge(decay_ready.sem, decay_ready.now(t, 2 * min(c + 2, SUB)))
                        b = banks[4][:].bitcast(F16).rearrange("p (n k t) -> p n k t", n=2, k=KC)
                        for n in range(2):
                            for k in range(KC):
                                last = nc.tensor.transpose(b[:, n, k, :], ysplit[:, n, k * P:(k + 1) * P], ident_h[:])
                        yt_done.inc(last)

                    def project_out(t, c):
                        pe.wait_ge(yt_ready.sem, yt_ready.now(t, c + 1))
                        pe.wait_ge(o_read.sem, o_read.prev(t, SUB + c))
                        o_done.inc(split_products(banks[5][:], [
                            (yt[:, n, k, :], w[:, k, :]) for k in range(KC)
                            for n, w in ((0, wout_hi), (0, wout_lo), (1, wout_hi))]))

                    def body(t, half, row, more):
                        project_z(t, 0, more)
                        project_z(t, 1, more)
                        prepare(t, half, 0)
                        segment_sums(t, 0)
                        project_z(t, 2, more)
                        scan(t, half, row, 0)
                        project_z(t, 3, more)
                        prepare(t, half, 1)
                        segment_sums(t, 1)
                        pe.wait_ge(s_diag, 2 * PAIRS)
                        pe.wait_ge(s_lo, len(PIECES))
                        decode(t, 0, more)
                        transpose_y(t, 0)
                        input_transpose(t, 0, more)
                        input_transpose(t, 1, more)
                        scan(t, half, row, 1)
                        project_out(t, 0)
                        prepare(t, half, 2)
                        segment_sums(t, 2)
                        decode(t, 1, more)
                        input_transpose(t, 2, more)
                        input_transpose(t, 3, more)
                        transpose_y(t, 1)
                        scan(t, half, row, 2)
                        if more:
                            project_conv(t, 0)
                        project_out(t, 1)
                        prepare(t, half, 3)
                        segment_sums(t, 3)
                        if more:
                            project_conv(t, 1)
                            project_conv(t, 2)
                        transpose_y(t, 2)
                        decode(t, 2, more)
                        if more:
                            project_conv(t, 3)
                        scan(t, half, row, 3)
                        project_out(t, 2)
                        if more:
                            project_conv(t, 4)
                            project_dt(t)
                        decode(t, 3, more)
                        transpose_y(t, 3)
                        project_out(t, 3)
                        decode(t, 4, more)

                    pe.wait_ge(s_ident, 1)
                    for s in range(SUB):
                        input_transpose(-1, s)
                    pe.wait_ge(s_lo, 2)
                    project_dt(-1)
                    for f in range(FB):
                        project_conv(-1, f)
                    pe.wait_ge(s_lo, 3)
                    iterations(pe, body)

                @block.vector
                def _(dve):
                    for g in (gram_ready, state_ready, y_steps):
                        g.start(dve)

                    def chain(sig, t, k, ins):
                        sig.inc(ins)
                        dve.wait_ge(sig.sem, sig.now(t, k))

                    def one_mask(row, half, k, j, more=True):
                        t = row * HALVES + half
                        n, q = divmod(j, PAIRS)
                        if q == 0:
                            dve.wait_ge(masks_used.sem, masks_used.prev(t, (TILE_UNITS + k - 1) * 2 + n + 1))
                        elif q == GROUP and k > 0:
                            dve.wait_ge(filled.sem, use(t, f"D{k - 1}" + "'" * n, more) + 1)
                        elif q == GROUP:
                            dve.wait_ge(filled.sem, use(t - 1, f"D{TILE_UNITS - 1}" + "'" * n) + 1)
                        if j == 0:
                            dve.wait_ge(as_half.sem, as_half.now(t, k + 1))
                            chain(lowered, t, k + 1, nc.vector.tensor_scalar(
                                codes_h[NST:P], codes_h[NST:P], -1.0, None, ALU.add))
                        ins = nc.vector.tensor_scalar(mask[:, n, q, :], codes_h[:, n, :], float(2 * q), None,
                                                      ALU.is_equal)
                        if q % GROUP == GROUP - 1:
                            masks_ready.inc(ins)

                    def masks(row, half, k, more=True, first=0):
                        for j in range(first, 2 * PAIRS):
                            one_mask(row, half, k, j, more)

                    def ln_stats(i):
                        dve.wait_ge(u_loaded.sem, u_loaded.now(i, 1))
                        for s in range(SUB):
                            ln_steps.inc(nc.vector.bn_stats(stats[:, s, :], ut[:, s, :]))
                        for s in range(SUB):
                            wait_apart(dve, ln_steps.sem, ln_steps.now(i, s + 1), dve_passed)
                            ln_steps.inc(nc.vector.bn_aggr(mv[:, s, :], stats[:, s, :]))

                    def ln_split(i, s):
                        dve.wait_ge(norm_steps.sem, norm_steps.now(i, 2 * (s + 1)))
                        split_ready.inc(nc.vector.tensor_sub(xsplit[:, s % 2, 1, :], ut[:, s, :], xsplit[:, s % 2, 0, :]))

                    def conv(i, f):
                        slot = f % 2
                        dve.wait_ge(conv_first.sem, conv_first.now(i, f + 1))
                        for k in range(1, TAPS):
                            chain(conv_steps, i, CSTEPS * f + k, nc.vector.scalar_tensor_tensor(
                                cacc[:, slot, :], cin[:, slot, k:k + TILE], conv_w_sb[:, f, k:k + 1],
                                cacc[:, slot, :], ALU.mult, ALU.add))

                    def conv_silu(i, p, f):
                        dve.wait_ge(ctanh_ready.sem, ctanh_ready.now(i, f + 1))
                        if f < KC:
                            xs_ready.inc(nc.vector.scalar_tensor_tensor(
                                xs[:, p, f, :], ctanh[:], 1.0, cacc[:, f % 2, :], ALU.add, ALU.mult))
                        else:
                            h = slice(p * NST, (p + 1) * NST)
                            for dst, lo in ((bs, 0), (cs, NST)):
                                xs_ready.inc(nc.vector.scalar_tensor_tensor(
                                    dst[h, :], ctanh[lo:lo + NST, :], 1.0, cacc[lo:lo + NST, f % 2, :],
                                    ALU.add, ALU.mult))

                    def dt_input(i):
                        dve.wait_ge(freed.sem, use_of_front(i, "dt") + 1)
                        chain(dt_steps, i, 1, nc.vector.tensor_tensor(
                            dtx[:], dtr[:], dt_bias_sb[:].unsqueeze(1).broadcast_to((P, SUB, HEADS)), ALU.add))
                        chain(dt_steps, i, 2, nc.vector.tensor_scalar(dtp[:], dtx[:], -1.0, None, ALU.mult))
                        chain(dt_steps, i, 3, nc.vector.tensor_tensor(dtz[:], dtx[:], dtp[:], ALU.max))

                    def time_steps(i, p, beside=lambda j: None):
                        def t_step(k, ins):
                            dt_steps.inc(ins)
                            beside(k - 4)
                            dve.wait_ge(dt_steps.sem, dt_steps.now(i, k))

                        dve.wait_ge(dt_exp.sem, dt_exp.now(i, 1))
                        t_step(4, nc.vector.tensor_scalar(dtp[:], dte[:], 2.0, None, ALU.add))
                        t_step(5, nc.vector.reciprocal(dtp[:], dtp[:]))
                        t_step(6, nc.vector.tensor_tensor(dtz[:], dte[:], dtp[:], ALU.mult))
                        t_step(7, nc.vector.tensor_tensor(dtz2[:], dtz[:], dtz[:], ALU.mult))
                        t_step(8, nc.vector.tensor_scalar(dtp[:], dtz2[:], 2.0 / 15, None, ALU.mult))
                        for n, k in enumerate((13, 11, 9, 7, 5, 3)):
                            t_step(9 + n, nc.vector.scalar_tensor_tensor(
                                dtp[:], dtp[:], 2.0 / k, dtz2[:], ALU.add, ALU.mult))
                        t_step(15, nc.vector.scalar_tensor_tensor(
                            dtp[:], dtp[:], 2.0, dtz[:], ALU.add, ALU.mult))
                        t_step(16, nc.vector.scalar_tensor_tensor(
                            dt[:], dtx[:], 0.0, dtp[:], ALU.max, ALU.add))
                        t_step(17, nc.vector.tensor_tensor(
                            da[:, p], dt[:], a_sb[:].unsqueeze(1).broadcast_to((P, SUB, HEADS)), ALU.mult))
                        t_step(18, nc.vector.tensor_scalar(dt4[:, p], dt[:], 0.25, None, ALU.mult))

                    def weigh(t, half, c):
                        dve.wait_ge(sums_ready.sem, sums_ready.now(t, 2 * c + 2))
                        chain(gram_ready, t, c + 1, nc.vector.tensor_tensor(gsb[:], banks[3][:, 0:P], causal[:], ALU.mult))

                    def decayed(t, c):
                        dve.wait_ge(decay_ready.sem, decay_ready.now(t, 2 * c + 2))
                        mt_ready.inc(nc.vector.tensor_tensor(
                            decay[:], decay[:], gsb[:].unsqueeze(1).broadcast_to((P, HEADS, P)), ALU.mult))

                    def outputs(t, half, row, c, unit, more=True, done=0):
                        def beside(j):
                            if done + j < 2 * PAIRS:
                                one_mask(row, half, unit, done + j, more)

                        def y_step(k, ins):
                            y_steps.inc(ins)
                            beside(0 if k == 1 else k)
                            dve.wait_ge(y_steps.sem, y_steps.now(t, YSTEPS * c + k))

                        h = slice(half * NST, (half + 1) * NST)
                        dve.wait_ge(yi_done.sem, yi_done.now(t, c + 1))
                        dve.wait_ge(yt_done.sem, yt_done.now(t, c))
                        y_step(1, nc.vector.tensor_tensor(
                            y[:].rearrange("p (h d) -> p h d", h=HEADS),
                            banks[7][:].rearrange("p (h d) -> p h d", h=HEADS),
                            ex[:, 0, :].unsqueeze(2).broadcast_to((P, HEADS, HD)), ALU.mult))
                        dve.wait_ge(s_done.sem, s_done.now(t, c + 1))
                        dve.wait_ge(stated.sem, stated.now(t, c + 1))
                        to = slice(NST, P) if half == 0 and c == SUB - 1 else h
                        state_ready.inc(nc.vector.tensor_tensor(state[to, :], state[h, :], banks[2][h, :], ALU.add))
                        beside(1)
                        dve.wait_ge(y_done.sem, y_done.now(t, c + 1))
                        y_step(2, nc.vector.tensor_tensor(y[:], y[:], banks[6][:], ALU.add))
                        dve.wait_ge(xd_ready.sem, xd_ready.now(t, c + 1))
                        y_step(3, nc.vector.tensor_tensor(y[:], y[:], xd[:], ALU.add))
                        dve.wait_ge(zs_ready.sem, zs_ready.now(t, c + 1))
                        y_step(4, nc.vector.tensor_tensor(y[:], y[:], zs[:, c, :], ALU.mult))
                        y_step(5, nc.vector.tensor_reduce(ymax[:], y[:], AX_X, ALU.max,
                                                                          apply_absolute_value=True))
                        y_step(6, nc.vector.tensor_scalar(ymax[:], ymax[:], TINY, None, ALU.max))
                        y_step(7, nc.vector.tensor_scalar(
                            yexp[:, c:c + 1].bitcast(I32), ymax[:].bitcast(I32), 0x7F800000, None, ALU.bitwise_and))
                        y_step(8, nc.vector.reciprocal(yq[:], yexp[:, c:c + 1]))
                        y_step(9, nc.vector.tensor_scalar(yq[:], yq[:], WS, None, ALU.mult))
                        y_step(10, nc.vector.tensor_scalar(ysplit[:, 0, :], y[:], yq[:], None, ALU.mult))
                        y_step(11, nc.vector.scalar_tensor_tensor(
                            ysplit[:, 1, :], y[:], yq[:], ysplit[:, 0, :], ALU.mult, ALU.subtract))
                        masks(row, half, unit, more, first=done + YSTEPS + 1)

                    def out_stats(t, c):
                        n0 = OSTEPS * c
                        dve.wait_ge(o_read.sem, o_read.now(t, c + 1))
                        o_steps.inc(nc.vector.bn_stats(ostat[:], x1[:, c % 2, :]))
                        wait_apart(dve, o_steps.sem, o_steps.now(t, n0 + 1), dve_passed)
                        o_steps.inc(nc.vector.bn_aggr(omv[:, c % 2, :], ostat[:]))

                    def body(t, half, row, more):
                        i, p = t + 1, 1 - half
                        weigh(t, half, 0)
                        if half == 0:
                            state_cleared.inc(nc.vector.memset(state[0:NST, :], 0.0))
                        decayed(t, 0)
                        masks(row, half, 0)
                        outputs(t, half, row, 0, 0, done=2 * PAIRS)
                        ln_split(i, 0)
                        ln_split(i, 1)
                        weigh(t, half, 1)
                        decayed(t, 1)
                        outputs(t, half, row, 1, 1, more)
                        ln_split(i, 2)
                        ln_split(i, 3)
                        weigh(t, half, 2)
                        out_stats(t, 0)
                        decayed(t, 2)
                        outputs(t, half, row, 2, 2, more)
                        if more:
                            conv(i, 0)
                        weigh(t, half, 3)
                        decayed(t, 3)
                        if more:
                            ln_stats(i + 1)
                            conv_silu(i, p, 0)
                            conv(i, 1)
                            conv_silu(i, p, 1)
                            conv(i, 2)
                        out_stats(t, 1)
                        if more:
                            conv_silu(i, p, 2)
                        outputs(t, half, row, 3, 3, more)
                        if more:
                            dt_input(i)
                        out_stats(t, 2)
                        if more:
                            conv(i, 3)
                            time_steps(i, p, lambda j: one_mask(row, half, 4, j))
                            masks(row, half, 4, first=TSTEPS)
                        else:
                            masks(row, half, 4, more)
                        out_stats(t, 3)
                        if more:
                            conv_silu(i, p, 3)
                            conv(i, 4)
                            conv_silu(i, p, 4)
                    steps = [0]

                    def step(ins):
                        steps[0] += 1
                        ins.then_inc(s_step, 1)
                        dve.wait_ge(s_step, steps[0])

                    def low_half(n):
                        src, hi, lo, which = PIECES[n]
                        dve.wait_ge(s_hi, n + 1)
                        nc.vector.scalar_tensor_tensor(lo, src, wscale[:, which:which + 1], hi, ALU.mult,
                                                       ALU.subtract).then_inc(s_lo, 1)

                    dve.wait_ge(s_const, 3)
                    nc.vector.tensor_copy(ident_h[:], ident[:]).then_inc(s_ident, 1)
                    ln_stats(0)
                    for k in range(KC):
                        dve.wait_ge(s_win[k], 16)
                        nc.vector.tensor_reduce(win_max[:, k:k + 1], w_in_f[:, k, :], AX_X, ALU.max,
                                                apply_absolute_value=True).then_inc(s_big, 1)
                        ln_split(0, k)
                    dve.wait_ge(s_small, 96)
                    nc.vector.tensor_reduce(lowest[:, 2:3], lut_sb[:], AX_X, ALU.max,
                                            apply_absolute_value=True).then_inc(s_big, 1)
                    dve.wait_ge(s_wout, 16)
                    nc.vector.tensor_reduce(lowest[:, 1:2], w_out_f, AX_XY, ALU.max,
                                            apply_absolute_value=True).then_inc(s_big, 1)
                    dve.wait_ge(s_big, KC)
                    nc.vector.tensor_reduce(lowest[:, 0:1], win_max[:], AX_X, ALU.max).then_inc(s_big, 1)
                    dve.wait_ge(s_all, 1)
                    step(nc.vector.tensor_scalar(big[:], big[:], TINY, None, ALU.max))
                    step(nc.vector.tensor_scalar(expo[:].bitcast(I32), big[:].bitcast(I32), 0x7F800000, None,
                                                 ALU.bitwise_and))
                    step(nc.vector.reciprocal(wscale[:], expo[:]))
                    nc.vector.tensor_scalar(wscale[:], wscale[:], WS, None, ALU.mult).then_inc(s_scale, 1)
                    dve.wait_ge(s_scale, 1)
                    step(nc.vector.tensor_scalar(c_in[:], expo[:, 0:1], 1.0 / (XS * WS), None, ALU.mult))
                    step(nc.vector.tensor_scalar(c_in_half[:], c_in[:], 0.5, None, ALU.mult))
                    step(nc.vector.tensor_scalar(c_out[:], c_in[:], expo[:, 1:2], 0.25 / (WS * WS), ALU.mult, ALU.mult))
                    for n in range(3):
                        low_half(n)
                    dve.wait_ge(s_alog, 1)
                    step(nc.vector.tensor_scalar(a_sb[:], a_sb[:], -1.0, None, ALU.mult))
                    dt_input(0)
                    step(nc.vector.tensor_scalar(c_gate_half[:], expo[:, 2:3], 0.5 / (XS * WS), None, ALU.mult))
                    step(nc.vector.tensor_scalar(c_down[:], expo[:, 2:3], expo[:, 2:3], 32.0 / WS, ALU.mult, ALU.mult))
                    step(nc.vector.tensor_scalar(c_down[:], c_down[:], expo[:, 2:3], None, ALU.mult))
                    step(nc.vector.tensor_scalar(lut_s[:], lut_sb[:], wscale[:, 2:3], None, ALU.mult))
                    step(nc.vector.tensor_copy(lut_hi[:], lut_s[:]))
                    step(nc.vector.tensor_copy(lut_hi32[:], lut_hi[:]))
                    step(nc.vector.tensor_sub(lut_lo32[:], lut_s[:], lut_hi32[:]))
                    setup = sem("decoding_set_up")
                    nc.vector.tensor_tensor(fold[:], ident[:, 0:NST], ident[:, NST:P], ALU.add).then_inc(setup, 1)
                    for b in range(2):
                        rows = slice(b * NST, (b + 1) * NST)
                        for n, v in enumerate((lut_hi32, lut_lo32)):
                            nc.vector.tensor_copy(lut_sel[rows, n, :], v[rows, :].rearrange(
                                "p (q b) -> p q b", b=2)[:, :, b]).then_inc(setup, 1)
                    dve.wait_ge(setup, 1 + 2 * 2)
                    for q in range(PAIRS):
                        for n in range(2):
                            nc.vector.tensor_scalar(diag[:, q, n, :], fold[:], lut_sel[:, n, q:q + 1], None,
                                                    ALU.mult).then_inc(s_diag, 1)
                    low_half(3)
                    for f in range(FB):
                        if f >= 1:
                            conv_silu(0, 0, f - 1)
                        conv(0, f)
                        if f == 1:
                            time_steps(0, 0)
                    conv_silu(0, 0, FB - 1)
                    ln_stats(1)
                    iterations(dve, body)

        with ExitStack() as stage:
            def st(name, shape, dt=F32):
                return stage.enter_context(nc.sbuf_tensor(name, shape, dt))
            xf = [st(f"xf{i}", [P, SUB, D]) for i in range(2)]
            stats = st("fstats", [P, SUB, 6])
            mv = st("fmv", [P, SUB, 2])
            vare = st("fvare", [P, SUB])
            rstd = st("frstd", [P, SUB])
            xn = st("fxn", [P, D])
            xsplit = st("fxsplit", [P, SUB, 2, D], F16)
            xts = [xt, st("xt_odd", [P, 2, KC, TILE], F16)]
            gtanh = st("gtanh", [P, 2, TILE])
            gsilu = st("gsilu", [P, 2, TILE])
            hf = st("hf", [P, 2, TILE])
            h_hi = st("h_hi", [P, MB, TILE], F16)
            h_lo = st("h_lo", [P, MB, TILE], F16)
            dstat = st("dstat", [P, SUB, 6])
            dmv = st("dmv", [P, SUB, 2])
            dvar = st("dvar", [P, SUB])
            drstd = st("drstd", [P, SUB])
            dscale = st("dscale", [P, SUB])
            dn = st("dn", [P, 2, D])
            res = st("res", [P, 2, D])

            x_loaded = [Signal(sem(f"x1_loaded{i}"), 1, step=16) for i in range(2)]
            ln_steps = Signal(sem("f_ln_steps"), 3 * SUB)
            rstd_ready = Signal(sem("f_rstd_ready"), 1)
            split_steps = Signal(sem("f_split_steps"), 3 * SUB)
            xt_filled = Signal(sem("f_xt_transposed"), SUB)
            xt_ready = Signal(sem("f_xt_ready"), SUB)
            gate_done = Signal(sem("gate_done"), MB)
            up_done = Signal(sem("up_done"), MB)
            gtanh_ready = Signal(sem("gate_tanh_ready"), MB)
            gsilu_ready = Signal(sem("gate_silu_ready"), MB, credit=True)
            hf_ready = Signal(sem("h_ready"), MB, credit=True)
            hhi_ready = Signal(sem("h_hi_ready"), MB)
            hlo_ready = Signal(sem("h_lo_ready"), MB)
            down_done = Signal(sem("down_done"), SUB, credit=True)
            d_steps = Signal(sem("down_ln_steps"), SUB * 5)
            drstd_ready = Signal(sem("down_rstd_ready"), SUB)
            dn_ready = Signal(sem("down_normalised"), SUB, credit=True)
            res_ready = Signal(sem("output_ready"), SUB, credit=True)
            res_stored = [Signal(sem(f"output_stored{i}"), SUB // 2, step=16, credit=True) for i in range(2)]
            out_chunks = out.rearrange("(c p) d -> c p d", p=P)
            STATS_AT, SPLIT_AT, TRANSPOSE_AT = 2, 3, 5
            assert TRANSPOSE_AT + SUB <= MB

            def tiles(eng, body):
                with eng.Fori(0, TILES // 2 - 1) as pair:
                    for i in range(2):
                        body(pair * 2 + i, i, pair, True)
                for i in range(2):
                    body(TILES - 2 + i, i, TILES // 2 - 1, i == 0)

            with nc.Block() as block:
                @block.sync
                def _(sp):
                    for g in res_stored:
                        g.start(sp)
                    for i in range(2):
                        x_loaded[i].inc(sp.dma_start(xf[i][:], x1_tiles[i]))

                    def store_then_load(pair, more):
                        for i in range(2):
                            t = pair * 2 + i
                            for c in range(SUB):
                                sp.wait_ge(res_ready.sem, res_ready.now(t, c + 1))
                                res_stored[c % 2].inc(sp.dma_start(out_chunks[t * SUB + c], res[:, c % 2, :]))
                            if more:
                                x_loaded[i].inc(sp.dma_start(xf[i][:], x1_tiles[t + 2]))

                    with sp.Fori(0, TILES // 2 - 1) as pair:
                        store_then_load(pair, True)
                    store_then_load(TILES // 2 - 1, False)
                    for g in res_stored:
                        sp.wait_ge(g.sem, g.now(TILES - 1, SUB // 2))

                @block.gpsimd
                def _(pool):
                    res_ready.start(pool)

                    def body(t, i, pair, more):
                        if more:
                            pool.wait_ge(ln_steps.sem, ln_steps.now(t, 3 * SUB))
                            rstd_ready.inc(nc.gpsimd.tensor_tensor(rstd[:], vare[:], neg_half[:], ALU.pow))
                        pool.wait_ge(x_loaded[i].sem, x_loaded[i].now(pair, 1))
                        for c in range(SUB):
                            pool.wait_ge(d_steps.sem, d_steps.now(t, 5 * c + 4))
                            drstd_ready.inc(nc.gpsimd.tensor_tensor(drstd[:, c:c + 1], dvar[:, c:c + 1],
                                                                    neg_half[:, 0:1], ALU.pow))
                            pool.wait_ge(dn_ready.sem, dn_ready.now(t, c + 1))
                            g = res_stored[c % 2]
                            pool.wait_ge(g.sem, g.prev(t, SUB // 2) if c < 2 else g.now(t, c // 2))
                            res_ready.inc(nc.gpsimd.tensor_tensor(res[:, c % 2, :], dn[:, c % 2, :],
                                                                  xf[i][:, c, :], ALU.add))

                    tiles(pool, body)

                @block.scalar
                def _(act):
                    def body(t, i, pair, more):
                        def high(m):
                            w = MW[m]
                            act.wait_ge(hf_ready.sem, hf_ready.now(t, m + 1))
                            if m == 0:
                                act.wait_ge(down_done.sem, down_done.prev(t, SUB))
                            hhi_ready.inc(nc.scalar.activation(h_hi[0:w, m, :], hf[0:w, m % 2, :], ACT.Copy))

                        for m in range(MB):
                            w = MW[m]
                            act.wait_ge(gate_done.sem, gate_done.now(t, m + 1))
                            act.wait_ge(gsilu_ready.sem, gsilu_ready.prev(t, LAST_OF_SLOT[m]) if m < 2
                                        else gsilu_ready.now(t, m - 1))
                            gtanh_ready.inc(nc.scalar.activation(gtanh[0:w, m % 2, :], banks[2 + m % 2][0:w, :],
                                                                 ACT.Tanh, scale=c_gate_half[0:w, :]))
                            if m >= 1:
                                high(m - 1)
                            s = m - TRANSPOSE_AT - 1
                            if more and 0 <= s < SUB:
                                act.wait_ge(xt_filled.sem, xt_filled.now(t, s + 1))
                                xt_ready.inc(nc.scalar.activation(
                                    xts[1 - i][:, :, :, s * P:(s + 1) * P],
                                    banks[s % 2][:].bitcast(F16).rearrange("p (n k t) -> p n k t", n=2, k=KC), ACT.Copy))
                        high(MB - 1)

                    tiles(act, body)

                @block.tensor
                def _(pe):
                    down_done.start(pe)

                    def body(t, i, pair, more):
                        if not isinstance(t, int) or t > 0:
                            pe.wait_ge(xt_ready.sem, xt_ready.now(t, 0))
                        for m in range(MB):
                            w = MW[m]
                            for col0, base, done, free in ((GATE0, 2, gate_done, gsilu_ready), (UP0, 4, up_done, hf_ready)):
                                if m < 2:
                                    pe.wait_ge(free.sem, free.prev(t, LAST_OF_SLOT[m]))
                                else:
                                    pe.wait_ge(free.sem, free.now(t, m - 1))
                                bank = banks[base + m % 2][0:w, :]
                                for k in range(KC):
                                    c0 = col0 + k * INTER + m * P
                                    for n, (wt, half) in enumerate(((ffn_hi, 0), (ffn_hi, 1), (ffn_lo, 0))):
                                        last = nc.tensor.matmul(bank, wt[:, c0:c0 + w], xts[i][:, half, k, :],
                                                                start=(k == 0 and n == 0),
                                                                stop=(k == KC - 1 and n == 2))
                                done.inc(last)
                            s = m - TRANSPOSE_AT
                            if more and 0 <= s < SUB:
                                pe.wait_ge(split_steps.sem, split_steps.now(t, 3 * (s + 1)))
                                pe.wait_ge(xt_ready.sem, xt_ready.now(t, max(s - 1, 0)))
                                b = banks[s % 2][:].bitcast(F16).rearrange("p (n k t) -> p n k t", n=2, k=KC)
                                for n in range(2):
                                    for k in range(KC):
                                        last = nc.tensor.transpose(b[:, n, k, :], xsplit[:, s, n, k * P:(k + 1) * P],
                                                                   ident_h[:])
                                xt_filled.inc(last)
                        for c in range(SUB):
                            tok = slice(c * P, (c + 1) * P)
                            pe.wait_ge(dn_ready.sem, dn_ready.prev(t, SUB - 1 + c) if c < 2 else dn_ready.now(t, c - 1))
                            for m in range(MB):
                                w = MW[m]
                                if c == 0:
                                    pe.wait_ge(hlo_ready.sem, hlo_ready.now(t, m + 1))
                                d0 = DOWN0 + m * D
                                for n, (h, wt) in enumerate(((h_hi, ffn_hi), (h_hi, ffn_lo), (h_lo, ffn_hi))):
                                    last = nc.tensor.matmul(banks[6 + c % 2][:], h[0:w, m, tok], wt[0:w, d0:d0 + D],
                                                            start=(m == 0 and n == 0), stop=(m == MB - 1 and n == 2))
                            down_done.inc(last)

                    tiles(pe, body)

                @block.vector
                def _(dve):
                    for g in (gsilu_ready, hf_ready, dn_ready):
                        g.start(dve)

                    def body(t, i, pair, more):
                        def chain(sig, k, ins):
                            sig.inc(ins)
                            dve.wait_ge(sig.sem, sig.now(t, k))

                        def next_stats():
                            x = x_loaded[1 - i]
                            dve.wait_ge(x.sem, x.now(pair + i, 1))
                            for s in range(SUB):
                                ln_steps.inc(nc.vector.bn_stats(stats[:, s, :], xf[1 - i][:, s, :]))
                            for s in range(SUB):
                                wait_apart(dve, ln_steps.sem, ln_steps.now(t, s + 1), dve_passed)
                                ln_steps.inc(nc.vector.bn_aggr(mv[:, s, :], stats[:, s, :]))
                            for s in range(SUB):
                                dve.wait_ge(ln_steps.sem, ln_steps.now(t, SUB + s + 1))
                                ln_steps.inc(nc.vector.tensor_scalar(vare[:, s:s + 1], mv[:, s, 1:2], 1.0 / XS ** 2,
                                                                     EPS / XS ** 2, ALU.mult, ALU.add))

                        def next_split(s):
                            dve.wait_ge(rstd_ready.sem, rstd_ready.now(t, 1))
                            chain(split_steps, 3 * s + 1, nc.vector.tensor_scalar(
                                xn[:], xf[1 - i][:, s, :], mv[:, s, 0:1], rstd[:, s:s + 1], ALU.subtract, ALU.mult))
                            chain(split_steps, 3 * s + 2, nc.vector.tensor_copy(xsplit[:, s, 0, :], xn[:]))
                            chain(split_steps, 3 * s + 3, nc.vector.tensor_sub(xsplit[:, s, 1, :], xn[:],
                                                                               xsplit[:, s, 0, :]))

                        def low(m):
                            w = MW[m]
                            dve.wait_ge(hhi_ready.sem, hhi_ready.now(t, m + 1))
                            hlo_ready.inc(nc.vector.tensor_sub(h_lo[0:w, m, :], hf[0:w, m % 2, :], h_hi[0:w, m, :]))

                        for m in range(MB):
                            w = MW[m]
                            dve.wait_ge(gtanh_ready.sem, gtanh_ready.now(t, m + 1))
                            gsilu_ready.inc(nc.vector.scalar_tensor_tensor(
                                gsilu[0:w, m % 2, :], gtanh[0:w, m % 2, :], 1.0, banks[2 + m % 2][0:w, :],
                                ALU.add, ALU.mult))
                            dve.wait_ge(gsilu_ready.sem, gsilu_ready.now(t, m + 1))
                            dve.wait_ge(up_done.sem, up_done.now(t, m + 1))
                            hf_ready.inc(nc.vector.scalar_tensor_tensor(
                                hf[0:w, m % 2, :], gsilu[0:w, m % 2, :], HSCALE, banks[4 + m % 2][0:w, :],
                                ALU.mult, ALU.mult))
                            if m >= 1:
                                low(m - 1)
                            if more and m == STATS_AT:
                                next_stats()
                            if more and 0 <= m - SPLIT_AT < SUB:
                                next_split(m - SPLIT_AT)
                        low(MB - 1)
                        for c in range(SUB):
                            dve.wait_ge(down_done.sem, down_done.now(t, c + 1))
                            bank = banks[6 + c % 2]
                            d0 = 5 * c
                            d_steps.inc(nc.vector.bn_stats(dstat[:, c, :], bank[:]))
                            wait_apart(dve, d_steps.sem, d_steps.now(t, d0 + 1), dve_passed)
                            chain(d_steps, d0 + 2, nc.vector.bn_aggr(dmv[:, c, :], dstat[:, c, :]))
                            chain(d_steps, d0 + 3, nc.vector.tensor_scalar(dscale[:, c:c + 1], dmv[:, c, 1:2],
                                                                           c_down[:], c_down[:], ALU.mult, ALU.mult))
                            chain(d_steps, d0 + 4, nc.vector.tensor_scalar(dvar[:, c:c + 1], dscale[:, c:c + 1],
                                                                           EPS, None, ALU.add))
                            dve.wait_ge(drstd_ready.sem, drstd_ready.now(t, c + 1))
                            chain(d_steps, d0 + 5, nc.vector.tensor_scalar(dscale[:, c:c + 1], drstd[:, c:c + 1],
                                                                           c_down[:], None, ALU.mult))
                            dve.wait_ge(res_ready.sem, res_ready.prev(t, SUB - 1 + c) if c < 2
                                        else res_ready.now(t, c - 1))
                            dn_ready.inc(nc.vector.tensor_scalar(dn[:, c % 2, :], bank[:], dmv[:, c, 0:1],
                                                                 dscale[:, c:c + 1], ALU.subtract, ALU.mult))

                    tiles(dve, body)


def kernel(**inputs):
    import numpy as np
    import concourse.bacc as bacc
    from concourse.bass_utils import run_bass_kernel_spmd

    v = {k[3:]: np.asarray(a) for k, a in inputs.items()}
    B, L, _ = v["attn_u"].shape

    def blocks(codes_t):
        rows, n = codes_t.shape
        full = np.zeros((-(-rows // P) * P, n), codes_t.dtype)
        full[:rows] = codes_t
        return full.reshape(-1, P, n).transpose(1, 0, 2).reshape(P, -1)

    arrays = {
        "u": v["attn_u"].reshape(B * L, D),
        "w_in_t": v["attn_W_in"].T,
        "conv_w": v["attn_conv_w"].reshape(-1, TAPS),
        "conv_b": v["attn_conv_b"],
        "w_out_t": v["attn_W_out"].T,
        "a_log": v["attn_A_log"],
        "d_param": v["attn_D_param"],
        "dt_bias": v["attn_dt_bias"],
        "lut": v["ffn_lut"],
        "codes": np.concatenate([blocks(v["ffn_gate_idx"].T), blocks(v["ffn_up_idx"].T),
                                 blocks(v["ffn_down_idx"].T)], axis=1),
    }
    arrays = {k: np.ascontiguousarray(a) for k, a in arrays.items()}
    nc = bacc.Bacc("TRN2", target_bir_lowering=False, num_devices=1)
    args = [nc.dram_tensor(k, a.shape, mybir.dt.from_np(a.dtype), kind="ExternalInput").ap()
            for k, a in arrays.items()]
    out = nc.dram_tensor("out", (B * L, D), F32, kind="ExternalOutput").ap()
    sandwich_kernel(nc, *args, out)
    r = run_bass_kernel_spmd(nc, [arrays], core_ids=[0])
    return r.results[0]["out"].reshape(B, L, D)
```
